# Optimizing a Trainium2 kernel written in Bass

```python
import numpy as np
import jax
import jax.numpy as jnp

def _softmax(x, axis=-1):
    return jax.nn.softmax(x, axis=axis)

def _gelu(x):
    return jax.nn.gelu(x, approximate=True)

def _silu(x):
    return jax.nn.silu(x)

def _sigmoid(x):
    return jax.nn.sigmoid(x)

def _layernorm(x, axis=-1, eps=1e-05):
    m = jnp.mean(x, axis=axis, keepdims=True)
    v = jnp.var(x, axis=axis, keepdims=True)
    return (x - m) / jnp.sqrt(v + eps)

def _scatter_add(tgt, idx, src, axis=0):
    return tgt.at[idx].add(src)

def _segment_sum(src, seg, n):
    return jax.ops.segment_sum(src, seg, n)
kernel_name = 'mk_adaln_d1_jaxref_r8_4e652f'

def setup_inputs(seed: int=0):
    np.random.seed(seed)
    _w = jnp.asarray

    def _L0_attn_setup():
        import jax, jax.numpy as jnp
        import numpy as np
        LN_EPS = 1e-05
        key = jax.random.key(seed)
        k_u, k_B, k_C = jax.random.split(key, 3)
        Bsz, L, d_model, d_state = (8, 512, 128, 64)
        u = jax.random.normal(k_u, (Bsz, L, d_model), dtype=jnp.float32)
        log_neg_real = -0.5 * jnp.ones((d_state,), jnp.float32)
        imag = jnp.arange(1, d_state + 1, dtype=jnp.float32)
        B_mat = jax.random.normal(k_B, (d_state, d_model), jnp.float32) / d_model ** 0.5
        C_mat = jax.random.normal(k_C, (d_model, d_state), jnp.float32) / d_state ** 0.5
        D = jnp.zeros((d_model,), jnp.float32)
        gamma = jnp.ones((d_model,), jnp.float32)
        beta = jnp.zeros((d_model,), jnp.float32)
        return {'u': u, 'log_neg_real': log_neg_real, 'imag': imag, 'B_mat': B_mat, 'C_mat': C_mat, 'D': D, 'gamma': gamma, 'beta': beta}
    _L0_attn_in = _L0_attn_setup()

    def _L0_ffn_setup():
        import jax, jax.numpy as jnp
        import numpy as np
        D_MODEL = 128
        D_HIDDEN = 512
        NUM_EXPERTS = 8
        B, T = (2, 256)
        key = jax.random.key(seed)
        ks = jax.random.split(key, 8)
        s = 0.02
        x = jax.random.normal(ks[0], (B, T, D_MODEL), dtype=jnp.float32)
        Wg = jax.random.normal(ks[1], (D_MODEL, NUM_EXPERTS), dtype=jnp.float32) * s
        bg = jnp.zeros((NUM_EXPERTS,), dtype=jnp.float32)
        W1 = jax.random.normal(ks[2], (NUM_EXPERTS, D_MODEL, D_HIDDEN), dtype=jnp.float32) * s
        b1 = jnp.zeros((NUM_EXPERTS, D_HIDDEN), dtype=jnp.float32)
        W2 = jax.random.normal(ks[3], (NUM_EXPERTS, D_HIDDEN, D_MODEL), dtype=jnp.float32) * s
        b2 = jnp.zeros((NUM_EXPERTS, D_MODEL), dtype=jnp.float32)
        return {'x': x, 'Wg': Wg, 'bg': bg, 'W1': W1, 'b1': b1, 'W2': W2, 'b2': b2}
    _L0_ffn_in = _L0_ffn_setup()
    _L0_c = _w((lambda *s: np.random.randn(*s).astype(np.float32) * 0.05)(4, 128))
    _L0_wmod = _w((lambda *s: np.random.randn(*s).astype(np.float32) * 0.05)(128, 6 * 128) * 128 ** (-0.5))
    _d = {'L0_attn_u': _L0_attn_in['u'], 'L0_attn_log_neg_real': _L0_attn_in['log_neg_real'], 'L0_attn_imag': _L0_attn_in['imag'], 'L0_attn_B_mat': _L0_attn_in['B_mat'], 'L0_attn_C_mat': _L0_attn_in['C_mat'], 'L0_attn_D': _L0_attn_in['D'], 'L0_attn_gamma': _L0_attn_in['gamma'], 'L0_attn_beta': _L0_attn_in['beta'], 'L0_ffn_Wg': _L0_ffn_in['Wg'], 'L0_ffn_bg': _L0_ffn_in['bg'], 'L0_ffn_W1': _L0_ffn_in['W1'], 'L0_ffn_b1': _L0_ffn_in['b1'], 'L0_ffn_W2': _L0_ffn_in['W2'], 'L0_ffn_b2': _L0_ffn_in['b2'], 'L0_c': _L0_c, 'L0_wmod': _L0_wmod}
    _x0 = _d['L0_attn_u']
    _d['L0_attn_u'] = jax.random.normal(jax.random.fold_in(jax.random.key(seed), 1), (4, 1024, 128), dtype=_x0.dtype)
    del _x0
    return _d

def reference(L0_attn_u, L0_attn_log_neg_real, L0_attn_imag, L0_attn_B_mat, L0_attn_C_mat, L0_attn_D, L0_attn_gamma, L0_attn_beta, L0_ffn_Wg, L0_ffn_bg, L0_ffn_W1, L0_ffn_b1, L0_ffn_W2, L0_ffn_b2, L0_c, L0_wmod):

    def _L0_attn_ref(u, log_neg_real, imag, B_mat, C_mat, D, gamma, beta):
        import jax, jax.numpy as jnp
        import numpy as np
        LN_EPS = 1e-05
        Bsz, L, d_model = u.shape
        d_state = log_neg_real.shape[0]
        a = jax.lax.complex(-jnp.exp(log_neg_real), imag)
        a_bar = jnp.exp(a)
        b_bar = ((a_bar - 1.0) / a)[:, None] * B_mat.astype(a.dtype)
        Bu = jnp.einsum('bld,nd->bln', u.astype(a.dtype), b_bar)

        def step(h, x_t):
            h = h * a_bar + x_t
            return (h, h)
        h0 = jnp.zeros((Bsz, d_state), a.dtype)
        _, hs = jax.lax.scan(step, h0, jnp.swapaxes(Bu, 0, 1))
        hs = jnp.swapaxes(hs, 0, 1)
        y = jnp.einsum('bln,dn->bld', hs, C_mat.astype(a.dtype)).real + D * u
        x = u + y
        mu = jnp.mean(x, axis=-1, keepdims=True)
        var = jnp.mean((x - mu) ** 2, axis=-1, keepdims=True)
        return (x - mu) * jax.lax.rsqrt(var + LN_EPS) * gamma + beta

    def _L0_ffn_ref(x, Wg, bg, W1, b1, W2, b2):
        import jax, jax.numpy as jnp
        import numpy as np
        D_MODEL = 128
        D_HIDDEN = 512
        NUM_EXPERTS = 8
        B, T = (2, 256)
        gate_logits = jnp.einsum('btd,de->bte', x, Wg) + bg
        gate_scores = jax.nn.softmax(gate_logits, axis=-1)
        top1_idx = jnp.argmax(gate_scores, axis=-1)
        top1_mask = jax.nn.one_hot(top1_idx, NUM_EXPERTS, dtype=x.dtype)
        top1_weight = jnp.sum(gate_scores * top1_mask, axis=-1, keepdims=True)
        h = jax.nn.silu(jnp.einsum('btd,edh->bteh', x, W1) + b1)
        o = jnp.einsum('bteh,ehd->bted', h, W2) + b2
        y = jnp.sum(o * top1_mask[..., None], axis=2) * top1_weight
        return y
    x = L0_attn_u
    mod = (_silu(L0_c) @ L0_wmod).reshape(L0_c.shape[0], 6, 1, -1)
    sa, ca, ga, sb, cb, gb = (mod[:, 0], mod[:, 1], mod[:, 2], mod[:, 3], mod[:, 4], mod[:, 5])
    ga = (2 * (ga >= 0) - 1) * jnp.maximum(jnp.abs(ga), 0.25)
    gb = (2 * (gb >= 0) - 1) * jnp.maximum(jnp.abs(gb), 0.25)
    h = _layernorm(x, axis=-1) * (1 + ca) + sa
    x = x + ga * _L0_attn_ref(h, L0_attn_log_neg_real, L0_attn_imag, L0_attn_B_mat, L0_attn_C_mat, L0_attn_D, L0_attn_gamma, L0_attn_beta)
    h = _layernorm(x, axis=-1) * (1 + cb) + sb
    x = x + gb * _L0_ffn_ref(h, L0_ffn_Wg, L0_ffn_bg, L0_ffn_W1, L0_ffn_b1, L0_ffn_W2, L0_ffn_b2)
    return x

_drawn_inputs = setup_inputs


def setup_inputs(seed=0):
    import zlib

    import numpy as np

    out = dict(_drawn_inputs(seed))
    spreads = {'L0_attn_log_neg_real': (-0.5, 0.6),
     'L0_attn_D': (0.0, 0.335),
     'L0_attn_gamma': (1.0, 0.2),
     'L0_attn_beta': (0.0, 0.373),
     'L0_ffn_bg': (0.0, 0.8),
     'L0_ffn_b1': (0.0, 0.8),
     'L0_ffn_b2': (0.0, 0.8)}
    factors = {'L0_ffn_Wg': 8.0, 'L0_ffn_W1': 8.0, 'L0_ffn_W2': 8.0}
    for name, (base, spread) in spreads.items():
        noise = np.random.default_rng([zlib.crc32(name.encode()), seed]).standard_normal(out[name].shape)
        drawn = base * np.exp(spread * noise) if base else spread * noise
        out[name] = jnp.asarray(drawn.astype(out[name].dtype))
    for name, factor in factors.items():
        out[name] = (out[name] * factor).astype(out[name].dtype)
    return out
```

```python
from contextlib import ExitStack

import concourse.bass as bass
from concourse import mybir

P = 128
ALU = mybir.AluOpType
ACT = mybir.ActivationFunctionType
AX_X = mybir.AxisListType.X
F32 = mybir.dt.float32
F16 = mybir.dt.float16
BF16 = mybir.dt.bfloat16
I32 = mybir.dt.int32

ROUND = 12582912.0
TWO_PI = 6.283185307179586
PI_A = 6.28125
PI_B = 0.0019350051879882812
PI_C = TWO_PI - PI_A - PI_B
SIN_SCALE = 6.2831850
EPS = 1e-5
LO_SCALE = 2048.0
FAR = 1000000.0


class Tile:

    def __init__(self, i, c):
        self.i, self.c = i, c

    def __add__(self, n):
        return Tile(self.i, self.c + n)

    @property
    def val(self):
        return self.i * 4 + self.c

    @property
    def mod4(self):
        return self.c % 4

    @property
    def mod2(self):
        return self.c % 2

    @property
    def uses4(self):
        return self.i + self.c // 4


def adaln_block(nc, u, lnr, imag, B_mat, C_mat, D, gamma, beta, Wg, bg, W1, b1, W2, b2, c, wmod, out):
    NG, L, DM = u.shape
    NS = lnr.shape[0]
    NE, _, DH = W1.shape
    TPG = L // P
    NTOK = NG * L
    TT = NTOK // P
    NT = TT + NE - 1
    HC = DH // P
    HALF = L // 2
    TPH = TPG // 2
    ROW = 3 * DM
    GW = DM + NE
    WW = DH + HC
    assert DM == P and 2 * NS == P and HALF == 512 and TPH == 4 and NT % 4 == 3

    ctx = ExitStack()
    with ctx:
        def sb(name, shape, dt=F32):
            return ctx.enter_context(nc.sbuf_tensor(name, shape, dt))

        def sem(name):
            return ctx.enter_context(nc.semaphore(name))

        banks = [ctx.enter_context(nc.psum_tensor(f"bank{i}", [P, 512], F32)) for i in range(8)]

        rows = nc.dram_tensor("rows", (NTOK, ROW), F32).ap()
        out_rows = out.rearrange("b l d -> (b l) d")

        x = sb("x", [P, TT, DM])
        pay = sb("pay", [P, TT, 2 * DM])
        ident = sb("ident", [P, P])
        swap = sb("swap", [P, P])
        cent = sb("cent", [P, P])
        ones = sb("ones", [P, P])
        upper = sb("upper", [P, P], BF16)
        ones_b = sb("ones_b", [P, P], BF16)
        iota_p = sb("iota_p", [P, 1])
        iota_b = sb("iota_b", [P, P], F16)
        iota_k = sb("iota_k", [P, NT])
        iota_t = sb("iota_t", [P, TT, NT], F16)
        iota_r = sb("iota_r", [P, NE])
        eps = sb("eps", [P, 1])
        quarter = sb("quarter", [P, 1])
        sign = sb("sign", [P, 1])
        reset = sb("reset", [P, NE, TPG])
        onesN = sb("onesN", [P, NE])

        th = sb("th", [P, 1])
        ln_r = sb("ln_r", [P, 1])
        cols = sb("cols", [P, 32])
        Bdup = sb("Bdup", [P, DM])
        Cdup = sb("Cdup", [P, P])
        BT = sb("BT", [P, P])
        Cc = sb("Cc", [P, DM])
        Dcol = sb("Dcol", [P, 1])
        Dc = sb("Dc", [P, P])
        rot = sb("rot", [P, P])
        tabs = sb("tabs", [P, 4, L])
        tab = tabs[:, 0, :]
        tab2 = tabs[:, 1, :]
        z = tabs[:, 2:4, :]
        c_in = sb("c_in", [NG, DM])
        scT = sb("scT", [P, NG])
        wm = sb("wm", [P, 6 * DM])
        modT = sb("modT", [P, 6, NG])
        modb = sb("modb", [P, NG, 4, DM])
        cla = z[:, 0, :].rearrange("p (g k d) -> p g k d", g=NG, k=2)
        clb = z[:, 1, :].rearrange("p (g k d) -> p g k d", g=NG, k=2)
        gam_b = sb("gam_b", [P, DM])
        bet_b = sb("bet_b", [P, DM])
        gg = sb("gg", [P, NG, DM])
        gbeta = sb("gbeta", [P, NG, DM])
        Wg_s = sb("Wg_s", [P, NE])
        bg_b = sb("bg_b", [P, NE])
        wgp = sb("wgp", [P, NG, NE])
        sbw = sb("sbw", [P, NG, NE])
        cst = sb("cst", [P, NG, NE])
        rmat = sb("rmat", [P, NG, GW])

        W1s = sb("W1s", [P, NE, WW])
        W2s = sb("W2s", [P, NE, HC, DM])
        b1r = sb("b1r", [NE * HC, P])
        b2b = sb("b2b", [P, NE, DM])

        st = sb("st", [P, 2, TPG, 6])
        sm = sb("sm", [P, 2, 12, TPG])
        st3 = sb("st3", [P, 2, TPG, 6])
        sm3 = sb("sm3", [P, 2, 12, TPG])
        sm2 = sb("sm2", [P, 2, 4, TPG])
        xn = sb("xn", [P, 2, TPG, DM])
        hT = sb("hT", [P, 2, L])
        drive = sb("drive", [P, L])
        state = sb("state", [P, L])
        ang, ang2 = drive, state
        sq = sb("sq", [P, TPH, P], BF16)
        gated = sb("gated", [P, 2, TPG, DM])
        x2T = sb("x2T", [P, 2, L])
        steps = x2T[:, 0, :]
        scb = gated[:, 0, 0:NG, :]
        hg = sb("hg", [P, 2, TPG, GW])

        lgt = sb("lgt", [P, TT, NE])
        lmx = sb("lmx", [P, TT])
        lwk = sb("lwk", [P, TPG, NE])
        lbest = sb("lbest", [P, TPG])
        oh = sb("oh", [P, TT, NE], BF16)
        tote = sb("tote", [P, NE, TPG])
        inc = sb("inc", [P, NE, TPG])
        exc = sb("exc", [P, NE, TPG])
        carry = sb("carry", [P, NG + 1, NE])
        rk = sb("rk", [P, TPG, NE])
        rank = sb("rank", [P, TPG])
        rdiv = sb("rdiv", [P, TT])
        rmod = sb("rmod", [P, TPG])
        OB = sb("OB", [P, TT, P], F16)

        ntile = sb("ntile", [P, NE])
        tend = sb("tend", [P, NE])
        tstart = sb("tstart", [P, NE])
        stk = sb("stk", [P, TT, NE])
        acol = sb("acol", [P, TT])
        OA = drive[:, 0:TT * NT // 2].bitcast(F16).rearrange("p (t k) -> p t k", k=NT)
        OAv = tabs[:, :, :].rearrange("p a b -> p (a b)")[:, 0:TT * 4 * NT // 2].bitcast(F16).rearrange(
            "p (t v k) -> p t v k", v=4, k=NT)
        ecmp = sb("ecmp", [P, NT, NE])
        etile = sb("etile", [P, NT])
        etile_i = sb("etile_i", [P, NT], I32)
        tokv = sb("tokv", [P, 2, NT])
        gidx = sb("gidx", [P, NT])
        gidx_i = sb("gidx_i", [P, NT], I32)
        sidx_i = sb("sidx_i", [P, NT], I32)
        padv = sb("padv", [P, NT])
        lex = sb("lex", [P, TT, NE])
        wsum = sb("wsum", [P, TT])
        wgt = sb("wgt", [P, TT])
        whi = sb("whi", [P, TT], F16)
        wlo = sb("wlo", [P, TT], F16)
        wslot2 = sb("wslot2", [P, 2, NT])
        wslot = sb("wslot", [P, NT])

        hgf, gaf, xnf = (t[:, :, :, :].rearrange("p a b c -> p (a b c)") for t in (hg, gated, xn))
        grow = [hgf[:, i * ROW:(i + 1) * ROW] for i in range(4)]
        w1t = [gaf[:, i * WW:(i + 1) * WW] for i in range(2)]
        hTt = [gaf[:, 2 * WW + i * P:2 * WW + (i + 1) * P] for i in range(2)]
        outb = [gaf[:, 2 * WW + (2 + i) * P:2 * WW + (3 + i) * P] for i in range(4)]
        hid = [xnf[:, i * DH:(i + 1) * DH].rearrange("p (k t) -> p k t", t=P) for i in range(2)]
        y1 = xnf[:, 2 * DH:2 * DH + DM]
        y2 = xnf[:, 2 * DH + DM:2 * DH + 2 * DM]

        x_in = [sem(f"x_in{g}") for g in range(NG)]
        ssm_in = sem("ssm_in")
        mod_in = sem("mod_in")
        w_in = sem("w_in")
        b1_in = sem("b1_in")
        gb_out = sem("gb_out")
        rows_out = sem("rows_out")
        pool_step, dve_step, act_step = sem("pool_step"), sem("dve_step"), sem("act_step")
        consts = sem("consts")
        abs_a, cossin, decay_e, decay_r = sem("angles"), sem("cossin"), sem("decay_e"), sem("decay_r")
        tab_ang, tab_ready = sem("tab_ang"), sem("tab_ready")
        rot_ready, tab2_ps, tab2_ready = sem("rot_ready"), sem("tab2_ps"), sem("tab2_ready")
        setT, setT_used = sem("setT"), sem("setT_used")
        sc_ready, scb_ready = sem("sc_ready"), sem("scb_ready")
        modT_ps, modb_ps = sem("modT_ps"), sem("modb_ps")
        modb_copied = sem("modb_copied")
        modT_ready, modb_ready = sem("modT_ready"), sem("modb_ready")
        small_in, small_ps, rmat_ready = sem("small_in"), sem("small_ps"), sem("rmat_ready")
        ssm_mats = sem("ssm_mats")
        gg_ready = sem("gg_ready")

        stats1, std1, rstd1 = sem("stats1"), sem("std1"), sem("rstd1")
        xn_ready, xnT_ready, hT_ready = sem("xn_ready"), sem("xnT_ready"), sem("hT_ready")
        bh_ready, drive_ready, z_ready = sem("bh_ready"), sem("drive_ready"), sem("z_ready")
        xc_ready, std2, gated_ready = sem("xc_ready"), sem("std2"), sem("gated_ready")
        x2_ready, stats3, std3, rstd3 = sem("x2_ready"), sem("stats3"), sem("std3"), sem("rstd3")
        x2T_ps, x2T_ready = sem("x2T_ps"), sem("x2T_ready")
        hg_ps, hg_ready, h2_ready = sem("hg_ps"), sem("hg_ready"), sem("h2_ready")
        lgt_ready, oh_ready, rank_ps = sem("lgt_ready"), sem("oh_ready"), sem("rank_ps")

        lsh_ready, lex_ready = sem("lsh_ready"), sem("lex_ready")
        OA_tok, OA_w = sem("OA_tok"), sem("OA_w")
        tok_ps, w_ps = sem("tok_ps"), sem("w_ps")
        tables, wslot_ready = sem("tables"), sem("wslot_ready")

        row_in = [sem(f"row_in{i}") for i in range(4)]
        stored = [sem(f"stored{i}") for i in range(4)]
        hTt_ps, hTt_ready = sem("hTt_ps"), sem("hTt_ready")
        w1t_ready = sem("w1t_ready")
        y2_made = sem("y2_made")
        pre_ps, hid_ready, y_ps, y_read, outb_ready = (
            sem("pre_ps"), sem("hid_ready"), sem("y_ps"), sem("y_read"), sem("outb_ready"))

        turn = banks[0:2]
        bh_bank = banks[2]
        xc_bank = banks[3:5]
        hg_bank = banks[5:7]
        rank_bank = banks[7]

        ROUNDS = [[(s, g) for s, g in ((2, k - 1), (1, k), (3, k - 2)) if 0 <= g < NG] for k in range(NG + 2)]
        turns = [(s, g, h) for r in ROUNDS for s, g in r if s in (1, 3) for h in range(2)]
        turn_no = {t: n for n, t in enumerate(turns)}

        def uses_before(t):
            n = turn_no[t] - 2
            if n < 0:
                return None
            s = turns[n][0]
            return s, sum(1 for q in turns[:n + 1] if q[0] == s)

        block = ctx.enter_context(nc.Block())

        def col(i):
            return cols[:, i:i + 1]

        (K_, RED, F_, F1, F2, FQ, RQ, SN, CS, EE, RR, XR, YI, DEN, RDEN, WRE, WIM, T1, T2, RQ2, CM) = range(21)

        @block.sync
        def _(sp):
            for g in range(NG):
                if g == 0:
                    for lo in (0, NS):
                        sp.dma_start(th[lo:lo + NS, :], imag.rearrange("(n o) -> n o", o=1)).then_inc(ssm_in, 16)
                        sp.dma_start(ln_r[lo:lo + NS, :], lnr.rearrange("(n o) -> n o", o=1)).then_inc(ssm_in, 16)
                        sp.dma_start(Bdup[lo:lo + NS, :], B_mat).then_inc(ssm_in, 16)
                        sp.dma_start(Cdup[:, lo:lo + NS], C_mat).then_inc(ssm_in, 16)
                    sp.dma_start(Dcol[:, :], D.rearrange("(n o) -> n o", o=1)).then_inc(ssm_in, 16)
                sp.dma_start(x[:, g * TPG:(g + 1) * TPG, :],
                             u[g].rearrange("(t p) d -> p t d", p=P)).then_inc(x_in[g], 16)
            for e in range(NE):
                sp.dma_start(W1s[:, e, 0:DH], W1[e]).then_inc(w_in, 16)
                sp.dma_start(W2s[:, e, :, :], W2[e].rearrange("(k p) d -> p k d", p=P)).then_inc(w_in, 16)
            sp.wait_ge(modb_ready, 1)
            for g in range(NG):
                sp.dma_start(rows[g * L:(g + 1) * L, 2 * DM:ROW].rearrange("(t p) d -> p t d", p=P),
                             modb[:, g, 3, :].unsqueeze(1).broadcast_to([P, TPG, DM])).then_inc(gb_out, 16)
            for g in range(NG):
                for h in range(2):
                    sp.wait_ge(h2_ready, 2 * g + h + 1)
                    t0 = g * TPG + h * TPH
                    sp.dma_start(rows[t0 * P:(t0 + TPH) * P, 0:2 * DM].rearrange("(t p) d -> p t d", p=P),
                                 pay[:, t0:t0 + TPH, :]).then_inc(rows_out, 16)

        @block.gpsimd
        def _(pool):
            n = [0]

            def step(ins):
                n[0] += 1
                ins.then_inc(pool_step, 1)
                return n[0]

            step(nc.gpsimd.memset(ident[:, :], 0.0))
            step(nc.gpsimd.memset(swap[:, :], 0.0))
            s = step(nc.gpsimd.memset(ones[:, :], 1.0))
            pool.wait_ge(pool_step, s)
            step(nc.gpsimd.affine_select(out=ident[:, :], in_=ident[:, :], compare_op=ALU.not_equal, fill=1.0,
                                         base=0, pattern=[[-1, P]], channel_multiplier=1))
            step(nc.gpsimd.affine_select(out=swap[:, :], in_=swap[:, :], compare_op=ALU.not_equal, fill=1.0,
                                         base=NS, pattern=[[-1, P]], channel_multiplier=1))
            s = step(nc.gpsimd.iota(steps[:, :], [[1, L]], base=0, channel_multiplier=0,
                                    allow_small_or_imprecise_dtypes=True))
            pool.wait_ge(pool_step, s)
            step(nc.gpsimd.affine_select(out=swap[:, :], in_=swap[:, :], compare_op=ALU.not_equal, fill=1.0,
                                         base=-NS, pattern=[[-1, P]], channel_multiplier=1))
            step(nc.gpsimd.affine_select(out=upper[:, :], in_=ones[:, :], compare_op=ALU.is_gt, fill=0.0,
                                         base=0, pattern=[[1, P]], channel_multiplier=-1))
            step(nc.gpsimd.iota(iota_p[:, :], [[0, 1]], base=0, channel_multiplier=1,
                                allow_small_or_imprecise_dtypes=True))
            step(nc.gpsimd.iota(iota_b[:, :], [[1, P]], base=0, channel_multiplier=0,
                                allow_small_or_imprecise_dtypes=True))
            step(nc.gpsimd.iota(iota_k[:, :], [[1, NT]], base=0, channel_multiplier=0,
                                allow_small_or_imprecise_dtypes=True))
            step(nc.gpsimd.iota(iota_t[:, :, :], [[1, TT], [0, NT]], base=1, channel_multiplier=0,
                                allow_small_or_imprecise_dtypes=True))
            s = step(nc.gpsimd.iota(iota_r[:, :], [[-1, NE]], base=NE, channel_multiplier=0,
                                    allow_small_or_imprecise_dtypes=True))
            pool.wait_ge(pool_step, s)
            nc.gpsimd.memset(ones_b[:, :], 1.0).then_inc(consts, 1)
            def residual(g):
                pool.wait_ge(gg_ready, 1)
                pool.wait_ge(xn_ready, 2 * g + 2)
                xs = x[:, g * TPG:(g + 1) * TPG, :]
                return step(nc.gpsimd.tensor_tensor(xs, xs, gbeta[:, g, :].unsqueeze(1).broadcast_to([P, TPG, DM]),
                                                    ALU.add))

            def join(g):
                for h in range(2):
                    t0 = g * TPG + h * TPH
                    pool.wait_ge(gated_ready, 2 * g + h + 1)
                    nc.gpsimd.tensor_tensor(pay[:, t0:t0 + TPH, DM:2 * DM], gated[:, g % 2, h * TPH:(h + 1) * TPH, :],
                                            x[:, t0:t0 + TPH, :], ALU.add).then_inc(x2_ready, 1)

            def shift(g):
                for h in range(2):
                    t0 = g * TPG + h * TPH
                    pool.wait_ge(hg_ready, TPH * (2 * g + h + 1))
                    nc.gpsimd.tensor_tensor(pay[:, t0:t0 + TPH, 0:DM], hg[:, g % 2, h * TPH:(h + 1) * TPH, 0:DM],
                                            modb[:, g, 1, :].unsqueeze(1).broadcast_to([P, TPH, DM]),
                                            ALU.add).then_inc(h2_ready, 1)

            for r in ROUNDS:
                for stage, g in r:
                    if stage == 1:
                        s = residual(g)
                        pool.wait_ge(pool_step, s)
                    elif stage == 2:
                        join(g)
                    else:
                        shift(g)

            def gather(j):
                nc.gpsimd.indirect_dma_start(grow[j % 4], None, rows,
                                             bass.IndirectOffsetOnAxis(ap=gidx_i[:, j:j + 1], axis=0)
                                             ).then_inc(row_in[j % 4], 16)

            def scatter(j):
                nc.gpsimd.indirect_dma_start(out_rows, bass.IndirectOffsetOnAxis(ap=sidx_i[:, j:j + 1], axis=0),
                                             outb[j % 4], None, bounds_check=NTOK - 1, oob_is_err=False
                                             ).then_inc(stored[j % 4], 16)

            pool.wait_ge(rows_out, 16 * 2 * NG)
            pool.wait_ge(gb_out, 16 * NG)
            pool.wait_ge(tables, 1)
            for j in range(4):
                gather(j)
            for j in range(NT):
                pool.wait_ge(outb_ready, j + 1)
                scatter(j)
                if j + 4 < NT:
                    gather(j + 4)
            for q in range(4):
                pool.wait_ge(stored[q], 16 * len(range(q, NT, 4)))

        @block.scalar
        def _(act):
            for t, src in ((gam_b, gamma), (bet_b, beta), (bg_b, bg)):
                act.dma_start(t[:, :], src.partition_broadcast(P)).then_inc(mod_in, 16)
            act.dma_start(c_in[:, :], c).then_inc(mod_in, 16)
            act.dma_start(wm[:, :], wmod).then_inc(mod_in, 16)
            act.dma_start(Wg_s[:, :], Wg).then_inc(mod_in, 16)
            act.dma_start(b1r[:, :], b1.rearrange("e (k p) -> (e k) p", p=P)).then_inc(b1_in, 16)
            act.dma_start(b2b[:, :, :].rearrange("p e d -> p (e d)"),
                          b2.rearrange("e d -> (e d)").partition_broadcast(P)).then_inc(b1_in, 16)
            act.wait_ge(ssm_in, 16 * 9)
            nc.scalar.activation(col(EE), ln_r[:, :], ACT.Exp).then_inc(decay_e, 1)
            act.wait_ge(decay_e, 1)
            nc.scalar.activation(col(RR), col(EE), ACT.Exp, scale=-1.0).then_inc(decay_r, 1)
            act.wait_ge(setT, 1)
            nc.scalar.activation(scT[:, :], banks[6][:, 0:NG], ACT.Silu).then_inc(sc_ready, 1)
            act.wait_ge(abs_a, 1)
            nc.scalar.activation(col(SN), col(F_), ACT.Sin, scale=SIN_SCALE).then_inc(cossin, 1)
            nc.scalar.activation(col(CS), col(FQ), ACT.Sin, scale=SIN_SCALE).then_inc(cossin, 1)
            act.wait_ge(tab_ang, 1)
            nc.scalar.activation(tab[:, :], ang[:, :], ACT.Sin, scale=SIN_SCALE).then_inc(tab_ready, 1)

            for g in range(NG):
                act.wait_ge(modb_ps, g + 1)
                nc.scalar.activation(modb[:, g, :, :], banks[g][:, :].rearrange("p (k d) -> p k d", d=DM),
                                     ACT.Copy).then_inc(modb_copied, 1)

            def norm1(g):
                act.wait_ge(stats1, g + 1)
                nc.scalar.activation(sm[:, g % 2, 5, :], sm[:, g % 2, 4, :], ACT.Sqrt, bias=eps[:, :],
                                     scale=0.25).then_inc(std1, 1)
                act.wait_ge(rstd1, g + 1)
                if g >= 2:
                    act.wait_ge(xnT_ready, 2 * g - 2)
                for t in range(TPG):
                    i = nc.scalar.activation(xn[:, g % 2, t, :], x[:, g * TPG + t, :], ACT.Identity,
                                             bias=sm[:, g % 2, 7, t:t + 1], scale=sm[:, g % 2, 6, t:t + 1])
                    if t % TPH == TPH - 1:
                        i.then_inc(xn_ready, 1)

            def modulate1(g):
                for h in range(2):
                    n = turn_no[(1, g, h)]
                    act.wait_ge(xnT_ready, 2 * g + h + 1)
                    if g >= 2 and h == 0:
                        act.wait_ge(xc_ready, 2 * (g - 1))
                    nc.scalar.activation(hT[:, g % 2, h * HALF:(h + 1) * HALF], turn[n % 2][:, :], ACT.Identity,
                                         bias=modT[:, 0, g:g + 1], scale=modT[:, 1, g:g + 1]).then_inc(hT_ready, 1)

            def spread2(g):
                for h in range(2):
                    act.wait_ge(xc_ready, 2 * g + h + 1)
                    for t in range(TPH):
                        q = h * TPH + t
                        i = nc.scalar.activation(sq[:, t, :], xc_bank[h][:, t * P:(t + 1) * P], ACT.Square,
                                                 accum_out=sm2[:, g % 2, 0, q:q + 1])
                        step(i)
                    act.wait_ge(act_step, act_n[0])
                    nc.scalar.activation(sm2[:, g % 2, 1, h * TPH:(h + 1) * TPH], sm2[:, g % 2, 0, h * TPH:(h + 1) * TPH],
                                         ACT.Sqrt, bias=eps[:, :], scale=1.0 / DM).then_inc(std2, 1)

            act_n = [0]

            def step(ins):
                act_n[0] += 1
                ins.then_inc(act_step, 1)

            def turn3(g):
                for h in range(2):
                    n = turn_no[(3, g, h)]
                    act.wait_ge(x2T_ps, 2 * g + h + 1)
                    if g >= 2:
                        act.wait_ge(hg_ps, 4 * (g - 2) + 2 * h + 2)
                    nc.scalar.activation(x2T[:, g % 2, h * HALF:(h + 1) * HALF], turn[n % 2][:, :],
                                         ACT.Copy).then_inc(x2T_ready, 1)

            def gate3(g):
                act.wait_ge(stats3, g + 1)
                nc.scalar.activation(sm3[:, g % 2, 5, :], sm3[:, g % 2, 4, :], ACT.Sqrt, bias=eps[:, :],
                                     scale=0.25).then_inc(std3, 1)

            def scale3(g):
                act.wait_ge(rstd3, g + 1)
                if g >= 2:
                    act.wait_ge(h2_ready, 2 * (g - 1))
                    act.wait_ge(lgt_ready, g - 1)
                for t in range(TPG):
                    if t % 2 == 0:
                        act.wait_ge(hg_ps, 4 * g + t // 2 + 1)
                    o = (t % 2) * GW
                    nc.scalar.activation(hg[:, g % 2, t, :], hg_bank[(t // 2) % 2][:, o:o + GW], ACT.Copy,
                                         scale=sm3[:, g % 2, 6, t:t + 1]).then_inc(hg_ready, 1)

            act.wait_ge(modT_ready, 1)
            for r in ROUNDS:
                for stage, g in r:
                    if stage == 1:
                        norm1(g)
                        modulate1(g)
                        if g == 0:
                            act.wait_ge(tab2_ps, 1)
                            for h in range(2):
                                nc.scalar.activation(tab2[:, h * HALF:(h + 1) * HALF], banks[3 + h][:, :],
                                                     ACT.Copy).then_inc(tab2_ready, 1)
                    elif stage == 2:
                        spread2(g)
                    else:
                        turn3(g)
                        gate3(g)
                        scale3(g)

            act.wait_ge(lsh_ready, 1)
            nc.scalar.activation(lex[:, :, :], lgt[:, :, :], ACT.Exp).then_inc(lex_ready, 1)

            def turn_tile(j):
                act.wait_ge(hTt_ps, j.val + 1)
                nc.scalar.copy(hTt[j.mod2][:, :], banks[j.mod2][:, 0:P]).then_inc(hTt_ready, 1)

            def silu_tile(j, first=False):
                act.wait_ge(pre_ps, j.val + 1)
                if not first:
                    act.wait_ge(y_ps, j.val - 1)
                for k in range(HC):
                    i = nc.scalar.activation(hid[j.mod2][:, k, :], banks[2 + j.mod2][:, k * P:(k + 1) * P], ACT.Silu,
                                             bias=w1t[j.mod2][:, DH + k:DH + k + 1])
                i.then_inc(hid_ready, 1)

            turn_tile(Tile(0, 0))

            def act_tile(s, first=False, last=False):
                if not last:
                    turn_tile(s + 1)
                silu_tile(s, first)

            act_tile(Tile(0, 0), first=True)
            act_tile(Tile(0, 1), first=True)
            act_tile(Tile(0, 2))
            with act.Fori(0, (NT - 7) // 4) as i:
                for q in range(4):
                    act_tile(Tile(i, 3 + q))
            for s in range(NT - 4, NT):
                act_tile(Tile(0, s), last=s + 1 >= NT)

        @block.tensor
        def _(pe):
            pe.wait_ge(consts, 1)
            pe.wait_ge(mod_in, 16 * 6)
            nc.tensor.transpose(banks[6][:, 0:NG], c_in[:, :], ident[0:NG, 0:NG]).then_inc(setT, 1)
            pe.wait_ge(ssm_in, 16 * 9)
            nc.tensor.transpose(banks[5][:, 0:P], Bdup[:, :], ident[:, :]).then_inc(setT, 1)
            nc.tensor.transpose(banks[5][:, P:2 * P], Cdup[:, :], ident[:, :]).then_inc(setT, 1)
            pe.wait_ge(b1_in, 32)
            nc.tensor.transpose(banks[5][:, 2 * P:2 * P + NE * HC], b1r[:, :],
                                ident[0:NE * HC, 0:NE * HC]).then_inc(setT, 1)
            pe.wait_ge(sc_ready, 1)
            for k in range(6):
                i = nc.tensor.matmul(banks[7][:, k * NG:(k + 1) * NG], wm[:, k * DM:(k + 1) * DM], scT[:, :],
                                     start=True, stop=True)
            i.then_inc(modT_ps, 1)
            pe.wait_ge(scb_ready, 1)
            for g in range(NG):
                nc.tensor.matmul(banks[g][:, :], scb[:, g, :], wm[:, 2 * DM:6 * DM],
                                 start=True, stop=True).then_inc(modb_ps, 1)
            pe.wait_ge(small_in, 1)
            nc.tensor.matmul(banks[6][:, 64:64 + NG * NE], ones[:, :], sbw[:, :, :].rearrange("p g e -> p (g e)"),
                             start=True, stop=True)
            nc.tensor.matmul(banks[6][:, 128:128 + NG * NE], cent[:, :], wgp[:, :, :].rearrange("p g e -> p (g e)"),
                             start=True, stop=True).then_inc(small_ps, 1)

            def turn1(g):
                for h in range(2):
                    n = turn_no[(1, g, h)]
                    pe.wait_ge(xn_ready, 2 * g + h + 1)
                    free_turn((1, g, h))
                    for t in range(TPH):
                        i = nc.tensor.transpose(turn[n % 2][:, t * P:(t + 1) * P], xn[:, g % 2, h * TPH + t, :],
                                                ident[:, :])
                    i.then_inc(xnT_ready, 1)

            def free_turn(t):
                if uses_before(t):
                    s, k = uses_before(t)
                    pe.wait_ge(hT_ready if s == 1 else x2T_ready, k)

            def project(g):
                for h in range(2):
                    pe.wait_ge(hT_ready, 2 * g + h + 1)
                    if 2 * g + h >= 1:
                        pe.wait_ge(drive_ready, 2 * g + h)
                    nc.tensor.matmul(bh_bank[:, :], BT[:, :], hT[:, g % 2, h * HALF:(h + 1) * HALF],
                                     start=True, stop=True).then_inc(bh_ready, 1)

            def mix(g):
                for h in range(2):
                    pe.wait_ge(z_ready, 2 * g + h + 1)
                    if g >= 1:
                        pe.wait_ge(gated_ready, 2 * (g - 1) + h + 1)
                    for t in range(TPH):
                        s = h * HALF + t * P
                        nc.tensor.matmul(xc_bank[h][:, t * P:(t + 1) * P], hT[:, g % 2, s:s + P], Dc[:, :],
                                         start=True, stop=False)
                        i = nc.tensor.matmul(xc_bank[h][:, t * P:(t + 1) * P], z[:, g % 2, s:s + P], Cc[:, :],
                                             start=False, stop=True)
                    i.then_inc(xc_ready, 1)

            def turn2(g):
                for h in range(2):
                    n = turn_no[(3, g, h)]
                    pe.wait_ge(x2_ready, 2 * g + h + 1)
                    free_turn((3, g, h))
                    for t in range(TPH):
                        i = nc.tensor.transpose(turn[n % 2][:, t * P:(t + 1) * P],
                                                pay[:, g * TPG + h * TPH + t, DM:2 * DM], ident[:, :])
                    i.then_inc(x2T_ps, 1)

            def gate(g):
                pe.wait_ge(rmat_ready, 1)
                for t in range(TPG):
                    if t % TPH == 0:
                        pe.wait_ge(x2T_ready, 2 * g + t // TPH + 1)
                    k = 4 * g + t // 2
                    if t % 2 == 0 and k >= 2:
                        pe.wait_ge(hg_ready, 2 * (k - 1))
                    o = (t % 2) * GW
                    i = nc.tensor.matmul(hg_bank[k % 2][:, o:o + GW], x2T[:, g % 2, t * P:(t + 1) * P],
                                         rmat[:, g, :], start=True, stop=True)
                    if t % 2 == 1:
                        i.then_inc(hg_ps, 1)

            def count(g):
                pe.wait_ge(oh_ready, g + 1)
                ohg = oh[:, g * TPG:(g + 1) * TPG, :].rearrange("p t e -> p (t e)")
                w = TPG * NE
                nc.tensor.matmul(rank_bank[:, g * w:(g + 1) * w], upper[:, :], ohg, start=True, stop=True)
                nc.tensor.matmul(rank_bank[:, 256 + g * w:256 + (g + 1) * w], ones_b[:, :], ohg,
                                 start=True, stop=True).then_inc(rank_ps, 1)

            for k, r in enumerate(ROUNDS):
                for stage, g in r:
                    if stage == 1:
                        if g == 0:
                            pe.wait_ge(modb_copied, NG)
                        turn1(g)
                    elif stage == 2:
                        mix(g)
                    else:
                        if g >= 1:
                            count(g - 1)
                        turn2(g)
                        gate(g)
                if k < NG:
                    if k == 0:
                        pe.wait_ge(ssm_mats, 1)
                    project(k)
                if k == 0:
                    pe.wait_ge(rot_ready, 1)
                    pe.wait_ge(tab_ready, 1)
                    for h in range(2):
                        i = nc.tensor.matmul(banks[3 + h][:, :], rot[:, :], tab[:, h * HALF:(h + 1) * HALF],
                                             start=True, stop=True)
                    i.then_inc(tab2_ps, 1)
            count(NG - 1)

            pe.wait_ge(OA_tok, 1)
            for t in range(TT):
                i = nc.tensor.matmul(banks[4][:, 0:2 * NT], OB[:, t, :],
                                     OAv[:, t, 0:2, :].rearrange("p v k -> p (v k)"), start=(t == 0), stop=(t == TT - 1))
            i.then_inc(tok_ps, 1)
            pe.wait_ge(OA_w, 1)
            for t in range(TT):
                i = nc.tensor.matmul(banks[5][:, 0:2 * NT], OB[:, t, :],
                                     OAv[:, t, 2:4, :].rearrange("p v k -> p (v k)"), start=(t == 0), stop=(t == TT - 1))
            i.then_inc(w_ps, 1)

            def turn_tile(j, first=False):
                pe.wait_ge(row_in[j.mod4], 16 * (j.uses4 + 1))
                if not first:
                    pe.wait_ge(hTt_ready, j.val - 1)
                nc.tensor.transpose(banks[j.mod2][:, 0:P], grow[j.mod4][:, 0:DM], ident[:, :]).then_inc(hTt_ps, 1)

            def up(j, first=False):
                pe.wait_ge(hTt_ready, j.val + 1)
                pe.wait_ge(w1t_ready, j.val + 1)
                if not first:
                    pe.wait_ge(hid_ready, j.val - 1)
                for k in range(HC):
                    i = nc.tensor.matmul(banks[2 + j.mod2][:, k * P:(k + 1) * P], w1t[j.mod2][:, k * P:(k + 1) * P],
                                         hTt[j.mod2][:, :], start=True, stop=True)
                i.then_inc(pre_ps, 1)

            def down(j, first=False):
                e = pe.value_load(etile_i[0:1, bass.ds(j.val, 1)], min_val=0, max_val=NE - 1)
                pe.wait_ge(hid_ready, j.val + 1)
                if not first:
                    pe.wait_ge(y_read, j.val - 1)
                for k in range(HC):
                    i = nc.tensor.matmul(banks[6 + j.mod2][:, 0:DM], hid[j.mod2][:, k, :],
                                         W2s[:, bass.ds(e, 1), k, :].rearrange("p o d -> p (o d)"),
                                         start=(k == 0), stop=(k == HC - 1))
                i.then_inc(y_ps, 1)

            pe.wait_ge(tables, 1)
            pe.wait_ge(w_in, 16 * 2 * NE)
            pe.wait_ge(wslot_ready, 1)
            turn_tile(Tile(0, 0), True)

            def pe_tile(s, early=0, last=0):
                if last < 1:
                    turn_tile(s + 1, first=early > 2)
                if last < 2:
                    up(s, first=early > 1)
                if early < 3:
                    down(s + -1, first=early > 0)

            pe_tile(Tile(0, 0), early=3)
            pe_tile(Tile(0, 1), early=2)
            pe_tile(Tile(0, 2), early=1)
            with pe.Fori(0, (NT - 7) // 4) as i:
                for q in range(4):
                    pe_tile(Tile(i, 3 + q))
            for s in range(NT - 4, NT + 1):
                pe_tile(Tile(0, s), last=2 if s == NT else (1 if s == NT - 1 else 0))

        @block.vector
        def _(dve):
            V = nc.vector
            n = [0]

            def step(ins):
                n[0] += 1
                ins.then_inc(dve_step, 1)
                return n[0]

            def after(k=None):
                dve.wait_ge(dve_step, n[0] if k is None else k)

            step(V.memset(eps[:, :], EPS))
            step(V.memset(quarter[0:NS, :], 0.25))
            step(V.memset(quarter[NS:P, :], 0.0))
            step(V.memset(sign[0:NS, :], 1.0))
            step(V.memset(sign[NS:P, :], -1.0))
            step(V.memset(reset[:, :, :], 1.0))
            step(V.memset(onesN[:, :], 1.0))
            step(V.memset(carry[:, 0, :], 0.0))
            after()
            step(V.memset(reset[:, :, 0:1], 0.0))

            def stats(g, s_in, six, small, what):
                for t in range(TPG):
                    step(V.bn_stats(six[:, g % 2, t, :], s_in(t)))
                after()
                q = lambda k: six[:, g % 2, :, k]
                m = lambda k: small[:, g % 2, k, :]
                step(V.tensor_tensor(m(0), q(1), q(4), ALU.add))
                step(V.tensor_tensor(m(1), q(1), q(4), ALU.subtract))
                step(V.tensor_tensor(m(2), q(2), q(5), ALU.add))
                after(n[0] - 1)
                step(V.tensor_tensor(m(3), m(1), m(1), ALU.mult))
                after()
                V.scalar_tensor_tensor(m(4), m(2), 4.0 / DM, m(3), ALU.mult, ALU.add).then_inc(what, 1)

            def ln1(g):
                dve.wait_ge(x_in[g], 16)
                if g >= 2:
                    dve.wait_ge(xn_ready, 2 * (g - 1))
                stats(g, lambda t: x[:, g * TPG + t, :], st, sm, stats1)

            def ln1_end(g):
                dve.wait_ge(std1, g + 1)
                step(V.reciprocal(sm[:, g % 2, 6, :], sm[:, g % 2, 5, :]))
                after()
                V.scalar_tensor_tensor(sm[:, g % 2, 7, :], sm[:, g % 2, 0, :], -0.5, sm[:, g % 2, 6, :],
                                       ALU.mult, ALU.mult).then_inc(rstd1, 1)

            def angles():
                dve.wait_ge(ssm_in, 16 * 9)
                step(V.tensor_scalar(col(T1), th[:, :], 1.0 / TWO_PI, ROUND, ALU.mult, ALU.add))
                after()
                step(V.tensor_scalar(col(K_), col(T1), -ROUND, None, ALU.add))
                after()
                step(V.scalar_tensor_tensor(col(T1), col(K_), -PI_A, th[:, :], ALU.mult, ALU.add))
                after()
                step(V.scalar_tensor_tensor(col(T2), col(K_), -PI_B, col(T1), ALU.mult, ALU.add))
                after()
                step(V.scalar_tensor_tensor(col(RED), col(K_), -PI_C, col(T2), ALU.mult, ALU.add))
                after()
                step(V.tensor_scalar(col(T1), col(RED), 1.0 / TWO_PI, 0.5, ALU.mult, ALU.min))
                after()
                step(V.tensor_scalar(col(F_), col(T1), -0.5, None, ALU.max))
                after()
                step(V.tensor_scalar(col(T1), col(F_), 4096.0, ROUND, ALU.mult, ALU.add))
                step(V.tensor_scalar(col(RQ), col(F_), 0.25, ROUND, ALU.add, ALU.add))
                after()
                step(V.tensor_scalar(col(F1), col(T1), -ROUND, 1.0 / 4096.0, ALU.add, ALU.mult))
                step(V.tensor_scalar(col(RQ2), col(RQ), -ROUND, -0.25, ALU.add, ALU.add))
                after()
                step(V.tensor_tensor(col(F2), col(F_), col(F1), ALU.subtract))
                V.tensor_tensor(col(FQ), col(F_), col(RQ2), ALU.subtract).then_inc(abs_a, 1)

            def table_angles():
                dve.wait_ge(consts, 1)
                step(V.tensor_scalar(cent[:, :], ident[:, :], -1.0 / DM, None, ALU.add))
                after()
                step(V.tensor_scalar(ang[:, :], steps[:, :], col(F1), None, ALU.mult))
                after()
                step(V.tensor_scalar(ang2[:, :], ang[:, :], ROUND, -ROUND, ALU.add, ALU.add))
                after()
                step(V.tensor_tensor(ang[:, :], ang[:, :], ang2[:, :], ALU.subtract))
                after()
                step(V.scalar_tensor_tensor(ang2[:, :], steps[:, :], col(F2), ang[:, :], ALU.mult, ALU.add))
                after()
                step(V.tensor_scalar(ang[:, :], ang2[:, :], quarter[:, :], ROUND, ALU.add, ALU.add))
                after()
                step(V.tensor_scalar(ang[:, :], ang[:, :], -ROUND, quarter[:, :], ALU.add, ALU.subtract))
                after()
                V.tensor_tensor(ang[:, :], ang2[:, :], ang[:, :], ALU.subtract).then_inc(tab_ang, 1)

            def ssm_matrices():
                dve.wait_ge(setT, 4)
                step(V.tensor_copy(BT[:, :], banks[5][:, 0:P]))
                step(V.tensor_copy(W1s[:, :, DH:WW], banks[5][:, 2 * P:2 * P + NE * HC].rearrange(
                    "p (e k) -> p e k", k=HC)))
                step(V.tensor_reduce(col(CM), banks[5][:, P:2 * P], AX_X, ALU.add))
                step(V.tensor_scalar(col(T1), Dcol[:, :], 1.0, None, ALU.add))
                after()
                step(V.tensor_scalar(col(CM), col(CM), 1.0 / DM, None, ALU.mult))
                step(V.tensor_scalar(Dc[:, :], cent[:, :], col(T1), None, ALU.mult))
                after()
                V.tensor_scalar(Cc[:, :], banks[5][:, P:2 * P], col(CM), None, ALU.subtract).then_inc(ssm_mats, 1)

            def weights_w():
                dve.wait_ge(cossin, 2)
                dve.wait_ge(decay_r, 1)
                step(V.tensor_tensor(col(XR), col(RR), col(CS), ALU.mult))
                step(V.tensor_tensor(col(YI), col(RR), col(SN), ALU.mult))
                step(V.tensor_tensor(col(DEN), col(EE), col(EE), ALU.mult))
                after()
                step(V.tensor_scalar(col(XR), col(XR), -1.0, None, ALU.add))
                step(V.scalar_tensor_tensor(col(DEN), th[:, :], th[:, :], col(DEN), ALU.mult, ALU.add))
                after()
                step(V.reciprocal(col(RDEN), col(DEN)))
                step(V.tensor_tensor(col(T1), col(XR), col(EE), ALU.mult))
                step(V.tensor_tensor(col(T2), col(YI), col(EE), ALU.mult))
                after()
                step(V.scalar_tensor_tensor(col(T1), col(YI), th[:, :], col(T1), ALU.mult, ALU.subtract))
                step(V.scalar_tensor_tensor(col(T2), col(XR), th[:, :], col(T2), ALU.mult, ALU.add))
                after()
                step(V.tensor_tensor(col(WRE), col(T1), col(RDEN), ALU.mult))
                step(V.scalar_tensor_tensor(col(WIM), col(T2), -1.0, col(RDEN), ALU.mult, ALU.mult))
                after()
                step(V.tensor_tensor(col(WIM), col(WIM), sign[:, :], ALU.mult))
                step(V.tensor_scalar(rot[:, :], ident[:, :], col(WRE), None, ALU.mult))
                after()
                V.scalar_tensor_tensor(rot[:, :], swap[:, :], col(WIM), rot[:, :],
                                       ALU.mult, ALU.add).then_inc(rot_ready, 1)

            def modulation():
                dve.wait_ge(sc_ready, 1)
                V.tensor_copy(scb[:, :, :], scT[:, :].unsqueeze(2).broadcast_to([P, NG, P])).then_inc(scb_ready, 1)
                dve.wait_ge(modT_ps, 1)
                mt = banks[7][:, 0:6 * NG].rearrange("p (k g) -> p k g", g=NG)
                step(V.tensor_copy(modT[:, :, :], mt))
                after()
                step(V.tensor_scalar(modT[:, 4, :], modT[:, 4, :], 1.0, None, ALU.add))
                V.tensor_scalar(modT[:, 1, :], modT[:, 1, :], 1.0, None, ALU.add).then_inc(modT_ready, 1)
                after()
                wgb = Wg_s[:, :].unsqueeze(1).broadcast_to([P, NG, NE])
                step(V.tensor_tensor(sbw[:, :, :], wgb, modT[:, 3, :].unsqueeze(2).broadcast_to([P, NG, NE]), ALU.mult))
                after()
                V.tensor_tensor(wgp[:, :, :], wgb, modT[:, 4, :].unsqueeze(2).broadcast_to([P, NG, NE]),
                                ALU.mult).then_inc(small_in, 1)

            def modulation_rows():
                dve.wait_ge(modb_copied, NG)
                gates = modb[:, :, 0:4:3, :]
                for g in range(NG):
                    gates = modb[:, g, 0:4:3, :]
                    a = step(V.scalar_tensor_tensor(cla[:, g, :, :], gates, -1.0, gates, ALU.mult, ALU.max))
                    b = step(V.tensor_scalar(clb[:, g, :, :], gates, 0.0, 2.0, ALU.is_ge, ALU.mult))
                    after(a)
                    step(V.tensor_scalar(cla[:, g, :, :], cla[:, g, :, :], 0.25, None, ALU.max))
                    after()
                    step(V.scalar_tensor_tensor(gates, clb[:, g, :, :], -1.0, cla[:, g, :, :], ALU.add, ALU.mult))
                step(V.tensor_scalar(modb[:, :, 2, :], modb[:, :, 2, :], 1.0, None, ALU.add))
                after()
                dve.wait_ge(mod_in, 16 * 6)
                bc = lambda t: t[:, :].unsqueeze(1).broadcast_to([P, NG, DM])
                step(V.tensor_tensor(gg[:, :, :], modb[:, :, 0, :], bc(gam_b), ALU.mult))
                V.tensor_tensor(gbeta[:, :, :], modb[:, :, 0, :], bc(bet_b), ALU.mult).then_inc(gg_ready, 1)
                step(V.tensor_tensor(rmat[:, :, 0:DM], modb[:, :, 2, :], bc(cent), ALU.mult))
                dve.wait_ge(small_ps, 1)
                step(V.tensor_tensor(cst[:, :, :], banks[6][:, 64:64 + NG * NE].rearrange("p (g e) -> p g e", e=NE),
                                     bg_b[:, :].unsqueeze(1).broadcast_to([P, NG, NE]), ALU.add))
                after()
                V.tensor_copy(rmat[:, :, DM:GW], banks[6][:, 128:128 + NG * NE].rearrange("p (g e) -> p g e", e=NE)
                              ).then_inc(rmat_ready, 1)

            def scan_part(g):
                for h in range(2):
                    s = slice(h * HALF, (h + 1) * HALF)
                    dve.wait_ge(bh_ready, 2 * g + h + 1)
                    V.tensor_tensor(drive[:, s], bh_bank[:, :], tab[:, s], ALU.mult).then_inc(drive_ready, 1)
                    dve.wait_ge(drive_ready, 2 * g + h + 1)
                    init = 0.0 if h == 0 else state[:, HALF - 1:HALF]
                    step(V.tensor_tensor_scan(state[:, s], col(RR).broadcast_to([P, HALF]), drive[:, s], init,
                                              ALU.mult, ALU.add))
                    after()
                    if g == 0 and h == 0:
                        dve.wait_ge(tab2_ready, 2)
                    if g >= 2 and h == 0:
                        dve.wait_ge(xc_ready, 2 * (g - 1))
                    V.tensor_tensor(z[:, g % 2, s], state[:, s], tab2[:, s], ALU.mult).then_inc(z_ready, 1)

            def ln2(g):
                for h in range(2):
                    q = slice(h * TPH, (h + 1) * TPH)
                    dve.wait_ge(std2, 2 * g + h + 1)
                    step(V.reciprocal(sm2[:, g % 2, 2, q], sm2[:, g % 2, 1, q]))
                    after()
                    if g >= 2:
                        dve.wait_ge(x2_ready, 2 * (g - 2) + h + 1)
                    for t in range(TPH):
                        k = h * TPH + t
                        i = V.scalar_tensor_tensor(gated[:, g % 2, k, :], xc_bank[h][:, t * P:(t + 1) * P],
                                                   sm2[:, g % 2, 2, k:k + 1], gg[:, g, :], ALU.mult, ALU.mult)
                    i.then_inc(gated_ready, 1)

            def ln3(g):
                dve.wait_ge(x2_ready, 2 * g + 2)
                if g >= 2:
                    dve.wait_ge(hg_ready, TPG * (g - 1))
                stats(g, lambda t: pay[:, g * TPG + t, DM:2 * DM], st3, sm3, stats3)

            def ln3_end(g):
                dve.wait_ge(std3, g + 1)
                V.reciprocal(sm3[:, g % 2, 6, :], sm3[:, g % 2, 5, :]).then_inc(rstd3, 1)

            def choose(g):
                dve.wait_ge(hg_ready, TPG * (g + 1))
                ts = slice(g * TPG, (g + 1) * TPG)
                lg, bc = lgt[:, ts, :], lambda t: t.unsqueeze(2).broadcast_to([P, TPG, NE])
                V.tensor_tensor(lg, hg[:, g % 2, :, DM:GW], cst[:, g, :].unsqueeze(1).broadcast_to([P, TPG, NE]),
                                ALU.add).then_inc(lgt_ready, 1)
                dve.wait_ge(lgt_ready, g + 1)
                step(V.tensor_reduce(lmx[:, ts], lg, AX_X, ALU.max))
                after()
                step(V.tensor_tensor(lwk[:, :, :], lg, bc(lmx[:, ts]), ALU.is_equal))
                after()
                step(V.tensor_tensor(lwk[:, :, :], lwk[:, :, :],
                                     iota_r[:, :].unsqueeze(1).broadcast_to([P, TPG, NE]), ALU.mult))
                after()
                step(V.tensor_reduce(lbest[:, :], lwk[:, :, :], AX_X, ALU.max))
                after()
                V.tensor_tensor(oh[:, ts, :], lwk[:, :, :], bc(lbest[:, :]), ALU.is_equal).then_inc(oh_ready, 1)

            def ranks(g):
                dve.wait_ge(rank_ps, g + 1)
                w = TPG * NE
                within = rank_bank[:, g * w:(g + 1) * w].rearrange("p (t e) -> p t e", e=NE)
                total = rank_bank[:, 256 + g * w:256 + (g + 1) * w].rearrange("p (t e) -> p e t", e=NE)
                step(V.tensor_copy(tote[:, :, :], total))
                after()
                step(V.tensor_tensor_scan(inc[:, :, :].rearrange("p e t -> p (e t)"),
                                          reset[:, :, :].rearrange("p e t -> p (e t)"),
                                          tote[:, :, :].rearrange("p e t -> p (e t)"), 0.0, ALU.mult, ALU.add))
                after()
                step(V.tensor_tensor(carry[:, g + 1, :], carry[:, g, :], inc[:, :, TPG - 1], ALU.add))
                step(V.tensor_tensor(exc[:, :, :], inc[:, :, :], tote[:, :, :], ALU.subtract))
                after()
                step(V.tensor_tensor(inc[:, :, :], exc[:, :, :],
                                     carry[:, g, :].unsqueeze(2).broadcast_to([P, NE, TPG]), ALU.add))
                after()
                step(V.tensor_tensor(rk[:, :, :], within, inc[:, :, :].rearrange("p e t -> p t e"), ALU.add))
                after()
                ts = slice(g * TPG, (g + 1) * TPG)
                step(V.tensor_tensor(rk[:, :, :], rk[:, :, :], oh[:, ts, :], ALU.mult))
                after()
                step(V.tensor_reduce(rank[:, :], rk[:, :, :], AX_X, ALU.add))
                after()
                step(V.tensor_scalar(rmod[:, :], rank[:, :], 1.0 / P, -63.5 / P, ALU.mult, ALU.add))
                after()
                step(V.tensor_scalar(rdiv[:, ts], rmod[:, :], ROUND, -ROUND, ALU.add, ALU.add))
                after()
                step(V.scalar_tensor_tensor(rmod[:, :], rdiv[:, ts], -float(P), rank[:, :], ALU.mult, ALU.add))
                after()
                for t in range(TPG):
                    step(V.tensor_scalar(OB[:, g * TPG + t, :], iota_b[:, :], rmod[:, t:t + 1], None, ALU.is_equal))

            for k, r in enumerate(ROUNDS):
                if k == 0:
                    angles()
                    table_angles()
                    modulation()
                    ln1(0)
                    ln1_end(0)
                    ssm_matrices()
                    weights_w()
                    modulation_rows()
                    V.memset(sm2[:, 0, 3, :], 0.0).then_inc(modb_ready, 1)
                    continue
                for stage, g in r:
                    if stage == 1:
                        ln1(g)
                        ln1_end(g)
                    elif stage == 2:
                        scan_part(g)
                    else:
                        if g >= 1:
                            ranks(g - 1)
                        ln3(g)
                        ln3_end(g)
                for stage, g in r:
                    if stage == 2:
                        ln2(g)
                for stage, g in r:
                    if stage == 3:
                        choose(g)
            ranks(NG - 1)

            step(V.tensor_scalar(ntile[:, :], carry[:, NG, :], 1.0 / P, 63.5 / P, ALU.mult, ALU.add))
            after()
            step(V.tensor_scalar(ntile[:, :], ntile[:, :], ROUND, -ROUND, ALU.add, ALU.add))
            after()
            step(V.tensor_tensor_scan(tend[:, :], onesN[:, :], ntile[:, :], 0.0, ALU.mult, ALU.add))
            after()
            step(V.tensor_tensor(tstart[:, :], tend[:, :], ntile[:, :], ALU.subtract))
            after()
            step(V.tensor_tensor(stk[:, :, :], oh[:, :, :], tstart[:, :].unsqueeze(1).broadcast_to([P, TT, NE]), ALU.mult))
            after()
            step(V.tensor_reduce(acol[:, :], stk[:, :, :], AX_X, ALU.add))
            after()
            step(V.tensor_tensor(acol[:, :], acol[:, :], rdiv[:, :], ALU.add))
            after()
            step(V.tensor_tensor(OA[:, :, :], iota_k[:, :].unsqueeze(1).broadcast_to([P, TT, NT]),
                                 acol[:, :].unsqueeze(2).broadcast_to([P, TT, NT]), ALU.is_equal))
            after()
            step(V.tensor_scalar(OAv[:, :, 0, :], OA[:, :, :], iota_p[:, :], None, ALU.mult))
            after()
            V.tensor_tensor(OAv[:, :, 1, :], OA[:, :, :], iota_t[:, :, :], ALU.mult).then_inc(OA_tok, 1)
            V.tensor_tensor(lgt[:, :, :], lgt[:, :, :], lmx[:, :].unsqueeze(2).broadcast_to([P, TT, NE]),
                            ALU.subtract).then_inc(lsh_ready, 1)
            step(V.tensor_tensor(ecmp[:, :, :], tend[:, :].unsqueeze(1).broadcast_to([P, NT, NE]),
                                 iota_k[:, :].unsqueeze(2).broadcast_to([P, NT, NE]), ALU.is_le))
            after()
            step(V.tensor_reduce(etile[:, :], ecmp[:, :, :], AX_X, ALU.add))
            after()
            step(V.tensor_scalar(etile_i[:, :], etile[:, :], float(NE - 1), None, ALU.min))
            dve.wait_ge(tok_ps, 1)
            step(V.tensor_copy(tokv[:, :, :], banks[4][:, 0:2 * NT].rearrange("p (v k) -> p v k", k=NT)))
            after()
            step(V.scalar_tensor_tensor(gidx[:, :], tokv[:, 1, :], float(P), tokv[:, 0, :], ALU.mult, ALU.add))
            after()
            step(V.tensor_scalar(padv[:, :], gidx[:, :], 64.0, FAR, ALU.is_lt, ALU.mult))
            after()
            step(V.scalar_tensor_tensor(sidx_i[:, :], gidx[:, :], -float(P), padv[:, :], ALU.add, ALU.add))
            after()
            V.tensor_scalar(gidx_i[:, :], gidx[:, :], -float(P), 0.0, ALU.add, ALU.max).then_inc(tables, 1)
            dve.wait_ge(lex_ready, 1)
            step(V.tensor_reduce(wsum[:, :], lex[:, :, :], AX_X, ALU.add))
            after()
            step(V.reciprocal(wgt[:, :], wsum[:, :]))
            after()
            step(V.tensor_copy(whi[:, :], wgt[:, :]))
            after()
            step(V.tensor_tensor(wsum[:, :], wgt[:, :], whi[:, :], ALU.subtract))
            after()
            step(V.tensor_scalar(wlo[:, :], wsum[:, :], LO_SCALE, None, ALU.mult))
            after()
            step(V.tensor_tensor(OAv[:, :, 2, :], OA[:, :, :], whi[:, :].unsqueeze(2).broadcast_to([P, TT, NT]), ALU.mult))
            after()
            V.tensor_tensor(OAv[:, :, 3, :], OA[:, :, :], wlo[:, :].unsqueeze(2).broadcast_to([P, TT, NT]),
                            ALU.mult).then_inc(OA_w, 1)

            def copy_w1(j, first=False):
                e = dve.value_load(etile_i[0:1, bass.ds(j.val, 1)], min_val=0, max_val=NE - 1)
                if not first:
                    dve.wait_ge(pre_ps, j.val - 1)
                    dve.wait_ge(hid_ready, j.val - 1)
                V.tensor_copy(w1t[j.mod2][:, :], W1s[:, bass.ds(e, 1), :].rearrange("p o w -> p (o w)")
                              ).then_inc(w1t_ready, 1)

            def finish(j, first=False):
                e = dve.value_load(etile_i[0:1, bass.ds(j.val, 1)], min_val=0, max_val=NE - 1)
                dve.wait_ge(y_ps, j.val + 1)
                V.tensor_tensor(y1[:, :], banks[6 + j.mod2][:, 0:DM],
                                b2b[:, bass.ds(e, 1), :].rearrange("p o d -> p (o d)"), ALU.add).then_inc(y_read, 1)
                dve.wait_ge(y_read, j.val + 1)
                V.scalar_tensor_tensor(y2[:, :], y1[:, :], wslot[:, bass.ds(j.val, 1)], grow[j.mod4][:, 2 * DM:ROW],
                                       ALU.mult, ALU.mult).then_inc(y2_made, 1)
                dve.wait_ge(y2_made, j.val + 1)
                if not first:
                    dve.wait_ge(stored[j.mod4], 16 * j.uses4)
                V.tensor_tensor(outb[j.mod4][:, :], y2[:, :], grow[j.mod4][:, DM:2 * DM],
                                ALU.add).then_inc(outb_ready, 1)

            dve.wait_ge(w_in, 16 * 2 * NE)
            dve.wait_ge(b1_in, 32)
            after()
            copy_w1(Tile(0, 0), True)
            dve.wait_ge(w_ps, 1)
            step(V.tensor_copy(wslot2[:, :, :], banks[5][:, 0:2 * NT].rearrange("p (v k) -> p v k", k=NT)))
            after()
            V.scalar_tensor_tensor(wslot[:, :], wslot2[:, 1, :], 1.0 / LO_SCALE, wslot2[:, 0, :],
                                   ALU.mult, ALU.add).then_inc(wslot_ready, 1)
            dve.wait_ge(wslot_ready, 1)

            def dve_tile(s, early=0, last=False):
                if not last:
                    copy_w1(s + 1, first=early > 1)
                if early < 2:
                    finish(s + -1, first=s.c < 5 and isinstance(s.i, int) and s.i == 0)

            dve_tile(Tile(0, 0), early=2)
            dve_tile(Tile(0, 1), early=1)
            dve_tile(Tile(0, 2))
            dve_tile(Tile(0, 3))
            dve_tile(Tile(0, 4))
            with dve.Fori(0, (NT - 7) // 4 - 1) as i:
                for q in range(4):
                    dve_tile(Tile(i, 5 + q))
            for s in range(NT - 6, NT + 1):
                dve_tile(Tile(0, s), last=s + 1 >= NT)


def build(nc, ins, outs):
    adaln_block(nc, *ins, *outs)


_INS = ['L0_attn_u', 'L0_attn_log_neg_real', 'L0_attn_imag', 'L0_attn_B_mat', 'L0_attn_C_mat', 'L0_attn_D',
        'L0_attn_gamma', 'L0_attn_beta', 'L0_ffn_Wg', 'L0_ffn_bg', 'L0_ffn_W1', 'L0_ffn_b1', 'L0_ffn_W2',
        'L0_ffn_b2', 'L0_c', 'L0_wmod']


def kernel(**inputs):
    import numpy as _np
    import concourse.bacc as _bacc
    from concourse import mybir as _mybir
    from concourse.bass_utils import run_bass_kernel_spmd as _run

    nc = _bacc.Bacc("TRN2", target_bir_lowering=False, num_devices=1)
    arrays, args = {}, []
    for name in _INS:
        a = _np.ascontiguousarray(inputs[name])
        arrays[f"in_{name}"] = a
        args.append(nc.dram_tensor(f"in_{name}", a.shape, _mybir.dt.from_np(a.dtype), kind="ExternalInput").ap())
    shape = tuple(inputs['L0_attn_u'].shape)
    y = nc.dram_tensor("out_x", shape, _mybir.dt.float32, kind="ExternalOutput").ap()
    build(nc, args, [y])
    r = _run(nc, [arrays], core_ids=[0])
    return r.results[0]["out_x"]
```

```python
from contextlib import ExitStack

import concourse.bass as bass
from concourse import mybir

P = 128
ALU = mybir.AluOpType
ACT = mybir.ActivationFunctionType
AX_X = mybir.AxisListType.X
F32 = mybir.dt.float32
F16 = mybir.dt.float16
BF16 = mybir.dt.bfloat16
I32 = mybir.dt.int32

ROUND = 12582912.0
TWO_PI = 6.283185307179586
PI_A = 6.28125
PI_B = 0.0019350051879882812
PI_C = TWO_PI - PI_A - PI_B
SIN_SCALE = 6.2831850
EPS = 1e-5
FAR = 1000000.0


class Tile:

    def __init__(self, i, c):
        self.i, self.c = i, c

    def __add__(self, n):
        return Tile(self.i, self.c + n)

    @property
    def val(self):
        return self.i * 8 + self.c

    @property
    def mod4(self):
        return self.c % 4

    @property
    def mod2(self):
        return self.c % 2

    @property
    def mod8(self):
        return self.c % 8

    @property
    def uses4(self):
        return self.i * 2 + self.c // 4

    @property
    def uses8(self):
        return self.i + self.c // 8


def adaln_block(nc, u, lnr, imag, B_mat, C_mat, D, gamma, beta, Wg, bg, W1, b1, W2, b2, c, wmod, out):
    NG, L, DM = u.shape
    NS = lnr.shape[0]
    NE, _, DH = W1.shape
    TPG = L // P
    NTOK = NG * L
    TT = NTOK // P
    NT = TT + NE - 1
    HC = DH // P
    HALF = L // 2
    TPH = TPG // 2
    PAY = 2 * DM + 1
    ROW = PAY + DM
    GROW = 8
    GW = DM + NE
    WW = DH + HC
    assert DM == P and 2 * NS == P and HALF == 512 and TPH == 4 and (NT - 7) % 8 == 0

    ctx = ExitStack()
    with ctx:
        def sb(name, shape, dt=F32):
            return ctx.enter_context(nc.sbuf_tensor(name, shape, dt))

        def sem(name):
            return ctx.enter_context(nc.semaphore(name))

        banks = [ctx.enter_context(nc.psum_tensor(f"bank{i}", [P, 512], F32)) for i in range(8)]

        rows = nc.dram_tensor("rows", (NTOK, ROW), F32).ap()
        out_rows = out.rearrange("b l d -> (b l) d")

        x = sb("x", [P, TT, DM])
        pay = sb("pay", [P, TT, PAY])
        ident = sb("ident", [P, P])
        swap = sb("swap", [P, P])
        cent = sb("cent", [P, P])
        ones = sb("ones", [P, P])
        upper = sb("upper", [P, P], BF16)
        ones_b = sb("ones_b", [P, P], BF16)
        iota_p = sb("iota_p", [P, 1])
        iota_b = sb("iota_b", [P, P], F16)
        iota_k = sb("iota_k", [P, NT])
        iota_t = sb("iota_t", [P, TT, NT], F16)
        iota_r = sb("iota_r", [P, NE])
        eps = sb("eps", [P, 1])
        quarter = sb("quarter", [P, 1])
        sign = sb("sign", [P, 1])
        reset = sb("reset", [P, NE, TPG + 1])
        onesN = sb("onesN", [P, NE])

        th = sb("th", [P, 1])
        ln_r = sb("ln_r", [P, 1])
        cols = sb("cols", [P, 32])
        Bdup = sb("Bdup", [P, DM])
        Cdup = sb("Cdup", [P, P])
        BT = sb("BT", [P, P])
        Cc = sb("Cc", [P, DM])
        Dcol = sb("Dcol", [P, 1])
        Dc = sb("Dc", [P, P])
        rot = sb("rot", [P, P])
        tabs = sb("tabs", [P, 4, L])
        tab = tabs[:, 0, :]
        tab2 = tabs[:, 1, :]
        z = tabs[:, 2:4, :]
        c_in = sb("c_in", [NG, DM])
        scT = sb("scT", [P, NG])
        wm = sb("wm", [P, 6 * DM])
        modT = sb("modT", [P, 6, NG])
        modr = sb("modr", [NG, 8, DM])
        cla = sb("cla", [NG, 2, DM])
        clb = sb("clb", [NG, 2, DM])
        pick_g = sb("pick_g", [NG, NG, P])
        modb = sb("modb", [P, NG, 4, DM])
        gbeta = sb("gbeta", [P, NG, DM])
        gam_r = sb("gam_r", [NG, DM])
        bet_r = sb("bet_r", [NG, DM])
        Wg_s = sb("Wg_s", [P, NE])
        bg_b = sb("bg_b", [P, NE])
        wgp = sb("wgp", [P, NG, NE])
        sbw = sb("sbw", [P, NG, NE])
        cst = sb("cst", [P, NG, NE])
        rmat = sb("rmat", [P, NG, GW])

        W1s = sb("W1s", [P, NE, WW])
        W2s = sb("W2s", [P, NE, HC, DM])
        b1r = sb("b1r", [NE * HC, P])
        b2h = sb("b2h", [NE, 3, DM], BF16)
        b2w = sb("b2w", [NE, DM])
        b2s = sb("b2s", [3, NE, DM], BF16)

        st = sb("st", [P, 2, TPG, 6])
        sm = sb("sm", [P, 2, 12, TPG])
        st3 = sb("st3", [P, 2, TPG, 6])
        sm3 = sb("sm3", [P, 2, 12, TPG])
        sm2 = sb("sm2", [P, 2, 4, TPG])
        xn = sb("xn", [P, 2, TPG, DM])
        hT = sb("hT", [P, 2, L])
        drive = sb("drive", [P, L])
        state = sb("state", [P, L])
        ang, ang2 = drive, state
        b2done = sb("b2done", [P, 1])
        warm = sb("warm", [P, 1])
        sq = sb("sq", [P, TPG, P], BF16)
        gated = sb("gated", [P, 2, TPG, DM])
        x2T = sb("x2T", [P, 2, L])
        steps = x2T[:, 0, :]
        hg = sb("hg", [P, 2, TPG, GW])

        lgt = sb("lgt", [P, TT, NE])
        lmx = sb("lmx", [P, TT])
        lwk = sb("lwk", [P, TPG, NE])
        lbest = sb("lbest", [P, TPG])
        oh = sb("oh", [P, NG, NE, TPG + 1], BF16)
        ohsum = sb("ohsum", [P, NG, NE, TPG + 1], BF16)
        rk = sb("rk", [P, TPG, NE])
        rank = sb("rank", [P, TPG])
        rdiv = sb("rdiv", [P, TT])
        rmod = sb("rmod", [P, 2, TPG])
        OB = sb("OB", [P, TT, P], F16)

        ntile = sb("ntile", [P, NE])
        tend = sb("tend", [P, NE])
        tstart = sb("tstart", [P, NE])
        stk = sb("stk", [P, NG, TPG, NE])
        acol = sb("acol", [P, TT])
        OA = drive[:, 0:TT * NT // 2].bitcast(F16).rearrange("p (t k) -> p t k", k=NT)
        OAv = tabs[:, :, :].rearrange("p a b -> p (a b)")[:, 0:TT * NT].bitcast(F16).rearrange(
            "p (t v k) -> p t v k", v=2, k=NT)
        ecmp = sb("ecmp", [P, NT, NE])
        etile = sb("etile", [P, NT])
        etile_i = sb("etile_i", [P, NT], I32)
        tokv = sb("tokv", [P, NT])
        gidx = sb("gidx", [P, NT])
        gidx_i = sb("gidx_i", [P, NT], I32)
        sidx_i = sb("sidx_i", [P, NT], I32)
        padv = sb("padv", [P, NT])
        lex = sb("lex", [P, 2, TPG, NE])
        lsum = sb("lsum", [P, 2, TPG])

        hgf, gaf, xnf = (t[:, :, :, :].rearrange("p a b c -> p (a b c)") for t in (hg, gated, xn))
        hTf = hT[:, :, :].rearrange("p a b -> p (a b)")
        grow = [f[:, i * ROW:(i + 1) * ROW] for f in (hgf, hTf) for i in range(GROW // 2)]
        w1t = [gaf[:, i * WW:(i + 1) * WW] for i in range(2)]
        hTt = [gaf[:, 2 * WW + i * P:2 * WW + (i + 1) * P] for i in range(2)]
        outb = [gaf[:, 2 * WW + (2 + i) * P:2 * WW + (3 + i) * P] for i in range(4)]
        hid = [xnf[:, i * DH:(i + 1) * DH].rearrange("p (k t) -> p k t", t=P) for i in range(2)]
        y2 = [xnf[:, 2 * DH + i * DM:2 * DH + (i + 1) * DM] for i in range(2)]

        x_in = [sem(f"x_in{g}") for g in range(NG)]
        ssm_in = sem("ssm_in")
        mod_in = sem("mod_in")
        w_in = sem("w_in")
        b1_in = sem("b1_in")
        th_in, c_in_sem = sem("th_in"), sem("c_in_sem")
        b2_in, b2_parts, b2_ready = sem("b2_in"), sem("b2_parts"), sem("b2_ready")
        BT_ready, modr_ps, modr_copied, modr_ready = sem("BT_ready"), sem("modr_ps"), sem("modr_copied"), sem("modr_ready")
        cent_ready, rmat_d = sem("cent_ready"), sem("rmat_d")
        gb_out = sem("gb_out")
        rows_out = sem("rows_out")
        pool_step, dve_step, act_step = sem("pool_step"), sem("dve_step"), sem("act_step")
        consts = sem("consts")
        abs_a, cossin, decay_e, decay_r = sem("angles"), sem("cossin"), sem("decay_e"), sem("decay_r")
        tab_ang, tab_ready = sem("tab_ang"), sem("tab_ready")
        small_used = sem("small_used")
        rot_ready, tab2_ps, tab2_ready = sem("rot_ready"), sem("tab2_ps"), sem("tab2_ready")
        setT, setT_used = sem("setT"), sem("setT_used")
        sc_ready = sem("sc_ready")
        modT_ps, modb_ps = sem("modT_ps"), sem("modb_ps")
        modb_copied = sem("modb_copied")
        modT_ready = sem("modT_ready")
        small_in, small_ps, rmat_ready = sem("small_in"), sem("small_ps"), sem("rmat_ready")
        ssm_mats = sem("ssm_mats")

        stats1, std1, rstd1 = sem("stats1"), sem("std1"), sem("rstd1")
        xn_ready, xnT_ready, hT_ready = sem("xn_ready"), sem("xnT_ready"), sem("hT_ready")
        bh_ready, drive_ready, z_ready = sem("bh_ready"), sem("drive_ready"), sem("z_ready")
        xc_ready, std2, gated_ready = sem("xc_ready"), sem("std2"), sem("gated_ready")
        x2_ready, stats3, std3, rstd3 = sem("x2_ready"), sem("stats3"), sem("std3"), sem("rstd3")
        x2T_ps, x2T_ready = sem("x2T_ps"), sem("x2T_ready")
        hg_ps, hg_ready, h2_ready = sem("hg_ps"), sem("hg_ready"), sem("h2_ready")
        lgt_ready, oh_ready, rank_ps = sem("lgt_ready"), sem("oh_ready"), sem("rank_ps")

        lsh_ready = sem("lsh_ready")
        OA_ready, OAp_ready, OAt_ready = sem("OA_ready"), sem("OAp_ready"), sem("OAt_ready")
        tok_ps, tables, lex_ready, weight_ready = sem("tok_ps"), sem("tables"), sem("lex_ready"), sem("weight_ready")

        row_in = [sem(f"row_in{i}") for i in range(GROW)]
        stored = [sem(f"stored{i}") for i in range(4)]
        hTt_ps, hTt_ready = sem("hTt_ps"), sem("hTt_ready")
        w1t_ready = sem("w1t_ready")
        pre_ps, hid_ready, y_ps, y_read, outb_ready = (
            sem("pre_ps"), sem("hid_ready"), sem("y_ps"), sem("y_read"), sem("outb_ready"))

        turn = banks[0:2]
        bh_bank = banks[2]
        xc_bank = banks[3:5]
        hg_bank = banks[5:7]
        rank_bank = banks[7]

        ROUNDS = range(-1, NG + 2)

        def there(g):
            return 0 <= g < NG

        turns = [(s, g, h) for r in ROUNDS for s, g in ((1, r + 1), (3, r - 1)) if there(g) for h in range(2)]
        turn_no = {t: n for n, t in enumerate(turns)}

        def uses_before(t):
            n = turn_no[t] - 2
            if n < 0:
                return None
            s = turns[n][0]
            return s, sum(1 for q in turns[:n + 1] if q[0] == s)

        row_bank = (5, 6, 7, 0, 1)


        block = ctx.enter_context(nc.Block())

        def col(i):
            return cols[:, i:i + 1]

        (K_, RED, F_, F1, F2, FQ, RQ, SN, CS, EE, RR, XR, YI, DEN, RDEN, WRE, WIM, T1, T2, RQ2, CM) = range(21)

        @block.sync
        def _(sp):
            def load_x(g):
                sp.dma_start(x[:, g * TPG:(g + 1) * TPG, :],
                             u[g].rearrange("(t p) d -> p t d", p=P)).then_inc(x_in[g], 16)

            sp.dma_start(th[0:NS, :], imag.rearrange("(n o) -> n o", o=1)).then_inc(th_in, 16)
            load_x(0)
            for lo in (0, NS):
                sp.dma_start(ln_r[lo:lo + NS, :], lnr.rearrange("(n o) -> n o", o=1)).then_inc(ssm_in, 16)
                sp.dma_start(Bdup[lo:lo + NS, :], B_mat).then_inc(ssm_in, 16)
            for lo in (0, NS):
                sp.dma_start(Cdup[:, lo:lo + NS], C_mat).then_inc(ssm_in, 16)
            sp.dma_start(Dcol[:, :], D.rearrange("(n o) -> n o", o=1)).then_inc(ssm_in, 16)
            sp.dma_start(b1r[:, :], b1.rearrange("e (k p) -> (e k) p", p=P)).then_inc(b1_in, 16)
            sp.dma_start(Wg_s[:, :], Wg).then_inc(mod_in, 16)
            for t, src in ((gam_r, gamma), (bet_r, beta)):
                sp.dma_start(t[:, :], src.partition_broadcast(NG)).then_inc(mod_in, 16)
            sp.dma_start(bg_b[:, :], bg.partition_broadcast(P)).then_inc(mod_in, 16)
            load_x(1)
            sp.dma_start(b2w[:, :], b2).then_inc(b2_in, 16)
            for g in range(2, NG):
                load_x(g)
            sp.wait_ge(b2_parts, 1)
            for v in range(3):
                sp.dma_start(b2s[v:v + 1, :, :], b2h[:, v:v + 1, :]).then_inc(b2_ready, 16)
            for e in range(NE):
                sp.dma_start(W1s[:, e, 0:DH], W1[e]).then_inc(w_in, 16)
                sp.dma_start(W2s[:, e, :, :], W2[e].rearrange("(k p) d -> p k d", p=P)).then_inc(w_in, 16)
            sp.wait_ge(modb_copied, NG)
            for g in range(NG):
                sp.dma_start(rows[g * L:(g + 1) * L, PAY:ROW].rearrange("(t p) d -> p t d", p=P),
                             modb[:, g, 2, :].unsqueeze(1).broadcast_to([P, TPG, DM])).then_inc(gb_out, 16)
            for g in range(NG):
                sp.wait_ge(h2_ready, 2 * g + 2)
                sp.wait_ge(weight_ready, g + 1)
                sp.dma_start(rows[g * L:(g + 1) * L, 0:PAY].rearrange("(t p) d -> p t d", p=P),
                             pay[:, g * TPG:(g + 1) * TPG, :]).then_inc(rows_out, 16)

        @block.gpsimd
        def _(pool):
            n = [0]

            def step(ins):
                n[0] += 1
                ins.then_inc(pool_step, 1)
                return n[0]

            step(nc.gpsimd.memset(ident[:, :], 0.0))
            step(nc.gpsimd.memset(swap[:, :], 0.0))
            s = step(nc.gpsimd.memset(ones[:, :], 1.0))
            pool.wait_ge(pool_step, s)
            s = step(nc.gpsimd.affine_select(out=ident[:, :], in_=ident[:, :], compare_op=ALU.not_equal, fill=1.0,
                                             base=0, pattern=[[-1, P]], channel_multiplier=1))
            s = step(nc.gpsimd.affine_select(out=swap[:, :], in_=swap[:, :], compare_op=ALU.not_equal, fill=1.0,
                                             base=NS, pattern=[[-1, P]], channel_multiplier=1))
            s = step(nc.gpsimd.affine_select(out=pick_g[:, :, :], in_=ones[0:NG, :].unsqueeze(1).broadcast_to([NG, NG, P]),
                                             compare_op=ALU.is_equal, fill=0.0, base=0, pattern=[[-1, NG], [0, P]],
                                             channel_multiplier=1))
            s = step(nc.gpsimd.iota(steps[:, :], [[1, L]], base=0, channel_multiplier=0,
                                    allow_small_or_imprecise_dtypes=True))
            pool.wait_ge(pool_step, s)
            step(nc.gpsimd.affine_select(out=swap[:, :], in_=swap[:, :], compare_op=ALU.not_equal, fill=1.0,
                                         base=-NS, pattern=[[-1, P]], channel_multiplier=1))
            s = step(nc.gpsimd.tensor_scalar(cent[:, :], ident[:, :], -1.0 / DM, None, ALU.add))
            pool.wait_ge(pool_step, s)
            nc.gpsimd.memset(ones_b[:, :], 1.0).then_inc(consts, 1)
            step(nc.gpsimd.affine_select(out=upper[:, :], in_=ones[:, :], compare_op=ALU.is_gt, fill=0.0,
                                         base=0, pattern=[[1, P]], channel_multiplier=-1))
            step(nc.gpsimd.iota(iota_p[:, :], [[0, 1]], base=0, channel_multiplier=1,
                                allow_small_or_imprecise_dtypes=True))
            step(nc.gpsimd.iota(iota_b[:, :], [[1, P]], base=0, channel_multiplier=0,
                                allow_small_or_imprecise_dtypes=True))
            step(nc.gpsimd.iota(iota_k[:, :], [[1, NT]], base=0, channel_multiplier=0,
                                allow_small_or_imprecise_dtypes=True))
            step(nc.gpsimd.iota(iota_t[:, :, :], [[1, TT], [0, NT]], base=1, channel_multiplier=0,
                                allow_small_or_imprecise_dtypes=True))
            s = step(nc.gpsimd.iota(iota_r[:, :], [[-1, NE]], base=NE, channel_multiplier=0,
                                    allow_small_or_imprecise_dtypes=True))
            pool.wait_ge(pool_step, s)
            s = step(nc.gpsimd.memset(onesN[:, :], 1.0))
            pool.wait_ge(pool_step, s)
            consts2 = s

            pool.wait_ge(b2_in, 16)
            for v in range(3):
                s = step(nc.gpsimd.tensor_copy(b2h[:, v, :], b2w[:, :]))
                pool.wait_ge(pool_step, s)
                if v < 2:
                    s = step(nc.gpsimd.tensor_tensor(b2w[:, :], b2w[:, :], b2h[:, v, :], ALU.subtract))
                    pool.wait_ge(pool_step, s)
            nc.gpsimd.memset(b2done[:, :], 0.0).then_inc(b2_parts, 1)

            pool.wait_ge(modb_copied, NG)
            nc.gpsimd.tensor_tensor(rmat[:, :, 0:DM], modb[:, :, 1, :],
                                    cent[:, :].unsqueeze(1).broadcast_to([P, NG, DM]), ALU.mult).then_inc(rmat_d, 1)
            pool.wait_ge(modb_copied, NG + 1)

            def residual(g):
                pool.wait_ge(xn_ready, 2 * g + 2)
                xs = x[:, g * TPG:(g + 1) * TPG, :]
                return step(nc.gpsimd.tensor_tensor(xs, xs, gbeta[:, g, :].unsqueeze(1).broadcast_to([P, TPG, DM]),
                                                    ALU.add))

            def join(g):
                for h in range(2):
                    t0 = g * TPG + h * TPH
                    pool.wait_ge(gated_ready, TPH * (2 * g + h + 1))
                    nc.gpsimd.tensor_tensor(pay[:, t0:t0 + TPH, DM:2 * DM], gated[:, g % 2, h * TPH:(h + 1) * TPH, :],
                                            x[:, t0:t0 + TPH, :], ALU.add).then_inc(x2_ready, 1)

            def shift(g):
                for h in range(2):
                    t0 = g * TPG + h * TPH
                    pool.wait_ge(hg_ready, TPH * (2 * g + h + 1))
                    nc.gpsimd.tensor_tensor(pay[:, t0:t0 + TPH, 0:DM], hg[:, g % 2, h * TPH:(h + 1) * TPH, 0:DM],
                                            modb[:, g, 0, :].unsqueeze(1).broadcast_to([P, TPH, DM]),
                                            ALU.add).then_inc(h2_ready, 1)

            for r in ROUNDS:
                if there(r + 1):
                    s = residual(r + 1)
                    pool.wait_ge(pool_step, s)
                if there(r):
                    join(r)
                if there(r - 1):
                    shift(r - 1)

            def gather(j):
                nc.gpsimd.indirect_dma_start(grow[j % GROW], None, rows,
                                             bass.IndirectOffsetOnAxis(ap=gidx_i[:, j:j + 1], axis=0)
                                             ).then_inc(row_in[j % GROW], 16)

            def scatter(j):
                nc.gpsimd.indirect_dma_start(out_rows, bass.IndirectOffsetOnAxis(ap=sidx_i[:, j:j + 1], axis=0),
                                             outb[j % 4], None, bounds_check=NTOK - 1, oob_is_err=False
                                             ).then_inc(stored[j % 4], 16)

            pool.wait_ge(rows_out, 16 * NG)
            pool.wait_ge(gb_out, 16 * NG)
            pool.wait_ge(tables, 1)
            for j in range(GROW):
                gather(j)
            pool.wait_ge(tables, 2)
            for j in range(NT):
                pool.wait_ge(outb_ready, j + 1)
                scatter(j)
                if j + GROW < NT:
                    gather(j + GROW)
            for q in range(4):
                pool.wait_ge(stored[q], 16 * len(range(q, NT, 4)))

        @block.scalar
        def _(act):
            act.dma_start(th[NS:P, :], imag.rearrange("(n o) -> n o", o=1)).then_inc(th_in, 16)
            act.dma_start(c_in[:, :], c).then_inc(c_in_sem, 16)
            act.dma_start(wm[:, :], wmod).then_inc(c_in_sem, 16)

            act.wait_ge(setT, 1)
            nc.scalar.activation(scT[:, :], banks[6][:, 0:NG], ACT.Silu).then_inc(sc_ready, 1)
            act.wait_ge(ssm_in, 16 * 7)
            nc.scalar.activation(col(EE), ln_r[:, :], ACT.Exp).then_inc(decay_e, 1)
            act.wait_ge(decay_e, 1)
            nc.scalar.activation(col(RR), col(EE), ACT.Exp, scale=-1.0).then_inc(decay_r, 1)

            def std_1(g):
                act.wait_ge(stats1, g + 1)
                nc.scalar.activation(sm[:, g % 2, 5, :], sm[:, g % 2, 4, :], ACT.Sqrt, bias=eps[:, :],
                                     scale=0.25).then_inc(std1, 1)

            def norm1(g):
                act.wait_ge(rstd1, g + 1)
                if g >= 2:
                    act.wait_ge(xnT_ready, 2 * g - 2)
                for t in range(TPG):
                    i = nc.scalar.activation(xn[:, g % 2, t, :], x[:, g * TPG + t, :], ACT.Identity,
                                             bias=sm[:, g % 2, 7, t:t + 1], scale=sm[:, g % 2, 6, t:t + 1])
                    if t % TPH == TPH - 1:
                        i.then_inc(xn_ready, 1)

            def modulate1(g):
                for h in range(2):
                    n = turn_no[(1, g, h)]
                    act.wait_ge(xnT_ready, 2 * g + h + 1)
                    if g >= 2 and h == 0:
                        act.wait_ge(xc_ready, 2 * (g - 1))
                    nc.scalar.activation(hT[:, g % 2, h * HALF:(h + 1) * HALF], turn[n % 2][:, :], ACT.Identity,
                                         bias=modT[:, 0, g:g + 1], scale=modT[:, 1, g:g + 1]).then_inc(hT_ready, 1)

            def spread2(g):
                for h in range(2):
                    act.wait_ge(xc_ready, 2 * g + h + 1)
                    for t in range(TPH):
                        q = h * TPH + t
                        i = nc.scalar.activation(sq[:, q, :], xc_bank[h][:, t * P:(t + 1) * P], ACT.Square,
                                                 accum_out=sm2[:, g % 2, 0, q:q + 1])
                        step(i)
                act.wait_ge(act_step, act_n[0])
                nc.scalar.activation(sm2[:, g % 2, 1, :], sm2[:, g % 2, 0, :],
                                     ACT.Sqrt, bias=eps[:, :], scale=1.0 / DM).then_inc(std2, 1)

            act_n = [0]

            def step(ins):
                act_n[0] += 1
                ins.then_inc(act_step, 1)

            def turn3(g):
                for h in range(2):
                    n = turn_no[(3, g, h)]
                    act.wait_ge(x2T_ps, 2 * g + h + 1)
                    if g >= 2:
                        act.wait_ge(hg_ps, 4 * (g - 2) + 2 * h + 2)
                    nc.scalar.activation(x2T[:, g % 2, h * HALF:(h + 1) * HALF], turn[n % 2][:, :],
                                         ACT.Copy).then_inc(x2T_ready, 1)

            def gate3(g):
                act.wait_ge(stats3, g + 1)
                nc.scalar.activation(sm3[:, g % 2, 5, :], sm3[:, g % 2, 4, :], ACT.Sqrt, bias=eps[:, :],
                                     scale=0.25).then_inc(std3, 1)

            def exponentials(g):
                act.wait_ge(lsh_ready, g + 1)
                nc.scalar.activation(lex[:, g % 2, :, :], lex[:, g % 2, :, :], ACT.Exp).then_inc(lex_ready, 1)

            def scale3(g):
                act.wait_ge(rstd3, g + 1)
                if g >= 2:
                    act.wait_ge(h2_ready, 2 * (g - 1))
                    act.wait_ge(lgt_ready, g - 1)
                for t in range(TPG):
                    if t % 2 == 0:
                        act.wait_ge(hg_ps, 4 * g + t // 2 + 1)
                    o = (t % 2) * GW
                    nc.scalar.activation(hg[:, g % 2, t, :], hg_bank[(t // 2) % 2][:, o:o + GW], ACT.Copy,
                                         scale=sm3[:, g % 2, 6, t:t + 1]).then_inc(hg_ready, 1)

            std_1(0)
            norm1(0)
            act.wait_ge(modr_ps, 1)
            for lo, n in ((0, 4), (4, 2)):
                nc.scalar.activation(modr[:, lo:lo + n, :], banks[lo // 4][0:NG, 0:n * DM].rearrange("p (k d) -> p k d", d=DM),
                                     ACT.Copy).then_inc(modr_copied, 1)
            act.wait_ge(abs_a, 1)
            nc.scalar.activation(col(SN), col(F_), ACT.Sin, scale=SIN_SCALE).then_inc(cossin, 1)
            nc.scalar.activation(col(CS), col(FQ), ACT.Sin, scale=SIN_SCALE).then_inc(cossin, 1)
            act.wait_ge(setT, 4)
            nc.scalar.activation(BT[:, :], banks[5][:, 0:P], ACT.Copy).then_inc(BT_ready, 1)
            act.wait_ge(modT_ready, 1)
            modulate1(0)
            act.wait_ge(tab_ang, 1)
            nc.scalar.activation(tab[:, :], ang[:, :], ACT.Sin, scale=SIN_SCALE).then_inc(tab_ready, 1)
            act.wait_ge(tab2_ps, 1)
            for h in range(2):
                nc.scalar.activation(tab2[:, h * HALF:(h + 1) * HALF], banks[3 + h][:, :],
                                     ACT.Copy).then_inc(tab2_ready, 1)
            std_1(1)
            norm1(1)
            for g in range(NG):
                act.wait_ge(modb_ps, g + 1)
                nc.scalar.activation(modb[:, g, :, :], banks[row_bank[g]][:, :].rearrange("p (k d) -> p k d", d=DM),
                                     ACT.Copy).then_inc(modb_copied, 1)
            act.wait_ge(modb_ps, NG + 1)
            nc.scalar.activation(gbeta[:, :, :], banks[row_bank[NG]][:, :].rearrange("p (g d) -> p g d", d=DM),
                                 ACT.Copy).then_inc(modb_copied, 1)

            for r in ROUNDS[1:]:
                if there(r + 1):
                    modulate1(r + 1)
                if there(r - 1):
                    turn3(r - 1)
                if r == 0:
                    std_1(2)
                if there(r):
                    spread2(r)
                if there(r - 1):
                    gate3(r - 1)
                    if there(r + 2):
                        std_1(r + 2)
                if there(r - 1):
                    scale3(r - 1)
                if there(r + 2):
                    norm1(r + 2)
                if there(r - 2):
                    exponentials(r - 2)

            act.wait_ge(lex_ready, NG)
            nc.scalar.activation(warm[:, :], eps[:, :], ACT.Silu)
            for h in range(2):
                act.wait_ge(OA_ready, h + 1)
                ts = slice(h * TT // 2, (h + 1) * TT // 2)
                nc.scalar.activation(OAv[:, ts, 0, :], OA[:, ts, :], ACT.Copy, scale=iota_p[:, :]).then_inc(OAp_ready, 1)

            def turn_tile(j):
                act.wait_ge(hTt_ps, j.val + 1)
                nc.scalar.copy(hTt[j.mod2][:, :], banks[j.mod2][:, 0:P]).then_inc(hTt_ready, 1)

            def silu_tile(j, first=False):
                act.wait_ge(pre_ps, j.val + 1)
                if not first:
                    act.wait_ge(y_ps, j.val - 1)
                for k in range(HC):
                    i = nc.scalar.activation(hid[j.mod2][:, k, :], banks[2 + j.mod2][:, k * P:(k + 1) * P], ACT.Silu,
                                             bias=w1t[j.mod2][:, DH + k:DH + k + 1])
                i.then_inc(hid_ready, 1)

            turn_tile(Tile(0, 0))

            def act_tile(s, first=False, last=False):
                if not last:
                    turn_tile(s + 1)
                silu_tile(s, first)

            act_tile(Tile(0, 0), first=True)
            act_tile(Tile(0, 1), first=True)
            act_tile(Tile(0, 2))
            with act.Fori(0, (NT - 7) // 8) as i:
                for q in range(8):
                    act_tile(Tile(i, 3 + q))
            for s in range(NT - 4, NT):
                act_tile(Tile(0, s), last=s + 1 >= NT)

        @block.tensor
        def _(pe):
            pe.wait_ge(consts, 1)
            pe.wait_ge(c_in_sem, 32)
            nc.tensor.transpose(banks[6][:, 0:NG], c_in[:, :], ident[0:NG, 0:NG]).then_inc(setT, 1)
            pe.wait_ge(sc_ready, 1)
            for k in range(6):
                i = nc.tensor.matmul(banks[7][:, k * NG:(k + 1) * NG], wm[:, k * DM:(k + 1) * DM], scT[:, :],
                                     start=True, stop=True)
            i.then_inc(modT_ps, 1)
            for lo, n in ((0, 4), (4, 2)):
                i = nc.tensor.matmul(banks[lo // 4][0:NG, 0:n * DM], scT[:, :], wm[:, lo * DM:(lo + n) * DM],
                                     start=True, stop=True)
            i.then_inc(modr_ps, 1)
            pe.wait_ge(ssm_in, 16 * 7)
            nc.tensor.transpose(banks[5][:, 0:P], Bdup[:, :], ident[:, :]).then_inc(setT, 1)
            nc.tensor.transpose(banks[5][:, P:2 * P], Cdup[:, :], ident[:, :]).then_inc(setT, 1)
            pe.wait_ge(b1_in, 16)
            nc.tensor.transpose(banks[5][:, 2 * P:2 * P + NE * HC], b1r[:, :],
                                ident[0:NE * HC, 0:NE * HC]).then_inc(setT, 1)
            pe.wait_ge(small_in, 1)
            nc.tensor.matmul(banks[7][:, 64:64 + NG * NE], ones[:, :], sbw[:, :, :].rearrange("p g e -> p (g e)"),
                             start=True, stop=True)
            nc.tensor.matmul(banks[7][:, 128:128 + NG * NE], cent[:, :], wgp[:, :, :].rearrange("p g e -> p (g e)"),
                             start=True, stop=True).then_inc(small_ps, 1)

            def turn1(g):
                for h in range(2):
                    n = turn_no[(1, g, h)]
                    pe.wait_ge(xn_ready, 2 * g + h + 1)
                    free_turn((1, g, h))
                    for t in range(TPH):
                        i = nc.tensor.transpose(turn[n % 2][:, t * P:(t + 1) * P], xn[:, g % 2, h * TPH + t, :],
                                                ident[:, :])
                    i.then_inc(xnT_ready, 1)

            def free_turn(t):
                if uses_before(t):
                    s, k = uses_before(t)
                    pe.wait_ge(hT_ready if s == 1 else x2T_ready, k)

            def project(g, halves=(0, 1)):
                for h in halves:
                    pe.wait_ge(hT_ready, 2 * g + h + 1)
                    if 2 * g + h >= 1:
                        pe.wait_ge(drive_ready, 2 * g + h)
                    nc.tensor.matmul(bh_bank[:, :], BT[:, :], hT[:, g % 2, h * HALF:(h + 1) * HALF],
                                     start=True, stop=True).then_inc(bh_ready, 1)

            def mix(g):
                for h in range(2):
                    pe.wait_ge(z_ready, 2 * g + h + 1)
                    if g >= 1:
                        pe.wait_ge(gated_ready, TPH * (2 * (g - 1) + h + 1))
                    for t in range(TPH):
                        s = h * HALF + t * P
                        nc.tensor.matmul(xc_bank[h][:, t * P:(t + 1) * P], hT[:, g % 2, s:s + P], Dc[:, :],
                                         start=True, stop=False)
                        i = nc.tensor.matmul(xc_bank[h][:, t * P:(t + 1) * P], z[:, g % 2, s:s + P], Cc[:, :],
                                             start=False, stop=True)
                    i.then_inc(xc_ready, 1)

            def turn2(g):
                for h in range(2):
                    n = turn_no[(3, g, h)]
                    pe.wait_ge(x2_ready, 2 * g + h + 1)
                    free_turn((3, g, h))
                    for t in range(TPH):
                        i = nc.tensor.transpose(turn[n % 2][:, t * P:(t + 1) * P],
                                                pay[:, g * TPG + h * TPH + t, DM:2 * DM], ident[:, :])
                    i.then_inc(x2T_ps, 1)

            def gate(g):
                pe.wait_ge(rmat_ready, 1)
                pe.wait_ge(rmat_d, 1)
                for t in range(TPG):
                    if t % TPH == 0:
                        pe.wait_ge(x2T_ready, 2 * g + t // TPH + 1)
                    k = 4 * g + t // 2
                    if t % 2 == 0 and k >= 2:
                        pe.wait_ge(hg_ready, 2 * (k - 1))
                    o = (t % 2) * GW
                    i = nc.tensor.matmul(hg_bank[k % 2][:, o:o + GW], x2T[:, g % 2, t * P:(t + 1) * P],
                                         rmat[:, g, :], start=True, stop=True)
                    if t % 2 == 1:
                        i.then_inc(hg_ps, 1)

            def count(g):
                pe.wait_ge(oh_ready, g + 1)
                w = TPG * NE
                nc.tensor.matmul(rank_bank[:, g * w:(g + 1) * w], upper[:, :],
                                 oh[:, g, :, 1:TPG + 1].rearrange("p e t -> p t e"), start=True, stop=False)
                i = nc.tensor.matmul(rank_bank[:, g * w:(g + 1) * w], ones_b[:, :],
                                     ohsum[:, g, :, 0:TPG].rearrange("p e t -> p t e"), start=False, stop=True)
                if g == NG - 1:
                    i = nc.tensor.matmul(rank_bank[:, NG * w:NG * w + NE], ones_b[:, :],
                                         ohsum[:, g, :, TPG], start=True, stop=True)
                i.then_inc(rank_ps, 1)

            pe.wait_ge(modr_copied, 2)
            turn1(0)
            pe.wait_ge(BT_ready, 1)
            project(0, halves=(0,))
            pe.wait_ge(rot_ready, 1)
            pe.wait_ge(tab_ready, 1)
            for h in range(2):
                i = nc.tensor.matmul(banks[3 + h][:, :], rot[:, :], tab[:, h * HALF:(h + 1) * HALF],
                                     start=True, stop=True)
            i.then_inc(tab2_ps, 1)
            pe.wait_ge(modr_ready, 1)
            pe.wait_ge(small_used, 2)
            pe.wait_ge(hT_ready, 2)
            for g in range(NG):
                nc.tensor.matmul(banks[row_bank[g]][:, :], pick_g[:, g, :],
                                 modr[:, 3:7, :].rearrange("p k d -> p (k d)"), start=True, stop=True).then_inc(modb_ps, 1)
            for g in range(NG):
                i = nc.tensor.matmul(banks[row_bank[NG]][:, g * DM:(g + 1) * DM], pick_g[:, g, :], modr[:, 7, :],
                                     start=True, stop=True)
            i.then_inc(modb_ps, 1)
            project(0, halves=(1,))
            pe.wait_ge(modb_copied, NG + 1)
            pe.wait_ge(ssm_mats, 1)

            for r in ROUNDS[1:]:
                if there(r + 1):
                    turn1(r + 1)
                if there(r - 1):
                    turn2(r - 1)
                if there(r):
                    mix(r)
                if there(r - 2):
                    count(r - 2)
                if there(r + 1):
                    project(r + 1, halves=(0,))
                if there(r - 1):
                    gate(r - 1)
                if there(r + 1):
                    project(r + 1, halves=(1,))

            for t in range(TT):
                if t % (TT // 2) == 0:
                    pe.wait_ge(OAp_ready, 2 * t // TT + 1)
                    pe.wait_ge(OAt_ready, 2 * t // TT + 1)
                i = nc.tensor.matmul(banks[4][:, 0:2 * NT], OB[:, t, :], OAv[:, t, :, :].rearrange("p v k -> p (v k)"),
                                     start=(t == 0), stop=(t == TT - 1))
            i.then_inc(tok_ps, 1)

            def turn_tile(j, first=False):
                pe.wait_ge(row_in[j.mod8], 16 * (j.uses8 + 1))
                if not first:
                    pe.wait_ge(hTt_ready, j.val - 1)
                nc.tensor.transpose(banks[j.mod2][:, 0:P], grow[j.mod8][:, 0:DM], ident[:, :]).then_inc(hTt_ps, 1)

            def up(j, first=False):
                pe.wait_ge(hTt_ready, j.val + 1)
                pe.wait_ge(w1t_ready, j.val + 1)
                if not first:
                    pe.wait_ge(hid_ready, j.val - 1)
                for k in range(HC):
                    i = nc.tensor.matmul(banks[2 + j.mod2][:, k * P:(k + 1) * P], w1t[j.mod2][:, k * P:(k + 1) * P],
                                         hTt[j.mod2][:, :], start=True, stop=True)
                i.then_inc(pre_ps, 1)

            def down(j, first=False):
                e = pe.value_load(etile_i[0:1, bass.ds(j.val, 1)], min_val=0, max_val=NE - 1)
                pe.wait_ge(hid_ready, j.val + 1)
                if not first:
                    pe.wait_ge(y_read, j.val - 1)
                nc.tensor.matmul(banks[6 + j.mod2][:, 0:DM], ones_b[0:3, :],
                                 b2s[:, bass.ds(e, 1), :].rearrange("p o d -> p (o d)"), start=True, stop=False)
                for k in range(HC):
                    i = nc.tensor.matmul(banks[6 + j.mod2][:, 0:DM], hid[j.mod2][:, k, :],
                                         W2s[:, bass.ds(e, 1), k, :].rearrange("p o d -> p (o d)"),
                                         start=False, stop=(k == HC - 1))
                i.then_inc(y_ps, 1)

            pe.wait_ge(tables, 1)
            pe.wait_ge(w_in, 16 * 2 * NE)
            pe.wait_ge(b2_ready, 48)
            turn_tile(Tile(0, 0), True)

            def pe_tile(s, early=0, last=0):
                if last < 1:
                    turn_tile(s + 1, first=early > 2)
                if last < 2:
                    up(s, first=early > 1)
                if early < 3:
                    down(s + -1, first=early > 0)

            pe_tile(Tile(0, 0), early=3)
            pe_tile(Tile(0, 1), early=2)
            pe_tile(Tile(0, 2), early=1)
            with pe.Fori(0, (NT - 7) // 8) as i:
                for q in range(8):
                    pe_tile(Tile(i, 3 + q))
            for s in range(NT - 4, NT + 1):
                pe_tile(Tile(0, s), last=2 if s == NT else (1 if s == NT - 1 else 0))

        @block.vector
        def _(dve):
            V = nc.vector
            n = [0]

            def step(ins):
                n[0] += 1
                ins.then_inc(dve_step, 1)
                return n[0]

            def after(k=None):
                dve.wait_ge(dve_step, n[0] if k is None else k)

            step(V.memset(eps[:, :], EPS))
            step(V.memset(quarter[0:NS, :], 0.25))
            step(V.memset(quarter[NS:P, :], 0.0))
            step(V.memset(sign[0:NS, :], 1.0))
            step(V.memset(sign[NS:P, :], -1.0))
            step(V.memset(reset[:, :, :], 1.0))
            step(V.memset(oh[:, 0, :, 0:1], 0.0))
            after()
            step(V.memset(reset[:, :, 0:1], 0.0))

            def stats(g, s_in, six, small, what):
                for t in range(TPG):
                    step(V.bn_stats(six[:, g % 2, t, :], s_in(t)))
                after()
                q = lambda k: six[:, g % 2, :, k]
                m = lambda k: small[:, g % 2, k, :]
                step(V.tensor_tensor(m(0), q(1), q(4), ALU.add))
                step(V.tensor_tensor(m(1), q(1), q(4), ALU.subtract))
                step(V.tensor_tensor(m(2), q(2), q(5), ALU.add))
                after(n[0] - 1)
                step(V.tensor_tensor(m(3), m(1), m(1), ALU.mult))
                after()
                V.scalar_tensor_tensor(m(4), m(2), 4.0 / DM, m(3), ALU.mult, ALU.add).then_inc(what, 1)

            def ln1(g):
                dve.wait_ge(x_in[g], 16)
                if g >= 2:
                    dve.wait_ge(xn_ready, 2 * (g - 1))
                stats(g, lambda t: x[:, g * TPG + t, :], st, sm, stats1)

            def ln1_end(g):
                dve.wait_ge(std1, g + 1)
                step(V.reciprocal(sm[:, g % 2, 6, :], sm[:, g % 2, 5, :]))
                after()
                V.scalar_tensor_tensor(sm[:, g % 2, 7, :], sm[:, g % 2, 0, :], -0.5, sm[:, g % 2, 6, :],
                                       ALU.mult, ALU.mult).then_inc(rstd1, 1)

            def angles():
                dve.wait_ge(th_in, 32)
                step(V.tensor_scalar(col(T1), th[:, :], 1.0 / TWO_PI, ROUND, ALU.mult, ALU.add))
                after()
                step(V.tensor_scalar(col(K_), col(T1), -ROUND, None, ALU.add))
                after()
                step(V.scalar_tensor_tensor(col(T1), col(K_), -PI_A, th[:, :], ALU.mult, ALU.add))
                after()
                step(V.scalar_tensor_tensor(col(T2), col(K_), -PI_B, col(T1), ALU.mult, ALU.add))
                after()
                step(V.scalar_tensor_tensor(col(RED), col(K_), -PI_C, col(T2), ALU.mult, ALU.add))
                after()
                step(V.tensor_scalar(col(T1), col(RED), 1.0 / TWO_PI, 0.5, ALU.mult, ALU.min))
                after()
                step(V.tensor_scalar(col(F_), col(T1), -0.5, None, ALU.max))
                after()
                step(V.tensor_scalar(col(T1), col(F_), 4096.0, ROUND, ALU.mult, ALU.add))
                step(V.tensor_scalar(col(RQ), col(F_), 0.25, ROUND, ALU.add, ALU.add))
                after()
                step(V.tensor_scalar(col(F1), col(T1), -ROUND, 1.0 / 4096.0, ALU.add, ALU.mult))
                step(V.tensor_scalar(col(RQ2), col(RQ), -ROUND, -0.25, ALU.add, ALU.add))
                after()
                step(V.tensor_tensor(col(F2), col(F_), col(F1), ALU.subtract))
                V.tensor_tensor(col(FQ), col(F_), col(RQ2), ALU.subtract).then_inc(abs_a, 1)

            def table_angles(part):
                if part == 1:
                    return table_angles_end()
                dve.wait_ge(consts, 1)
                step(V.tensor_scalar(ang[:, :], steps[:, :], col(F1), quarter[:, :], ALU.mult, ALU.add))
                after()
                step(V.tensor_scalar(ang2[:, :], ang[:, :], ROUND, -ROUND, ALU.add, ALU.add))
                after()

            def table_angles_end():
                step(V.tensor_tensor(ang[:, :], ang[:, :], ang2[:, :], ALU.subtract))
                after()
                step(V.scalar_tensor_tensor(ang[:, :], steps[:, :], col(F2), ang[:, :], ALU.mult, ALU.add))
                after()
                step(V.tensor_scalar(ang2[:, :], ang[:, :], ROUND, -ROUND, ALU.add, ALU.add))
                after()
                V.tensor_tensor(ang[:, :], ang[:, :], ang2[:, :], ALU.subtract).then_inc(tab_ang, 1)

            def ssm_matrices():
                dve.wait_ge(BT_ready, 1)
                step(V.tensor_copy(W1s[:, :, DH:WW], banks[5][:, 2 * P:2 * P + NE * HC].rearrange(
                    "p (e k) -> p e k", k=HC)))
                step(V.tensor_reduce(col(CM), banks[5][:, P:2 * P], AX_X, ALU.add))
                step(V.tensor_scalar(col(T1), Dcol[:, :], 1.0, None, ALU.add))
                after()
                step(V.tensor_scalar(col(CM), col(CM), 1.0 / DM, None, ALU.mult))
                step(V.tensor_scalar(Dc[:, :], cent[:, :], col(T1), None, ALU.mult))
                after()
                V.tensor_scalar(Cc[:, :], banks[5][:, P:2 * P], col(CM), None, ALU.subtract).then_inc(ssm_mats, 1)
                dve.wait_ge(ssm_mats, 1)
                V.memset(sm2[:, 0, 3, :], 0.0).then_inc(small_used, 1)

            def weights_w():
                dve.wait_ge(cossin, 2)
                dve.wait_ge(decay_r, 1)
                step(V.tensor_tensor(col(XR), col(RR), col(CS), ALU.mult))
                step(V.tensor_tensor(col(YI), col(RR), col(SN), ALU.mult))
                step(V.tensor_tensor(col(DEN), col(EE), col(EE), ALU.mult))
                after()
                step(V.tensor_scalar(col(XR), col(XR), -1.0, None, ALU.add))
                step(V.scalar_tensor_tensor(col(DEN), th[:, :], th[:, :], col(DEN), ALU.mult, ALU.add))
                after()
                step(V.reciprocal(col(RDEN), col(DEN)))
                step(V.tensor_tensor(col(T1), col(XR), col(EE), ALU.mult))
                step(V.tensor_tensor(col(T2), col(YI), col(EE), ALU.mult))
                after()
                step(V.scalar_tensor_tensor(col(T1), col(YI), th[:, :], col(T1), ALU.mult, ALU.subtract))
                step(V.scalar_tensor_tensor(col(T2), col(XR), th[:, :], col(T2), ALU.mult, ALU.add))
                after()
                step(V.tensor_tensor(col(WRE), col(T1), col(RDEN), ALU.mult))
                step(V.scalar_tensor_tensor(col(WIM), col(T2), -1.0, col(RDEN), ALU.mult, ALU.mult))
                after()
                step(V.tensor_tensor(col(WIM), col(WIM), sign[:, :], ALU.mult))
                step(V.tensor_scalar(rot[:, :], ident[:, :], col(WRE), None, ALU.mult))
                after()
                V.scalar_tensor_tensor(rot[:, :], swap[:, :], col(WIM), rot[:, :],
                                       ALU.mult, ALU.add).then_inc(rot_ready, 1)

            def modulation():
                dve.wait_ge(modT_ps, 1)
                mt = banks[7][:, 0:6 * NG].rearrange("p (k g) -> p k g", g=NG)
                step(V.tensor_copy(modT[:, :, :], mt))
                after()
                step(V.tensor_scalar(modT[:, 4, :], modT[:, 4, :], 1.0, None, ALU.add))
                V.tensor_scalar(modT[:, 1, :], modT[:, 1, :], 1.0, None, ALU.add).then_inc(modT_ready, 1)
                after()
                dve.wait_ge(modT_ready, 1)
                dve.wait_ge(mod_in, 16 * 4)
                wgb = Wg_s[:, :].unsqueeze(1).broadcast_to([P, NG, NE])
                step(V.tensor_tensor(sbw[:, :, :], wgb, modT[:, 3, :].unsqueeze(2).broadcast_to([P, NG, NE]), ALU.mult))
                after()
                V.tensor_tensor(wgp[:, :, :], wgb, modT[:, 4, :].unsqueeze(2).broadcast_to([P, NG, NE]),
                                ALU.mult).then_inc(small_in, 1)

            def modulation_rows():
                dve.wait_ge(modr_copied, 2)
                gates = modr[:, 2:6:3, :]
                a = step(V.scalar_tensor_tensor(cla[:, :, :], gates, -1.0, gates, ALU.mult, ALU.max))
                step(V.tensor_scalar(clb[:, :, :], gates, 0.0, 2.0, ALU.is_ge, ALU.mult))
                step(V.tensor_scalar(modr[:, 4, :], modr[:, 4, :], 1.0, None, ALU.add))
                after(a)
                step(V.tensor_scalar(cla[:, :, :], cla[:, :, :], 0.25, None, ALU.max))
                after()
                step(V.scalar_tensor_tensor(gates, clb[:, :, :], -1.0, cla[:, :, :], ALU.add, ALU.mult))
                after()
                step(V.tensor_tensor(modr[:, 6, :], modr[:, 2, :], gam_r[:, :], ALU.mult))
                step(V.tensor_tensor(modr[:, 7, :], modr[:, 2, :], bet_r[:, :], ALU.mult))
                after()
                V.memset(sm2[:, 1, 3, :], 0.0).then_inc(modr_ready, 1)

            def gate_weights():
                dve.wait_ge(small_ps, 1)
                step(V.tensor_tensor(cst[:, :, :], banks[7][:, 64:64 + NG * NE].rearrange("p (g e) -> p g e", e=NE),
                                     bg_b[:, :].unsqueeze(1).broadcast_to([P, NG, NE]), ALU.add))
                V.tensor_copy(rmat[:, :, DM:GW], banks[7][:, 128:128 + NG * NE].rearrange("p (g e) -> p g e", e=NE)
                              ).then_inc(rmat_ready, 1)
                after()
                dve.wait_ge(rmat_ready, 1)
                V.memset(sm2[:, 0, 3, :], 0.0).then_inc(small_used, 1)

            def scan_part(g):
                for h in range(2):
                    s = slice(h * HALF, (h + 1) * HALF)
                    dve.wait_ge(bh_ready, 2 * g + h + 1)
                    V.tensor_tensor(drive[:, s], bh_bank[:, :], tab[:, s], ALU.mult).then_inc(drive_ready, 1)
                    dve.wait_ge(drive_ready, 2 * g + h + 1)
                    init = 0.0 if h == 0 else state[:, HALF - 1:HALF]
                    step(V.tensor_tensor_scan(state[:, s], col(RR).broadcast_to([P, HALF]), drive[:, s], init,
                                              ALU.mult, ALU.add))
                    after()
                    if g == 0 and h == 0:
                        dve.wait_ge(tab2_ready, 2)
                    if g >= 2 and h == 0:
                        dve.wait_ge(xc_ready, 2 * (g - 1))
                    V.tensor_tensor(z[:, g % 2, s], state[:, s], tab2[:, s], ALU.mult).then_inc(z_ready, 1)

            def ln2(g):
                dve.wait_ge(std2, g + 1)
                step(V.reciprocal(sm2[:, g % 2, 2, :], sm2[:, g % 2, 1, :]))
                after()
                for t in range(TPG):
                    h, q = t // TPH, t % TPH
                    if g >= 2 and q == 0:
                        dve.wait_ge(x2_ready, 2 * (g - 2) + h + 1)
                    V.scalar_tensor_tensor(gated[:, g % 2, t, :], xc_bank[h][:, q * P:(q + 1) * P],
                                           sm2[:, g % 2, 2, t:t + 1], modb[:, g, 3, :],
                                           ALU.mult, ALU.mult).then_inc(gated_ready, 1)

            def ln3(g):
                dve.wait_ge(x2_ready, 2 * g + 2)
                if g >= 2:
                    dve.wait_ge(hg_ready, TPG * (g - 1))
                stats(g, lambda t: pay[:, g * TPG + t, DM:2 * DM], st3, sm3, stats3)

            def ln3_end(g):
                dve.wait_ge(std3, g + 1)
                V.reciprocal(sm3[:, g % 2, 6, :], sm3[:, g % 2, 5, :]).then_inc(rstd3, 1)

            def choose(g):
                dve.wait_ge(hg_ready, TPG * (g + 1))
                ts = slice(g * TPG, (g + 1) * TPG)
                lg, bc = lgt[:, ts, :], lambda t: t.unsqueeze(2).broadcast_to([P, TPG, NE])
                V.tensor_tensor(lg, hg[:, g % 2, :, DM:GW], cst[:, g, :].unsqueeze(1).broadcast_to([P, TPG, NE]),
                                ALU.add).then_inc(lgt_ready, 1)
                dve.wait_ge(lgt_ready, g + 1)
                step(V.tensor_reduce(lmx[:, ts], lg, AX_X, ALU.max))
                after()
                step(V.tensor_tensor(lwk[:, :, :], lg, bc(lmx[:, ts]), ALU.is_equal))
                after()
                step(V.tensor_tensor(lwk[:, :, :], lwk[:, :, :],
                                     iota_r[:, :].unsqueeze(1).broadcast_to([P, TPG, NE]), ALU.mult))
                after()
                step(V.tensor_reduce(lbest[:, :], lwk[:, :, :], AX_X, ALU.max))
                after()
                s = step(V.tensor_tensor(oh[:, g, :, 1:TPG + 1].rearrange("p e t -> p t e"), lwk[:, :, :], bc(lbest[:, :]),
                                         ALU.is_equal))
                after()
                flat = lambda t: t.rearrange("p e t -> p (e t)")
                V.tensor_tensor_scan(flat(ohsum[:, g, :, :]), flat(reset[:, :, :]), flat(oh[:, g, :, :]), 0.0,
                                     ALU.mult, ALU.add).then_inc(oh_ready, 1)
                V.tensor_tensor(lex[:, g % 2, :, :], lg, bc(lmx[:, ts]), ALU.subtract).then_inc(lsh_ready, 1)
                if g + 1 < NG:
                    dve.wait_ge(oh_ready, g + 1)
                    step(V.tensor_copy(oh[:, g + 1, :, 0], ohsum[:, g, :, TPG]))

            def weight(g):
                dve.wait_ge(lex_ready, g + 1)
                step(V.tensor_reduce(lsum[:, g % 2, :], lex[:, g % 2, :, :], AX_X, ALU.add))
                after()
                V.reciprocal(pay[:, g * TPG:(g + 1) * TPG, 2 * DM], lsum[:, g % 2, :]).then_inc(weight_ready, 1)

            def ranks(g):
                dve.wait_ge(rank_ps, g + 1)
                w = TPG * NE
                ts = slice(g * TPG, (g + 1) * TPG)
                before = rank_bank[:, g * w:(g + 1) * w].rearrange("p (t e) -> p t e", e=NE)
                step(V.tensor_tensor(rk[:, :, :], before, oh[:, g, :, 1:TPG + 1].rearrange("p e t -> p t e"), ALU.mult))
                after()
                step(V.tensor_reduce(rank[:, :], rk[:, :, :], AX_X, ALU.add))
                after()
                step(V.tensor_scalar(rdiv[:, ts], rank[:, :], 1.0 / P, -63.5 / P, ALU.mult, ALU.add))
                after()
                step(V.tensor_scalar(rdiv[:, ts], rdiv[:, ts], ROUND, -ROUND, ALU.add, ALU.add))
                after()
                step(V.scalar_tensor_tensor(rmod[:, g % 2, :], rdiv[:, ts], -float(P), rank[:, :], ALU.mult,
                                            ALU.add))
                after()
                for t in range(TPG):
                    step(V.tensor_scalar(OB[:, g * TPG + t, :], iota_b[:, :], rmod[:, g % 2, t:t + 1], None, ALU.is_equal))

            angles()
            ln1(0)
            table_angles(0)
            ln1_end(0)
            modulation()
            table_angles(1)
            weights_w()
            modulation_rows()
            ssm_matrices()
            gate_weights()
            ln1(1)
            ln1_end(1)

            for r in ROUNDS[1:]:
                if there(r):
                    scan_part(r)
                if there(r - 2):
                    choose(r - 2)
                if there(r - 1):
                    ln3(r - 1)
                if there(r + 2):
                    ln1(r + 2)
                if there(r - 1):
                    ln3_end(r - 1)
                if there(r + 2):
                    ln1_end(r + 2)
                if there(r):
                    ln2(r)
                if there(r - 2):
                    ranks(r - 2)
                if there(r - 3):
                    weight(r - 3)
            weight(NG - 1)

            step(V.tensor_scalar(ntile[:, :], rank_bank[:, TT * NE:TT * NE + NE], 1.0 / P, 63.5 / P, ALU.mult, ALU.add))
            after()
            step(V.tensor_scalar(ntile[:, :], ntile[:, :], ROUND, -ROUND, ALU.add, ALU.add))
            after()
            step(V.tensor_tensor_scan(tend[:, :], onesN[:, :], ntile[:, :], 0.0, ALU.mult, ALU.add))
            after()
            step(V.tensor_tensor(tstart[:, :], tend[:, :], ntile[:, :], ALU.subtract))
            after()
            step(V.tensor_tensor(stk[:, :, :, :], oh[:, :, :, 1:TPG + 1].rearrange("p g e t -> p g t e"),
                                 tstart[:, :].unsqueeze(1).unsqueeze(1).broadcast_to([P, NG, TPG, NE]), ALU.mult))
            after()
            step(V.tensor_reduce(acol[:, :], stk[:, :, :, :].rearrange("p g t e -> p (g t) e"), AX_X, ALU.add))
            after()
            step(V.tensor_tensor(acol[:, :], acol[:, :], rdiv[:, :], ALU.add))
            after()
            for h in range(2):
                ts = slice(h * TT // 2, (h + 1) * TT // 2)
                V.tensor_tensor(OA[:, ts, :], iota_k[:, :].unsqueeze(1).broadcast_to([P, TT // 2, NT]),
                                acol[:, ts].unsqueeze(2).broadcast_to([P, TT // 2, NT]), ALU.is_equal).then_inc(OA_ready, 1)
            for h in range(2):
                ts = slice(h * TT // 2, (h + 1) * TT // 2)
                dve.wait_ge(OA_ready, h + 1)
                V.tensor_tensor(OAv[:, ts, 1, :], OA[:, ts, :], iota_t[:, ts, :], ALU.mult).then_inc(OAt_ready, 1)
            step(V.tensor_tensor(ecmp[:, :, :], tend[:, :].unsqueeze(1).broadcast_to([P, NT, NE]),
                                 iota_k[:, :].unsqueeze(2).broadcast_to([P, NT, NE]), ALU.is_le))
            after()
            step(V.tensor_reduce(etile[:, :], ecmp[:, :, :], AX_X, ALU.add))
            after()
            step(V.tensor_scalar(etile_i[:, :], etile[:, :], float(NE - 1), None, ALU.min))
            dve.wait_ge(tok_ps, 1)
            step(V.tensor_copy(tokv[:, :], banks[4][:, 0:NT]))
            after()
            step(V.scalar_tensor_tensor(gidx[:, :], banks[4][:, NT:2 * NT], float(P), tokv[:, :], ALU.mult, ALU.add))
            after()
            V.tensor_scalar(gidx_i[:, :], gidx[:, :], -float(P), 0.0, ALU.add, ALU.max).then_inc(tables, 1)
            step(V.tensor_scalar(padv[:, :], gidx[:, :], 64.0, FAR, ALU.is_lt, ALU.mult))
            after()
            V.scalar_tensor_tensor(sidx_i[:, :], gidx[:, :], -float(P), padv[:, :], ALU.add, ALU.add).then_inc(tables, 1)

            def copy_w1(j, first=False):
                e = dve.value_load(etile_i[0:1, bass.ds(j.val, 1)], min_val=0, max_val=NE - 1)
                if not first:
                    dve.wait_ge(pre_ps, j.val - 1)
                    dve.wait_ge(hid_ready, j.val - 1)
                V.tensor_copy(w1t[j.mod2][:, :], W1s[:, bass.ds(e, 1), :].rearrange("p o w -> p (o w)")
                              ).then_inc(w1t_ready, 1)

            def finish(j, first=False):
                dve.wait_ge(y_ps, j.val + 1)
                if j.c >= 2 or not first:
                    dve.wait_ge(outb_ready, j.val - 1)
                V.scalar_tensor_tensor(y2[j.mod2][:, :], banks[6 + j.mod2][:, 0:DM], grow[j.mod8][:, 2 * DM:PAY],
                                       grow[j.mod8][:, PAY:ROW], ALU.mult, ALU.mult).then_inc(y_read, 1)
                dve.wait_ge(y_read, j.val + 1)
                if not first:
                    dve.wait_ge(stored[j.mod4], 16 * j.uses4)
                V.tensor_tensor(outb[j.mod4][:, :], y2[j.mod2][:, :], grow[j.mod8][:, DM:2 * DM],
                                ALU.add).then_inc(outb_ready, 1)

            dve.wait_ge(w_in, 16 * 2 * NE)
            dve.wait_ge(b1_in, 16)
            after()
            copy_w1(Tile(0, 0), True)
            def dve_tile(s, early=0, last=False):
                if not last:
                    copy_w1(s + 1, first=early > 1)
                if early < 2:
                    finish(s + -1, first=s.c < 5 and isinstance(s.i, int) and s.i == 0)

            dve_tile(Tile(0, 0), early=2)
            dve_tile(Tile(0, 1), early=1)
            dve_tile(Tile(0, 2))
            dve_tile(Tile(0, 3))
            dve_tile(Tile(0, 4))
            with dve.Fori(0, (NT - 7) // 8 - 1) as i:
                for q in range(8):
                    dve_tile(Tile(i, 5 + q))
            for s in range(NT - 10, NT + 1):
                dve_tile(Tile(0, s), last=s + 1 >= NT)


def build(nc, ins, outs):
    adaln_block(nc, *ins, *outs)


_INS = ['L0_attn_u', 'L0_attn_log_neg_real', 'L0_attn_imag', 'L0_attn_B_mat', 'L0_attn_C_mat', 'L0_attn_D',
        'L0_attn_gamma', 'L0_attn_beta', 'L0_ffn_Wg', 'L0_ffn_bg', 'L0_ffn_W1', 'L0_ffn_b1', 'L0_ffn_W2',
        'L0_ffn_b2', 'L0_c', 'L0_wmod']


def kernel(**inputs):
    import numpy as _np
    import concourse.bacc as _bacc
    from concourse import mybir as _mybir
    from concourse.bass_utils import run_bass_kernel_spmd as _run

    nc = _bacc.Bacc("TRN2", target_bir_lowering=False, num_devices=1)
    arrays, args = {}, []
    for name in _INS:
        a = _np.ascontiguousarray(inputs[name])
        arrays[f"in_{name}"] = a
        args.append(nc.dram_tensor(f"in_{name}", a.shape, _mybir.dt.from_np(a.dtype), kind="ExternalInput").ap())
    shape = tuple(inputs['L0_attn_u'].shape)
    y = nc.dram_tensor("out_x", shape, _mybir.dt.float32, kind="ExternalOutput").ap()
    build(nc, args, [y])
    r = _run(nc, [arrays], core_ids=[0])
    return r.results[0]["out_x"]
```

```python
from contextlib import ExitStack

import concourse.bass as bass
from concourse import mybir

P = 128
ALU = mybir.AluOpType
ACT = mybir.ActivationFunctionType
AX_X = mybir.AxisListType.X
F32 = mybir.dt.float32
F16 = mybir.dt.float16
BF16 = mybir.dt.bfloat16
I32 = mybir.dt.int32

ROUND = 12582912.0
TWO_PI = 6.283185307179586
PI_A = 6.28125
PI_B = 0.0019350051879882812
PI_C = TWO_PI - PI_A - PI_B
SIN_SCALE = 6.2831850
EPS = 1e-5
FAR = 1000000.0


class Tile:

    def __init__(self, i, c):
        self.i, self.c = i, c

    def __add__(self, n):
        return Tile(self.i, self.c + n)

    @property
    def val(self):
        return self.i * 8 + self.c

    @property
    def mod4(self):
        return self.c % 4

    @property
    def mod2(self):
        return self.c % 2

    @property
    def mod8(self):
        return self.c % 8

    @property
    def uses4(self):
        return self.i * 2 + self.c // 4

    @property
    def uses8(self):
        return self.i + self.c // 8


def adaln_block(nc, u, lnr, imag, B_mat, C_mat, D, gamma, beta, Wg, bg, W1, b1, W2, b2, c, wmod, out):
    NG, L, DM = u.shape
    NS = lnr.shape[0]
    NE, _, DH = W1.shape
    TPG = L // P
    NTOK = NG * L
    TT = NTOK // P
    NT = TT + NE - 1
    HC = DH // P
    HALF = L // 2
    TPH = TPG // 2
    PAY = 2 * DM + 1
    ROW = PAY + DM
    GROW = 8
    GW = DM + NE
    WW = DH + HC
    assert DM == P and 2 * NS == P and HALF == 512 and TPH == 4 and (NT - 7) % 8 == 0

    ctx = ExitStack()
    with ctx:
        def sb(name, shape, dt=F32):
            return ctx.enter_context(nc.sbuf_tensor(name, shape, dt))

        def sem(name):
            return ctx.enter_context(nc.semaphore(name))

        banks = [ctx.enter_context(nc.psum_tensor(f"bank{i}", [P, 512], F32)) for i in range(8)]

        rows = nc.dram_tensor("rows", (NTOK, ROW), F32).ap()
        out_rows = out.rearrange("b l d -> (b l) d")

        x = sb("x", [P, TT, DM])
        pay = sb("pay", [P, TT, PAY])
        ident = sb("ident", [P, P])
        swap = sb("swap", [P, P])
        cent = sb("cent", [P, P])
        ones = sb("ones", [P, P])
        upper = sb("upper", [P, P], BF16)
        ones_b = sb("ones_b", [P, P], BF16)
        iota_p = sb("iota_p", [P, 1])
        iota_b = sb("iota_b", [P, P], F16)
        iota_k = sb("iota_k", [P, NT])
        iota_t = sb("iota_t", [P, TT, NT], F16)
        iota_r = sb("iota_r", [P, NE])
        eps = sb("eps", [P, 1])
        quarter = sb("quarter", [P, 1])
        sign = sb("sign", [P, 1])
        reset = sb("reset", [P, NE, TPG + 1])
        onesN = sb("onesN", [P, NE])

        th = sb("th", [P, 1])
        ln_r = sb("ln_r", [P, 1])
        cols = sb("cols", [P, 32])
        Bdup = sb("Bdup", [P, DM])
        Cdup = sb("Cdup", [P, P])
        BT = sb("BT", [P, P])
        Cc = sb("Cc", [P, DM])
        Dcol = sb("Dcol", [P, 1])
        Dc = sb("Dc", [P, P])
        rot = sb("rot", [P, P])
        tabs = sb("tabs", [P, 4, L])
        tab = tabs[:, 0, :]
        tab2 = tabs[:, 1, :]
        z = tabs[:, 2:4, :]
        c_in = sb("c_in", [NG, DM])
        scT = sb("scT", [P, NG])
        wm = sb("wm", [P, 6 * DM])
        modT = sb("modT", [P, 6, NG])
        modr = sb("modr", [NG, 8, DM])
        cla = sb("cla", [NG, 2, DM])
        clb = sb("clb", [NG, 2, DM])
        pick_g = sb("pick_g", [NG, NG, P])
        modb = sb("modb", [P, NG, 4, DM])
        gbeta = sb("gbeta", [P, NG, DM])
        gam_r = sb("gam_r", [NG, DM])
        bet_r = sb("bet_r", [NG, DM])
        Wg_s = sb("Wg_s", [P, NE])
        bg_b = sb("bg_b", [P, NE])
        wgp = sb("wgp", [P, NG, NE])
        sbw = sb("sbw", [P, NG, NE])
        cst = sb("cst", [P, NG, NE])
        rmat = sb("rmat", [P, NG, GW])

        W1s = sb("W1s", [P, NE, WW])
        W2s = sb("W2s", [P, NE, HC, DM])
        b1r = sb("b1r", [NE * HC, P])
        b2h = sb("b2h", [NE, 3, DM], BF16)
        b2w = sb("b2w", [NE, DM])
        b2s = sb("b2s", [3, NE, DM], BF16)

        st = sb("st", [P, 2, TPG, 6])
        sm = sb("sm", [P, 2, 12, TPG])
        st3 = sb("st3", [P, 2, TPG, 6])
        sm3 = sb("sm3", [P, 2, 12, TPG])
        sm2 = sb("sm2", [P, 2, 4, TPG])
        xn = sb("xn", [P, 2, TPG, DM])
        hT = sb("hT", [P, 2, L])
        drive = sb("drive", [P, L])
        state = sb("state", [P, L])
        ang, ang2 = drive, state
        warm = sb("warm", [P, NG + 1])
        sq = sb("sq", [P, TPG, P], BF16)
        gated = sb("gated", [P, 2, TPG, DM])
        x2T = sb("x2T", [P, 2, L])
        steps = x2T[:, 0, :]
        hg = sb("hg", [P, 2, TPG, GW])

        lgt = sb("lgt", [P, TT, NE])
        lmx = sb("lmx", [P, TT])
        lwk = sb("lwk", [P, TPG, NE])
        lbest = sb("lbest", [P, TPG])
        oh = sb("oh", [P, NG, NE, TPG + 1], BF16)
        ohsum = sb("ohsum", [P, NG, NE, TPG + 1], BF16)
        rk = sb("rk", [P, TPG, NE])
        rank = sb("rank", [P, TPG])
        rdiv = sb("rdiv", [P, TT])
        rmod = sb("rmod", [P, 2, TPG])
        OB = sb("OB", [P, TT, P], F16)

        ntile = sb("ntile", [P, NE])
        tend = sb("tend", [P, NE])
        tstart = sb("tstart", [P, NE])
        stk = sb("stk", [P, NG, TPG, NE])
        acol = sb("acol", [P, TT])
        OA = drive[:, 0:TT * NT // 2].bitcast(F16).rearrange("p (t k) -> p t k", k=NT)
        OAv = tabs[:, :, :].rearrange("p a b -> p (a b)")[:, 0:TT * NT].bitcast(F16).rearrange(
            "p (t v k) -> p t v k", v=2, k=NT)
        ecmp = sb("ecmp", [P, NT, NE])
        etile = sb("etile", [P, NT])
        etile_i = sb("etile_i", [P, NT], I32)
        tokv = sb("tokv", [P, NT])
        gidx = sb("gidx", [P, NT])
        gidx_i = sb("gidx_i", [P, NT], I32)
        sidx_i = sb("sidx_i", [P, NT], I32)
        padv = sb("padv", [P, NT])
        lex = sb("lex", [P, 2, TPG, NE])
        lsum = sb("lsum", [P, 2, TPG])

        hgf, gaf, xnf = (t[:, :, :, :].rearrange("p a b c -> p (a b c)") for t in (hg, gated, xn))
        hTf = hT[:, :, :].rearrange("p a b -> p (a b)")
        grow = [f[:, i * ROW:(i + 1) * ROW] for f in (hgf, hTf) for i in range(GROW // 2)]
        w1t = [gaf[:, i * WW:(i + 1) * WW] for i in range(2)]
        hTt = [gaf[:, 2 * WW + i * P:2 * WW + (i + 1) * P] for i in range(2)]
        outb = [gaf[:, 2 * WW + (2 + i) * P:2 * WW + (3 + i) * P] for i in range(4)]
        hid = [xnf[:, i * DH:(i + 1) * DH].rearrange("p (k t) -> p k t", t=P) for i in range(2)]
        y2 = [xnf[:, 2 * DH + i * DM:2 * DH + (i + 1) * DM] for i in range(2)]

        x_in = [sem(f"x_in{g}") for g in range(NG)]
        ssm_in = sem("ssm_in")
        mod_in = sem("mod_in")
        w_in = sem("w_in")
        b1_in = sem("b1_in")
        th_in, ln_r_in, c_in_sem, wm_in = sem("th_in"), sem("ln_r_in"), sem("c_in_sem"), sem("wm_in")
        b2_in, b2_parts, b2_ready = sem("b2_in"), sem("b2_parts"), sem("b2_ready")
        BT_ready, modr_ps, modr_copied, modr_ready = sem("BT_ready"), sem("modr_ps"), sem("modr_copied"), sem("modr_ready")
        rmat_d = sem("rmat_d")
        gb_out = sem("gb_out")
        rows_out = sem("rows_out")
        pool_step, dve_step, act_step = sem("pool_step"), sem("dve_step"), sem("act_step")
        consts = sem("consts")
        theta_ready, cossin, decay_e, decay_r = sem("theta_ready"), sem("cossin"), sem("decay_e"), sem("decay_r")
        tab_ang, tab_ang_pool, tab_ready = sem("tab_ang"), sem("tab_ang_pool"), sem("tab_ready")
        cst_ready = sem("cst_ready")
        state_ready = sem("state_ready")
        rot_ready, tab2_ps, tab2_ready = sem("rot_ready"), sem("tab2_ps"), sem("tab2_ready")
        setT = sem("setT")
        sc_ready = sem("sc_ready")
        modT_ps, modb_ps = sem("modT_ps"), sem("modb_ps")
        modb_copied = sem("modb_copied")
        modT_ready = sem("modT_ready")
        small_in, small_ps, rmat_ready = sem("small_in"), sem("small_ps"), sem("rmat_ready")
        ssm_mats = sem("ssm_mats")

        stats1, std1, rstd1 = sem("stats1"), sem("std1"), sem("rstd1")
        xn_ready, xnT_ready, hT_ready = sem("xn_ready"), sem("xnT_ready"), sem("hT_ready")
        bh_ready, drive_ready, z_ready = sem("bh_ready"), sem("drive_ready"), sem("z_ready")
        xc_ready, std2, gated_ready = sem("xc_ready"), sem("std2"), sem("gated_ready")
        x2_ready, stats3, std3, rstd3 = sem("x2_ready"), sem("stats3"), sem("std3"), sem("rstd3")
        x2T_ps, x2T_ready = sem("x2T_ps"), sem("x2T_ready")
        hg_ps, hg_ready, h2_ready = sem("hg_ps"), sem("hg_ready"), sem("h2_ready")
        lgt_ready, oh_ready, rank_ps = sem("lgt_ready"), sem("oh_ready"), sem("rank_ps")

        lsh_ready, OB_ready = sem("lsh_ready"), sem("OB_ready")
        OA_ready, OAp_ready, OAt_ready = sem("OA_ready"), sem("OAp_ready"), sem("OAt_ready")
        tok_ps, tables, lex_ready, weight_ready = sem("tok_ps"), sem("tables"), sem("lex_ready"), sem("weight_ready")

        row_in = [sem(f"row_in{i}") for i in range(GROW)]
        stored = [sem(f"stored{i}") for i in range(4)]
        hTt_ps, hTt_ready = sem("hTt_ps"), sem("hTt_ready")
        w1t_ready = sem("w1t_ready")
        pre_ps, hid_ready, y_ps, y_read, outb_ready = (
            sem("pre_ps"), sem("hid_ready"), sem("y_ps"), sem("y_read"), sem("outb_ready"))

        turn = banks[0:2]
        bh_bank = banks[2]
        xc_bank = banks[3:5]
        hg_bank = lambda g, k: banks[(5, 6, 2, 3)[k]] if g == NG - 1 else banks[5 + k % 2]
        rank_bank = banks[7]

        ROUNDS = range(-1, NG + 2)

        def there(g):
            return 0 <= g < NG

        turns = [(s, g, h) for r in ROUNDS for s, g in ((1, r + 1), (3, r - 1)) if there(g) for h in range(2)]
        turn_no = {t: n for n, t in enumerate(turns)}

        def uses_before(t):
            n = turn_no[t] - 2
            if n < 0:
                return None
            s = turns[n][0]
            return s, sum(1 for q in turns[:n + 1] if q[0] == s)

        row_bank = (5, 6, 7, 5, 1)


        block = ctx.enter_context(nc.Block())

        def col(i):
            return cols[:, i:i + 1]

        (K_, RED, F_, F1, F2, FQ, RQ, SN, CS, EE, RR, XR, YI, DEN, RDEN, WRE, WIM, T1, T2, RQ2, CM) = range(21)

        @block.sync
        def _(sp):
            def load_x(g):
                sp.dma_start(x[:, g * TPG:(g + 1) * TPG, :],
                             u[g].rearrange("(t p) d -> p t d", p=P)).then_inc(x_in[g], 16)

            sp.dma_start(th[0:NS, :], imag.rearrange("(n o) -> n o", o=1)).then_inc(th_in, 16)
            sp.dma_start(ln_r[0:NS, :], lnr.rearrange("(n o) -> n o", o=1)).then_inc(ln_r_in, 16)
            load_x(0)
            sp.dma_start(ln_r[NS:P, :], lnr.rearrange("(n o) -> n o", o=1)).then_inc(ln_r_in, 16)
            for lo in (0, NS):
                sp.dma_start(Bdup[lo:lo + NS, :], B_mat).then_inc(ssm_in, 16)
            for lo in (0, NS):
                sp.dma_start(Cdup[:, lo:lo + NS], C_mat).then_inc(ssm_in, 16)
            sp.dma_start(Dcol[:, :], D.rearrange("(n o) -> n o", o=1)).then_inc(ssm_in, 16)
            sp.dma_start(b1r[:, :], b1.rearrange("e (k p) -> (e k) p", p=P)).then_inc(b1_in, 16)
            sp.dma_start(Wg_s[:, :], Wg).then_inc(mod_in, 16)
            for t, src in ((gam_r, gamma), (bet_r, beta)):
                sp.dma_start(t[:, :], src.partition_broadcast(NG)).then_inc(mod_in, 16)
            sp.dma_start(bg_b[:, :], bg.partition_broadcast(P)).then_inc(mod_in, 16)
            load_x(1)
            sp.dma_start(b2w[:, :], b2).then_inc(b2_in, 16)
            for g in range(2, NG):
                load_x(g)
            for e in range(NE):
                sp.dma_start(W1s[:, e, 0:DH], W1[e]).then_inc(w_in, 16)
                sp.dma_start(W2s[:, e, :, :], W2[e].rearrange("(k p) d -> p k d", p=P)).then_inc(w_in, 16)
            sp.wait_ge(b2_parts, 3)
            for v in range(3):
                sp.dma_start(b2s[v:v + 1, :, :], b2h[:, v:v + 1, :]).then_inc(b2_ready, 16)
            sp.wait_ge(modb_copied, NG + 1)
            for g in range(NG):
                sp.dma_start(rows[g * L:(g + 1) * L, PAY:ROW].rearrange("(t p) d -> p t d", p=P),
                             modb[:, g, 2, :].unsqueeze(1).broadcast_to([P, TPG, DM])).then_inc(gb_out, 16)
            for g in range(NG):
                sp.wait_ge(h2_ready, 2 * g + 2)
                sp.wait_ge(weight_ready, g + 1)
                sp.dma_start(rows[g * L:(g + 1) * L, 0:PAY].rearrange("(t p) d -> p t d", p=P),
                             pay[:, g * TPG:(g + 1) * TPG, :]).then_inc(rows_out, 16)

        @block.gpsimd
        def _(pool):
            n = [0]

            def step(ins):
                n[0] += 1
                ins.then_inc(pool_step, 1)
                return n[0]

            step(nc.gpsimd.memset(ident[:, :], 0.0))
            step(nc.gpsimd.memset(swap[:, :], 0.0))
            s = step(nc.gpsimd.memset(ones[:, :], 1.0))
            pool.wait_ge(pool_step, s)
            s = step(nc.gpsimd.affine_select(out=ident[:, :], in_=ident[:, :], compare_op=ALU.not_equal, fill=1.0,
                                             base=0, pattern=[[-1, P]], channel_multiplier=1))
            s = step(nc.gpsimd.affine_select(out=swap[:, :], in_=swap[:, :], compare_op=ALU.not_equal, fill=1.0,
                                             base=NS, pattern=[[-1, P]], channel_multiplier=1))
            s = step(nc.gpsimd.affine_select(out=pick_g[:, :, :], in_=ones[0:NG, :].unsqueeze(1).broadcast_to([NG, NG, P]),
                                             compare_op=ALU.is_equal, fill=0.0, base=0, pattern=[[-1, NG], [0, P]],
                                             channel_multiplier=1))
            s = step(nc.gpsimd.iota(steps[:, :], [[1, L]], base=0, channel_multiplier=0,
                                    allow_small_or_imprecise_dtypes=True))
            pool.wait_ge(pool_step, s)
            step(nc.gpsimd.affine_select(out=swap[:, :], in_=swap[:, :], compare_op=ALU.not_equal, fill=1.0,
                                         base=-NS, pattern=[[-1, P]], channel_multiplier=1))
            s = step(nc.gpsimd.tensor_scalar(cent[:, :], ident[:, :], -1.0 / DM, None, ALU.add))
            pool.wait_ge(pool_step, s)
            nc.gpsimd.memset(ones_b[:, :], 1.0).then_inc(consts, 1)

            pool.wait_ge(theta_ready, 1)
            a, b, t = ang[:, HALF:L], ang2[:, HALF:L], steps[:, HALF:L]

            def then(ins):
                pool.wait_ge(pool_step, step(ins))

            then(nc.gpsimd.tensor_scalar(a, t, col(F1), quarter[:, :], ALU.mult, ALU.add))
            then(nc.gpsimd.tensor_scalar(b, a, ROUND, -ROUND, ALU.add, ALU.add))
            then(nc.gpsimd.tensor_tensor(a, a, b, ALU.subtract))
            then(nc.gpsimd.tensor_scalar(b, t, col(F2), None, ALU.mult))
            then(nc.gpsimd.tensor_tensor(a, a, b, ALU.add))
            then(nc.gpsimd.tensor_scalar(b, a, ROUND, -ROUND, ALU.add, ALU.add))
            nc.gpsimd.tensor_tensor(a, a, b, ALU.subtract).then_inc(tab_ang_pool, 1)
            def residual(g):
                pool.wait_ge(xn_ready, 2 * g + 2)
                xs = x[:, g * TPG:(g + 1) * TPG, :]
                return step(nc.gpsimd.tensor_tensor(xs, xs, gbeta[:, g, :].unsqueeze(1).broadcast_to([P, TPG, DM]),
                                                    ALU.add))

            def join(g):
                for h in range(2):
                    t0 = g * TPG + h * TPH
                    pool.wait_ge(gated_ready, TPH * (2 * g + h + 1))
                    nc.gpsimd.tensor_tensor(pay[:, t0:t0 + TPH, DM:2 * DM], gated[:, g % 2, h * TPH:(h + 1) * TPH, :],
                                            x[:, t0:t0 + TPH, :], ALU.add).then_inc(x2_ready, 1)

            def readout(g):
                for h in range(2):
                    s = slice(h * HALF, (h + 1) * HALF)
                    pool.wait_ge(state_ready, 2 * g + h + 1)
                    if g == 0 and h == 0:
                        pool.wait_ge(tab2_ready, 2)
                    if g >= 2 and h == 0:
                        pool.wait_ge(xc_ready, 2 * (g - 1))
                    nc.gpsimd.tensor_tensor(z[:, g % 2, s], state[:, s], tab2[:, s], ALU.mult).then_inc(z_ready, 1)
                    if g == 1 and h == 0:
                        pool.wait_ge(modb_copied, NG + 1)
                        nc.gpsimd.tensor_tensor(rmat[:, :, 0:DM], modb[:, :, 1, :],
                                                cent[:, :].unsqueeze(1).broadcast_to([P, NG, DM]), ALU.mult
                                                ).then_inc(rmat_d, 1)

            def later_constants():
                step(nc.gpsimd.affine_select(out=upper[:, :], in_=ones[:, :], compare_op=ALU.is_gt, fill=0.0,
                                             base=0, pattern=[[1, P]], channel_multiplier=-1))
                step(nc.gpsimd.iota(iota_p[:, :], [[0, 1]], base=0, channel_multiplier=1,
                                    allow_small_or_imprecise_dtypes=True))
                step(nc.gpsimd.iota(iota_b[:, :], [[1, P]], base=0, channel_multiplier=0,
                                    allow_small_or_imprecise_dtypes=True))
                step(nc.gpsimd.iota(iota_k[:, :], [[1, NT]], base=0, channel_multiplier=0,
                                    allow_small_or_imprecise_dtypes=True))
                step(nc.gpsimd.iota(iota_t[:, :, :], [[1, TT], [0, NT]], base=1, channel_multiplier=0,
                                    allow_small_or_imprecise_dtypes=True))
                step(nc.gpsimd.iota(iota_r[:, :], [[-1, NE]], base=NE, channel_multiplier=0,
                                    allow_small_or_imprecise_dtypes=True))
                return step(nc.gpsimd.memset(onesN[:, :], 1.0))

            def split_b2():
                pool.wait_ge(b2_in, 16)
                for v in range(3):
                    nc.gpsimd.tensor_copy(b2h[:, v, :], b2w[:, :]).then_inc(b2_parts, 1)
                    pool.wait_ge(b2_parts, v + 1)
                    if v < 2:
                        s = step(nc.gpsimd.tensor_tensor(b2w[:, :], b2w[:, :], b2h[:, v, :], ALU.subtract))
                        pool.wait_ge(pool_step, s)

            def shift(g):
                for h in range(2):
                    t0 = g * TPG + h * TPH
                    pool.wait_ge(hg_ready, TPH * (2 * g + h + 1))
                    nc.gpsimd.tensor_tensor(pay[:, t0:t0 + TPH, 0:DM], hg[:, g % 2, h * TPH:(h + 1) * TPH, 0:DM],
                                            modb[:, g, 0, :].unsqueeze(1).broadcast_to([P, TPH, DM]),
                                            ALU.add).then_inc(h2_ready, 1)

            for r in ROUNDS[1:-1]:
                if there(r):
                    readout(r)
                if r == 0:
                    pool.wait_ge(modb_copied, 2)
                    residual(0)
                    pool.wait_ge(pool_step, later_constants())
                    join(0)
                if there(r - 2):
                    shift(r - 2)
                if there(r + 1):
                    s = residual(r + 1)
                    pool.wait_ge(pool_step, s)
                if there(r) and r > 0:
                    join(r)
                if r == 1:
                    split_b2()
                if r == NG:
                    shift(r - 1)

            def gather(j):
                nc.gpsimd.indirect_dma_start(grow[j % GROW], None, rows,
                                             bass.IndirectOffsetOnAxis(ap=gidx_i[:, j:j + 1], axis=0)
                                             ).then_inc(row_in[j % GROW], 16)

            def scatter(j):
                nc.gpsimd.indirect_dma_start(out_rows, bass.IndirectOffsetOnAxis(ap=sidx_i[:, j:j + 1], axis=0),
                                             outb[j % 4], None, bounds_check=NTOK - 1, oob_is_err=False
                                             ).then_inc(stored[j % 4], 16)

            pool.wait_ge(rows_out, 16 * NG)
            pool.wait_ge(gb_out, 16 * NG)
            pool.wait_ge(tables, 1)
            for j in range(GROW):
                gather(j)
            pool.wait_ge(tables, 2)
            for j in range(NT):
                pool.wait_ge(outb_ready, j + 1)
                scatter(j)
                if j + GROW < NT:
                    gather(j + GROW)
            for q in range(4):
                pool.wait_ge(stored[q], 16 * len(range(q, NT, 4)))

        @block.scalar
        def _(act):
            act.dma_start(th[NS:P, :], imag.rearrange("(n o) -> n o", o=1)).then_inc(th_in, 16)
            act.dma_start(c_in[:, :], c).then_inc(c_in_sem, 16)
            act.dma_start(wm[:, :], wmod).then_inc(wm_in, 16)

            act.wait_ge(setT, 1)
            nc.scalar.activation(scT[:, :], banks[6][:, 0:NG], ACT.Silu).then_inc(sc_ready, 1)
            act.wait_ge(ln_r_in, 32)
            nc.scalar.activation(col(EE), ln_r[:, :], ACT.Exp).then_inc(decay_e, 1)
            act.wait_ge(decay_e, 1)
            nc.scalar.activation(col(RR), col(EE), ACT.Exp, scale=-1.0).then_inc(decay_r, 1)

            def std_1(g):
                act.wait_ge(stats1, g + 1)
                nc.scalar.activation(sm[:, g % 2, 5, :], sm[:, g % 2, 4, :], ACT.Sqrt, bias=eps[:, :],
                                     scale=0.25).then_inc(std1, 1)

            def norm1(g):
                act.wait_ge(rstd1, g + 1)
                if g >= 2:
                    act.wait_ge(xnT_ready, 2 * g - 2)
                for t in range(TPG):
                    i = nc.scalar.activation(xn[:, g % 2, t, :], x[:, g * TPG + t, :], ACT.Identity,
                                             bias=sm[:, g % 2, 7, t:t + 1], scale=sm[:, g % 2, 6, t:t + 1])
                    if t % TPH == TPH - 1:
                        i.then_inc(xn_ready, 1)

            def modulate1(g):
                for h in range(2):
                    n = turn_no[(1, g, h)]
                    act.wait_ge(xnT_ready, 2 * g + h + 1)
                    if g >= 2 and h == 0:
                        act.wait_ge(xc_ready, 2 * (g - 1))
                    nc.scalar.activation(hT[:, g % 2, h * HALF:(h + 1) * HALF], turn[n % 2][:, :], ACT.Identity,
                                         bias=modT[:, 0, g:g + 1], scale=modT[:, 1, g:g + 1]).then_inc(hT_ready, 1)

            def spread2(g):
                for h in range(2):
                    act.wait_ge(xc_ready, 2 * g + h + 1)
                    for t in range(TPH):
                        q = h * TPH + t
                        i = nc.scalar.activation(sq[:, q, :], xc_bank[h][:, t * P:(t + 1) * P], ACT.Square,
                                                 accum_out=sm2[:, g % 2, 0, q:q + 1])
                        step(i)
                act.wait_ge(act_step, act_n[0])
                nc.scalar.activation(sm2[:, g % 2, 1, :], sm2[:, g % 2, 0, :],
                                     ACT.Sqrt, bias=eps[:, :], scale=1.0 / DM).then_inc(std2, 1)

            act_n = [0]

            def step(ins):
                act_n[0] += 1
                ins.then_inc(act_step, 1)

            def turn3(g):
                for h in range(2):
                    n = turn_no[(3, g, h)]
                    act.wait_ge(x2T_ps, 2 * g + h + 1)
                    if g >= 2:
                        act.wait_ge(hg_ps, 4 * (g - 2) + 2 * h + 2)
                    nc.scalar.activation(x2T[:, g % 2, h * HALF:(h + 1) * HALF], turn[n % 2][:, :],
                                         ACT.Copy).then_inc(x2T_ready, 1)

            def gate3(g):
                act.wait_ge(stats3, g + 1)
                nc.scalar.activation(sm3[:, g % 2, 5, :], sm3[:, g % 2, 4, :], ACT.Sqrt, bias=eps[:, :],
                                     scale=0.25).then_inc(std3, 1)

            def exponentials(g):
                act.wait_ge(lsh_ready, g + 1)
                nc.scalar.activation(lex[:, g % 2, :, :], lex[:, g % 2, :, :], ACT.Exp).then_inc(lex_ready, 1)
                if g + 1 < NG:
                    step(nc.scalar.activation(warm[:, g:g + 1], eps[:, :], ACT.Sqrt))

            def scale3(g):
                act.wait_ge(rstd3, g + 1)
                if g >= 2:
                    act.wait_ge(h2_ready, 2 * (g - 1))
                    act.wait_ge(lgt_ready, g - 1)
                for t in range(TPG):
                    if t % 2 == 0:
                        act.wait_ge(hg_ps, 4 * g + t // 2 + 1)
                    o = (t % 2) * GW
                    nc.scalar.activation(hg[:, g % 2, t, :], hg_bank(g, t // 2)[:, o:o + GW], ACT.Copy,
                                         scale=sm3[:, g % 2, 6, t:t + 1]).then_inc(hg_ready, 1)

            std_1(0)
            norm1(0)
            act.wait_ge(modr_ps, 1)
            for lo, n in ((0, 4), (4, 2)):
                nc.scalar.activation(modr[:, lo:lo + n, :], banks[lo // 4][0:NG, 0:n * DM].rearrange("p (k d) -> p k d", d=DM),
                                     ACT.Copy).then_inc(modr_copied, 1)
            act.wait_ge(theta_ready, 1)
            nc.scalar.activation(col(SN), col(F_), ACT.Sin, scale=SIN_SCALE).then_inc(cossin, 1)
            nc.scalar.activation(col(CS), col(FQ), ACT.Sin, scale=SIN_SCALE).then_inc(cossin, 1)
            act.wait_ge(setT, 4)
            nc.scalar.activation(BT[:, :], banks[5][:, 0:P], ACT.Copy).then_inc(BT_ready, 1)
            act.wait_ge(modT_ready, 1)
            modulate1(0)
            for h, done in enumerate((tab_ang, tab_ang_pool)):
                act.wait_ge(done, 1)
                nc.scalar.activation(tab[:, h * HALF:(h + 1) * HALF], ang[:, h * HALF:(h + 1) * HALF], ACT.Sin,
                                     scale=SIN_SCALE).then_inc(tab_ready, 1)
            act.wait_ge(tab2_ps, 1)
            for h in range(2):
                nc.scalar.activation(tab2[:, h * HALF:(h + 1) * HALF], banks[3 + h][:, :],
                                     ACT.Copy).then_inc(tab2_ready, 1)
            step(nc.scalar.activation(warm[:, NG:NG + 1], eps[:, :], ACT.Sqrt))

            def copy_rows(g):
                nc.scalar.activation(modb[:, g, :, :], banks[row_bank[g]][:, :].rearrange("p (k d) -> p k d", d=DM),
                                     ACT.Copy).then_inc(modb_copied, 1)

            std_1(1)
            act.wait_ge(modb_ps, 1)
            copy_rows(0)
            act.wait_ge(modb_ps, 2)
            nc.scalar.activation(gbeta[:, :, :], banks[row_bank[NG]][:, :].rearrange("p (g d) -> p g d", d=DM),
                                 ACT.Copy).then_inc(modb_copied, 1)
            norm1(1)

            for r in ROUNDS[1:]:
                if there(r + 1) and r > 0:
                    modulate1(r + 1)
                if there(r - 1):
                    turn3(r - 1)
                if there(r):
                    spread2(r)
                if r == 0:
                    modulate1(1)
                    for g in range(1, NG):
                        act.wait_ge(modb_ps, 2 + g)
                        copy_rows(g)
                if there(r - 1):
                    gate3(r - 1)
                if there(r + 2):
                    std_1(r + 2)
                if there(r - 1):
                    scale3(r - 1)
                if there(r + 2):
                    norm1(r + 2)
                if there(r - 2):
                    exponentials(r - 2)

            act.wait_ge(lex_ready, NG)
            nc.scalar.activation(warm[:, NG - 1:NG], eps[:, :], ACT.Silu)
            for h in range(2):
                act.wait_ge(OA_ready, h + 1)
                ts = slice(h * TT // 2, (h + 1) * TT // 2)
                nc.scalar.activation(OAv[:, ts, 0, :], OA[:, ts, :], ACT.Copy, scale=iota_p[:, :]).then_inc(OAp_ready, 1)

            def turn_tile(j):
                act.wait_ge(hTt_ps, j.val + 1)
                nc.scalar.copy(hTt[j.mod2][:, :], banks[j.mod2][:, 0:P]).then_inc(hTt_ready, 1)

            def silu_tile(j, first=False):
                act.wait_ge(pre_ps, j.val + 1)
                if not first:
                    act.wait_ge(y_ps, j.val - 1)
                for k in range(HC):
                    i = nc.scalar.activation(hid[j.mod2][:, k, :], banks[2 + j.mod2][:, k * P:(k + 1) * P], ACT.Silu,
                                             bias=w1t[j.mod2][:, DH + k:DH + k + 1])
                i.then_inc(hid_ready, 1)

            turn_tile(Tile(0, 0))

            def act_tile(s, first=False, last=False):
                if not last:
                    turn_tile(s + 1)
                silu_tile(s, first)

            act_tile(Tile(0, 0), first=True)
            act_tile(Tile(0, 1), first=True)
            act_tile(Tile(0, 2))
            with act.Fori(0, (NT - 7) // 8) as i:
                for q in range(8):
                    act_tile(Tile(i, 3 + q))
            for s in range(NT - 4, NT):
                act_tile(Tile(0, s), last=s + 1 >= NT)

        @block.tensor
        def _(pe):
            pe.wait_ge(consts, 1)
            pe.wait_ge(c_in_sem, 16)
            nc.tensor.transpose(banks[6][:, 0:NG], c_in[:, :], ident[0:NG, 0:NG]).then_inc(setT, 1)
            pe.wait_ge(sc_ready, 1)
            pe.wait_ge(wm_in, 16)
            for k in range(6):
                i = nc.tensor.matmul(banks[7][:, k * NG:(k + 1) * NG], wm[:, k * DM:(k + 1) * DM], scT[:, :],
                                     start=True, stop=True)
            i.then_inc(modT_ps, 1)
            for lo, n in ((0, 4), (4, 2)):
                i = nc.tensor.matmul(banks[lo // 4][0:NG, 0:n * DM], scT[:, :], wm[:, lo * DM:(lo + n) * DM],
                                     start=True, stop=True)
            i.then_inc(modr_ps, 1)
            pe.wait_ge(ssm_in, 16 * 5)
            nc.tensor.transpose(banks[5][:, 0:P], Bdup[:, :], ident[:, :]).then_inc(setT, 1)
            nc.tensor.transpose(banks[5][:, P:2 * P], Cdup[:, :], ident[:, :]).then_inc(setT, 1)
            pe.wait_ge(b1_in, 16)
            nc.tensor.transpose(banks[5][:, 2 * P:2 * P + NE * HC], b1r[:, :],
                                ident[0:NE * HC, 0:NE * HC]).then_inc(setT, 1)
            pe.wait_ge(small_in, 1)
            nc.tensor.matmul(banks[7][:, 64:64 + NG * NE], ones[:, :], sbw[:, :, :].rearrange("p g e -> p (g e)"),
                             start=True, stop=True)
            nc.tensor.matmul(banks[7][:, 128:128 + NG * NE], cent[:, :], wgp[:, :, :].rearrange("p g e -> p (g e)"),
                             start=True, stop=True).then_inc(small_ps, 1)

            def turn1(g):
                for h in range(2):
                    n = turn_no[(1, g, h)]
                    pe.wait_ge(xn_ready, 2 * g + h + 1)
                    free_turn((1, g, h))
                    for t in range(TPH):
                        i = nc.tensor.transpose(turn[n % 2][:, t * P:(t + 1) * P], xn[:, g % 2, h * TPH + t, :],
                                                ident[:, :])
                    i.then_inc(xnT_ready, 1)

            def free_turn(t):
                if uses_before(t):
                    s, k = uses_before(t)
                    pe.wait_ge(hT_ready if s == 1 else x2T_ready, k)

            def project(g, halves=(0, 1)):
                for h in halves:
                    pe.wait_ge(hT_ready, 2 * g + h + 1)
                    if 2 * g + h >= 1:
                        pe.wait_ge(drive_ready, 2 * g + h)
                    nc.tensor.matmul(bh_bank[:, :], BT[:, :], hT[:, g % 2, h * HALF:(h + 1) * HALF],
                                     start=True, stop=True).then_inc(bh_ready, 1)

            def mix(g):
                for h in range(2):
                    pe.wait_ge(z_ready, 2 * g + h + 1)
                    if g >= 1:
                        pe.wait_ge(gated_ready, TPH * (2 * (g - 1) + h + 1))
                    for t in range(TPH):
                        s = h * HALF + t * P
                        nc.tensor.matmul(xc_bank[h][:, t * P:(t + 1) * P], hT[:, g % 2, s:s + P], Dc[:, :],
                                         start=True, stop=False)
                        i = nc.tensor.matmul(xc_bank[h][:, t * P:(t + 1) * P], z[:, g % 2, s:s + P], Cc[:, :],
                                             start=False, stop=True)
                    i.then_inc(xc_ready, 1)

            def turn2(g):
                for h in range(2):
                    n = turn_no[(3, g, h)]
                    pe.wait_ge(x2_ready, 2 * g + h + 1)
                    free_turn((3, g, h))
                    for t in range(TPH):
                        i = nc.tensor.transpose(turn[n % 2][:, t * P:(t + 1) * P],
                                                pay[:, g * TPG + h * TPH + t, DM:2 * DM], ident[:, :])
                    i.then_inc(x2T_ps, 1)

            def gate(g):
                pe.wait_ge(rmat_ready, 1)
                pe.wait_ge(modb_copied, NG + 1)
                pe.wait_ge(rmat_d, 1)
                for t in range(TPG):
                    if t % TPH == 0:
                        pe.wait_ge(x2T_ready, 2 * g + t // TPH + 1)
                    k = 4 * g + t // 2
                    if t % 2 == 0 and k >= 2 and not (g == NG - 1 and t >= 4):
                        pe.wait_ge(hg_ready, 2 * (k - 1))
                    if g == NG - 1 and t == 4:
                        pe.wait_ge(drive_ready, 2 * NG)
                        pe.wait_ge(gated_ready, TPH * (2 * NG - 1))
                    o = (t % 2) * GW
                    i = nc.tensor.matmul(hg_bank(g, t // 2)[:, o:o + GW], x2T[:, g % 2, t * P:(t + 1) * P],
                                         rmat[:, g, :], start=True, stop=True)
                    if t % 2 == 1:
                        i.then_inc(hg_ps, 1)

            def count(g):
                pe.wait_ge(oh_ready, g + 1)
                w = TPG * NE
                nc.tensor.matmul(rank_bank[:, g * w:(g + 1) * w], upper[:, :],
                                 oh[:, g, :, 1:TPG + 1].rearrange("p e t -> p t e"), start=True, stop=False)
                i = nc.tensor.matmul(rank_bank[:, g * w:(g + 1) * w], ones_b[:, :],
                                     ohsum[:, g, :, 0:TPG].rearrange("p e t -> p t e"), start=False, stop=True)
                if g == NG - 1:
                    i = nc.tensor.matmul(rank_bank[:, NG * w:NG * w + NE], ones_b[:, :],
                                         ohsum[:, g, :, TPG], start=True, stop=True)
                i.then_inc(rank_ps, 1)

            pe.wait_ge(modr_copied, 2)
            turn1(0)
            pe.wait_ge(BT_ready, 1)
            project(0, halves=(0,))
            pe.wait_ge(rot_ready, 1)
            for h in range(2):
                pe.wait_ge(tab_ready, h + 1)
                i = nc.tensor.matmul(banks[3 + h][:, :], rot[:, :], tab[:, h * HALF:(h + 1) * HALF],
                                     start=True, stop=True)
            i.then_inc(tab2_ps, 1)
            project(0, halves=(1,))
            pe.wait_ge(modr_ready, 2)
            pe.wait_ge(ssm_mats, 1)

            def broadcast_rows(g):
                nc.tensor.matmul(banks[row_bank[g]][:, :], pick_g[:, g, :],
                                 modr[:, 3:7, :].rearrange("p k d -> p (k d)"), start=True, stop=True).then_inc(modb_ps, 1)

            broadcast_rows(0)
            pe.wait_ge(hT_ready, 2)
            for g in range(NG):
                i = nc.tensor.matmul(banks[row_bank[NG]][:, g * DM:(g + 1) * DM], pick_g[:, g, :], modr[:, 7, :],
                                     start=True, stop=True)
            i.then_inc(modb_ps, 1)

            for r in ROUNDS[1:]:
                if r == 0:
                    mix(0)
                    pe.wait_ge(modb_copied, 2)
                if there(r + 1):
                    turn1(r + 1)
                if r == 0:
                    pe.wait_ge(cst_ready, 1)
                    pe.wait_ge(rmat_ready, 1)
                    for g in range(1, NG):
                        broadcast_rows(g)
                if there(r - 1):
                    turn2(r - 1)
                if there(r - 2):
                    count(r - 2)
                if there(r) and r > 0:
                    mix(r)
                if there(r + 1):
                    project(r + 1, halves=(0,))
                if there(r - 1):
                    gate(r - 1)
                if there(r + 1):
                    project(r + 1, halves=(1,))

            for t in range(TT):
                if t % (TT // 2) == 0:
                    pe.wait_ge(OAp_ready, 2 * t // TT + 1)
                    pe.wait_ge(OAt_ready, 2 * t // TT + 1)
                if t == TT - TPG:
                    pe.wait_ge(OB_ready, 1)
                i = nc.tensor.matmul(banks[4][:, 0:2 * NT], OB[:, t, :], OAv[:, t, :, :].rearrange("p v k -> p (v k)"),
                                     start=(t == 0), stop=(t == TT - 1))
            i.then_inc(tok_ps, 1)

            def turn_tile(j, first=False):
                pe.wait_ge(row_in[j.mod8], 16 * (j.uses8 + 1))
                if not first:
                    pe.wait_ge(hTt_ready, j.val - 1)
                nc.tensor.transpose(banks[j.mod2][:, 0:P], grow[j.mod8][:, 0:DM], ident[:, :]).then_inc(hTt_ps, 1)

            def up(j, first=False):
                pe.wait_ge(hTt_ready, j.val + 1)
                pe.wait_ge(w1t_ready, j.val + 1)
                if not first:
                    pe.wait_ge(hid_ready, j.val - 1)
                for k in range(HC):
                    i = nc.tensor.matmul(banks[2 + j.mod2][:, k * P:(k + 1) * P], w1t[j.mod2][:, k * P:(k + 1) * P],
                                         hTt[j.mod2][:, :], start=True, stop=True)
                i.then_inc(pre_ps, 1)

            def expert(j):
                return pe.value_load(etile_i[0:1, bass.ds(j.val, 1)], min_val=0, max_val=NE - 1)

            def bias(j, e, first=False):
                if not first:
                    pe.wait_ge(y_read, j.val - 1)
                nc.tensor.matmul(banks[6 + j.mod2][:, 0:DM], ones_b[0:3, :],
                                 b2s[:, bass.ds(e, 1), :].rearrange("p o d -> p (o d)"), start=True, stop=False)

            def down(j, e):
                pe.wait_ge(hid_ready, j.val + 1)
                for k in range(HC):
                    i = nc.tensor.matmul(banks[6 + j.mod2][:, 0:DM], hid[j.mod2][:, k, :],
                                         W2s[:, bass.ds(e, 1), k, :].rearrange("p o d -> p (o d)"),
                                         start=False, stop=(k == HC - 1))
                i.then_inc(y_ps, 1)

            pe.wait_ge(tables, 1)
            pe.wait_ge(w_in, 16 * 2 * NE)
            pe.wait_ge(b2_ready, 48)
            turn_tile(Tile(0, 0), True)

            def pe_tile(s, early=0, last=0):
                if early < 3:
                    e = expert(s + -1)
                if last < 1:
                    turn_tile(s + 1, first=early > 2)
                if last < 2:
                    up(s, first=early > 1)
                if early < 3:
                    bias(s + -1, e, first=early > 0)
                    down(s + -1, e)

            pe_tile(Tile(0, 0), early=3)
            pe_tile(Tile(0, 1), early=2)
            pe_tile(Tile(0, 2), early=1)
            with pe.Fori(0, (NT - 7) // 8) as i:
                for q in range(8):
                    pe_tile(Tile(i, 3 + q))
            for s in range(NT - 4, NT + 1):
                pe_tile(Tile(0, s), last=2 if s == NT else (1 if s == NT - 1 else 0))

        @block.vector
        def _(dve):
            V = nc.vector
            n = [0]

            def step(ins):
                n[0] += 1
                ins.then_inc(dve_step, 1)
                return n[0]

            def after(k=None):
                dve.wait_ge(dve_step, n[0] if k is None else k)

            step(V.memset(eps[:, :], EPS))
            step(V.memset(quarter[0:NS, :], 0.25))
            step(V.memset(quarter[NS:P, :], 0.0))
            step(V.memset(sign[0:NS, :], 1.0))
            step(V.memset(sign[NS:P, :], -1.0))
            step(V.memset(reset[:, :, :], 1.0))
            step(V.memset(oh[:, 0, :, 0:1], 0.0))
            after()
            step(V.memset(reset[:, :, 0:1], 0.0))

            def stats(g, s_in, six, small, what):
                for t in range(TPG):
                    step(V.bn_stats(six[:, g % 2, t, :], s_in(t)))
                after()
                q = lambda k: six[:, g % 2, :, k]
                m = lambda k: small[:, g % 2, k, :]
                step(V.tensor_tensor(m(0), q(1), q(4), ALU.add))
                step(V.tensor_tensor(m(1), q(1), q(4), ALU.subtract))
                step(V.tensor_tensor(m(2), q(2), q(5), ALU.add))
                after(n[0] - 1)
                step(V.tensor_tensor(m(3), m(1), m(1), ALU.mult))
                after()
                V.scalar_tensor_tensor(m(4), m(2), 4.0 / DM, m(3), ALU.mult, ALU.add).then_inc(what, 1)

            def ln1(g):
                dve.wait_ge(x_in[g], 16)
                if g >= 2:
                    dve.wait_ge(xn_ready, 2 * (g - 1))
                stats(g, lambda t: x[:, g * TPG + t, :], st, sm, stats1)

            def ln1_end(g):
                dve.wait_ge(std1, g + 1)
                step(V.reciprocal(sm[:, g % 2, 6, :], sm[:, g % 2, 5, :]))
                after()
                V.scalar_tensor_tensor(sm[:, g % 2, 7, :], sm[:, g % 2, 0, :], -0.5, sm[:, g % 2, 6, :],
                                       ALU.mult, ALU.mult).then_inc(rstd1, 1)

            def angles():
                dve.wait_ge(th_in, 32)
                step(V.tensor_scalar(col(T1), th[:, :], 1.0 / TWO_PI, ROUND, ALU.mult, ALU.add))
                after()
                step(V.tensor_scalar(col(K_), col(T1), -ROUND, None, ALU.add))
                after()
                step(V.scalar_tensor_tensor(col(T1), col(K_), -PI_A, th[:, :], ALU.mult, ALU.add))
                after()
                step(V.scalar_tensor_tensor(col(T2), col(K_), -PI_B, col(T1), ALU.mult, ALU.add))
                after()
                step(V.scalar_tensor_tensor(col(RED), col(K_), -PI_C, col(T2), ALU.mult, ALU.add))
                after()
                step(V.tensor_scalar(col(T1), col(RED), 1.0 / TWO_PI, 0.5, ALU.mult, ALU.min))
                after()
                step(V.tensor_scalar(col(F_), col(T1), -0.5, None, ALU.max))
                after()
                step(V.tensor_scalar(col(T1), col(F_), 4096.0, ROUND, ALU.mult, ALU.add))
                step(V.tensor_scalar(col(RQ), col(F_), 0.25, ROUND, ALU.add, ALU.add))
                after()
                step(V.tensor_scalar(col(F1), col(T1), -ROUND, 1.0 / 4096.0, ALU.add, ALU.mult))
                step(V.tensor_scalar(col(RQ2), col(RQ), -ROUND, -0.25, ALU.add, ALU.add))
                after()
                step(V.tensor_tensor(col(F2), col(F_), col(F1), ALU.subtract))
                V.tensor_tensor(col(FQ), col(F_), col(RQ2), ALU.subtract).then_inc(theta_ready, 1)

            def table_angles():
                dve.wait_ge(consts, 1)
                a, b, t = ang[:, 0:HALF], ang2[:, 0:HALF], steps[:, 0:HALF]
                step(V.tensor_scalar(a, t, col(F1), quarter[:, :], ALU.mult, ALU.add))
                after()
                step(V.tensor_scalar(b, a, ROUND, -ROUND, ALU.add, ALU.add))
                after()
                step(V.tensor_tensor(a, a, b, ALU.subtract))
                after()
                step(V.scalar_tensor_tensor(a, t, col(F2), a, ALU.mult, ALU.add))
                after()
                step(V.tensor_scalar(b, a, ROUND, -ROUND, ALU.add, ALU.add))
                after()
                V.tensor_tensor(a, a, b, ALU.subtract).then_inc(tab_ang, 1)

            def ssm_matrices():
                dve.wait_ge(BT_ready, 1)
                step(V.tensor_copy(W1s[:, :, DH:WW], banks[5][:, 2 * P:2 * P + NE * HC].rearrange(
                    "p (e k) -> p e k", k=HC)))
                step(V.tensor_reduce(col(CM), banks[5][:, P:2 * P], AX_X, ALU.add))
                step(V.tensor_scalar(col(T1), Dcol[:, :], 1.0, None, ALU.add))
                after()
                step(V.tensor_scalar(col(CM), col(CM), 1.0 / DM, None, ALU.mult))
                step(V.tensor_scalar(Dc[:, :], cent[:, :], col(T1), None, ALU.mult))
                after()
                V.tensor_scalar(Cc[:, :], banks[5][:, P:2 * P], col(CM), None, ALU.subtract).then_inc(ssm_mats, 1)

            def weights_w():
                dve.wait_ge(cossin, 2)
                dve.wait_ge(decay_r, 1)
                step(V.tensor_tensor(col(XR), col(RR), col(CS), ALU.mult))
                step(V.tensor_tensor(col(YI), col(RR), col(SN), ALU.mult))
                step(V.tensor_tensor(col(DEN), col(EE), col(EE), ALU.mult))
                after()
                step(V.tensor_scalar(col(XR), col(XR), -1.0, None, ALU.add))
                step(V.scalar_tensor_tensor(col(DEN), th[:, :], th[:, :], col(DEN), ALU.mult, ALU.add))
                after()
                step(V.reciprocal(col(RDEN), col(DEN)))
                step(V.tensor_tensor(col(T1), col(XR), col(EE), ALU.mult))
                step(V.tensor_tensor(col(T2), col(YI), col(EE), ALU.mult))
                after()
                step(V.scalar_tensor_tensor(col(T1), col(YI), th[:, :], col(T1), ALU.mult, ALU.subtract))
                step(V.scalar_tensor_tensor(col(T2), col(XR), th[:, :], col(T2), ALU.mult, ALU.add))
                after()
                step(V.tensor_tensor(col(WRE), col(T1), col(RDEN), ALU.mult))
                step(V.scalar_tensor_tensor(col(WIM), col(T2), -1.0, col(RDEN), ALU.mult, ALU.mult))
                after()
                step(V.tensor_tensor(col(WIM), col(WIM), sign[:, :], ALU.mult))
                step(V.tensor_scalar(rot[:, :], ident[:, :], col(WRE), None, ALU.mult))
                after()
                V.scalar_tensor_tensor(rot[:, :], swap[:, :], col(WIM), rot[:, :],
                                       ALU.mult, ALU.add).then_inc(rot_ready, 1)

            def modulation():
                dve.wait_ge(modT_ps, 1)
                mt = banks[7][:, 0:6 * NG].rearrange("p (k g) -> p k g", g=NG)
                step(V.tensor_copy(modT[:, :, :], mt))
                after()
                step(V.tensor_scalar(modT[:, 4, :], modT[:, 4, :], 1.0, None, ALU.add))
                V.tensor_scalar(modT[:, 1, :], modT[:, 1, :], 1.0, None, ALU.add).then_inc(modT_ready, 1)
                after()
                dve.wait_ge(modT_ready, 1)
                dve.wait_ge(mod_in, 16 * 4)
                wgb = Wg_s[:, :].unsqueeze(1).broadcast_to([P, NG, NE])
                step(V.tensor_tensor(sbw[:, :, :], wgb, modT[:, 3, :].unsqueeze(2).broadcast_to([P, NG, NE]), ALU.mult))
                after()
                V.tensor_tensor(wgp[:, :, :], wgb, modT[:, 4, :].unsqueeze(2).broadcast_to([P, NG, NE]),
                                ALU.mult).then_inc(small_in, 1)

            def modulation_rows():
                dve.wait_ge(modr_copied, 2)
                gates = modr[:, 2:6:3, :]
                a = step(V.scalar_tensor_tensor(cla[:, :, :], gates, -1.0, gates, ALU.mult, ALU.max))
                step(V.tensor_scalar(clb[:, :, :], gates, 0.0, 2.0, ALU.is_ge, ALU.mult))
                step(V.tensor_scalar(modr[:, 4, :], modr[:, 4, :], 1.0, None, ALU.add))
                after(a)
                step(V.tensor_scalar(cla[:, :, :], cla[:, :, :], 0.25, None, ALU.max))
                after()
                step(V.scalar_tensor_tensor(gates, clb[:, :, :], -1.0, cla[:, :, :], ALU.add, ALU.mult))
                after()
                V.tensor_tensor(modr[:, 6, :], modr[:, 2, :], gam_r[:, :], ALU.mult).then_inc(modr_ready, 1)
                V.tensor_tensor(modr[:, 7, :], modr[:, 2, :], bet_r[:, :], ALU.mult).then_inc(modr_ready, 1)

            def gate_weights():
                dve.wait_ge(small_ps, 1)
                V.tensor_tensor(cst[:, :, :], banks[7][:, 64:64 + NG * NE].rearrange("p (g e) -> p g e", e=NE),
                                bg_b[:, :].unsqueeze(1).broadcast_to([P, NG, NE]), ALU.add).then_inc(cst_ready, 1)
                V.tensor_copy(rmat[:, :, DM:GW], banks[7][:, 128:128 + NG * NE].rearrange("p (g e) -> p g e", e=NE)
                              ).then_inc(rmat_ready, 1)

            def scan_part(g, halves=(0, 1)):
                for h in halves:
                    s = slice(h * HALF, (h + 1) * HALF)
                    dve.wait_ge(bh_ready, 2 * g + h + 1)
                    if g == 0 and h == 0:
                        dve.wait_ge(tab_ready, 1)
                    if g == 0 and h == 1:
                        dve.wait_ge(tab_ready, 2)
                    V.tensor_tensor(drive[:, s], bh_bank[:, :], tab[:, s], ALU.mult).then_inc(drive_ready, 1)
                    dve.wait_ge(drive_ready, 2 * g + h + 1)
                    init = 0.0 if h == 0 else state[:, HALF - 1:HALF]
                    if g >= 1:
                        dve.wait_ge(z_ready, 2 * (g - 1) + h + 1)
                    V.tensor_tensor_scan(state[:, s], col(RR).broadcast_to([P, HALF]), drive[:, s], init,
                                         ALU.mult, ALU.add).then_inc(state_ready, 1)
                    dve.wait_ge(state_ready, 2 * g + h + 1)

            def ln2(g):
                dve.wait_ge(std2, g + 1)
                dve.wait_ge(modb_copied, 1 if g == 0 else NG + 1)
                step(V.reciprocal(sm2[:, g % 2, 2, :], sm2[:, g % 2, 1, :]))
                after()
                for t in range(TPG):
                    h, q = t // TPH, t % TPH
                    if g >= 2 and q == 0:
                        dve.wait_ge(x2_ready, 2 * (g - 2) + h + 1)
                    V.scalar_tensor_tensor(gated[:, g % 2, t, :], xc_bank[h][:, q * P:(q + 1) * P],
                                           sm2[:, g % 2, 2, t:t + 1], modb[:, g, 3, :],
                                           ALU.mult, ALU.mult).then_inc(gated_ready, 1)

            def ln3(g):
                dve.wait_ge(x2_ready, 2 * g + 2)
                if g >= 2:
                    dve.wait_ge(hg_ready, TPG * (g - 1))
                stats(g, lambda t: pay[:, g * TPG + t, DM:2 * DM], st3, sm3, stats3)

            def ln3_end(g):
                dve.wait_ge(std3, g + 1)
                V.reciprocal(sm3[:, g % 2, 6, :], sm3[:, g % 2, 5, :]).then_inc(rstd3, 1)

            def choose(g):
                dve.wait_ge(hg_ready, TPG * (g + 1))
                dve.wait_ge(cst_ready, 1)
                ts = slice(g * TPG, (g + 1) * TPG)
                lg, bc = lgt[:, ts, :], lambda t: t.unsqueeze(2).broadcast_to([P, TPG, NE])
                V.tensor_tensor(lg, hg[:, g % 2, :, DM:GW], cst[:, g, :].unsqueeze(1).broadcast_to([P, TPG, NE]),
                                ALU.add).then_inc(lgt_ready, 1)
                dve.wait_ge(lgt_ready, g + 1)
                step(V.tensor_reduce(lmx[:, ts], lg, AX_X, ALU.max))
                after()
                step(V.tensor_tensor(lwk[:, :, :], lg, bc(lmx[:, ts]), ALU.is_equal))
                after()
                step(V.tensor_tensor(lwk[:, :, :], lwk[:, :, :],
                                     iota_r[:, :].unsqueeze(1).broadcast_to([P, TPG, NE]), ALU.mult))
                after()
                step(V.tensor_reduce(lbest[:, :], lwk[:, :, :], AX_X, ALU.max))
                after()
                s = step(V.tensor_tensor(oh[:, g, :, 1:TPG + 1].rearrange("p e t -> p t e"), lwk[:, :, :], bc(lbest[:, :]),
                                         ALU.is_equal))
                after()
                flat = lambda t: t.rearrange("p e t -> p (e t)")
                V.tensor_tensor_scan(flat(ohsum[:, g, :, :]), flat(reset[:, :, :]), flat(oh[:, g, :, :]), 0.0,
                                     ALU.mult, ALU.add).then_inc(oh_ready, 1)
                V.tensor_tensor(lex[:, g % 2, :, :], lg, bc(lmx[:, ts]), ALU.subtract).then_inc(lsh_ready, 1)
                if g + 1 < NG:
                    dve.wait_ge(oh_ready, g + 1)
                    step(V.tensor_copy(oh[:, g + 1, :, 0], ohsum[:, g, :, TPG]))

            def weight(g):
                dve.wait_ge(lex_ready, g + 1)
                step(V.tensor_reduce(lsum[:, g % 2, :], lex[:, g % 2, :, :], AX_X, ALU.add))
                after()
                V.reciprocal(pay[:, g * TPG:(g + 1) * TPG, 2 * DM], lsum[:, g % 2, :]).then_inc(weight_ready, 1)

            def ranks(g):
                dve.wait_ge(rank_ps, g + 1)
                w = TPG * NE
                ts = slice(g * TPG, (g + 1) * TPG)
                before = rank_bank[:, g * w:(g + 1) * w].rearrange("p (t e) -> p t e", e=NE)
                step(V.tensor_tensor(rk[:, :, :], before, oh[:, g, :, 1:TPG + 1].rearrange("p e t -> p t e"), ALU.mult))
                after()
                step(V.tensor_reduce(rank[:, :], rk[:, :, :], AX_X, ALU.add))
                after()
                step(V.tensor_scalar(rdiv[:, ts], rank[:, :], 1.0 / P, -63.5 / P, ALU.mult, ALU.add))
                after()
                step(V.tensor_scalar(rdiv[:, ts], rdiv[:, ts], ROUND, -ROUND, ALU.add, ALU.add))
                after()
                step(V.scalar_tensor_tensor(rmod[:, g % 2, :], rdiv[:, ts], -float(P), rank[:, :], ALU.mult,
                                            ALU.add))
                after()
                for t in range(TPG):
                    step(V.tensor_scalar(OB[:, g * TPG + t, :], iota_b[:, :], rmod[:, g % 2, t:t + 1], None, ALU.is_equal))

            angles()
            ln1(0)
            ln1_end(0)
            table_angles()
            modulation()
            ln1(1)
            weights_w()
            scan_part(0, halves=(0,))
            modulation_rows()
            ssm_matrices()
            scan_part(0, halves=(1,))
            gate_weights()

            for r in ROUNDS[1:]:
                if there(r) and r > 0:
                    scan_part(r, halves=(0,))
                if there(r - 2):
                    choose(r - 2)
                if r == 1:
                    ln1(3)
                if there(r) and r > 0:
                    scan_part(r, halves=(1,))
                if there(r - 1):
                    ln3(r - 1)
                if r == 0:
                    ln1_end(1)
                    ln1(2)
                if there(r - 2) and r < NG:
                    ranks(r - 2)
                if there(r - 1):
                    ln3_end(r - 1)
                if there(r):
                    ln2(r)
                if there(r + 2):
                    ln1_end(r + 2)
                if r == NG:
                    ranks(r - 2)
                if there(r - 3):
                    weight(r - 3)

            g = NG - 1
            dve.wait_ge(rank_ps, NG)
            ts = slice(g * TPG, (g + 1) * TPG)
            ohg = oh[:, g, :, 1:TPG + 1].rearrange("p e t -> p t e")
            a = step(V.tensor_tensor(rk[:, :, :], rank_bank[:, g * TPG * NE:(g + 1) * TPG * NE].rearrange(
                "p (t e) -> p t e", e=NE), ohg, ALU.mult))
            b = step(V.tensor_scalar(ntile[:, :], rank_bank[:, TT * NE:TT * NE + NE], 1.0 / P, 63.5 / P, ALU.mult, ALU.add))
            after(a)
            a = step(V.tensor_reduce(rank[:, :], rk[:, :, :], AX_X, ALU.add))
            after(b)
            b = step(V.tensor_scalar(ntile[:, :], ntile[:, :], ROUND, -ROUND, ALU.add, ALU.add))
            after(a)
            a = step(V.tensor_scalar(rdiv[:, ts], rank[:, :], 1.0 / P, -63.5 / P, ALU.mult, ALU.add))
            after(b)
            b = step(V.tensor_tensor_scan(tend[:, :], onesN[:, :], ntile[:, :], 0.0, ALU.mult, ALU.add))
            after(a)
            a = step(V.tensor_scalar(rdiv[:, ts], rdiv[:, ts], ROUND, -ROUND, ALU.add, ALU.add))
            after(b)
            b = step(V.tensor_tensor(tstart[:, :], tend[:, :], ntile[:, :], ALU.subtract))
            after(a)
            a = step(V.scalar_tensor_tensor(rmod[:, g % 2, :], rdiv[:, ts], -float(P), rank[:, :], ALU.mult, ALU.add))
            after(b)
            b = step(V.tensor_tensor(stk[:, :, :, :], oh[:, :, :, 1:TPG + 1].rearrange("p g e t -> p g t e"),
                                     tstart[:, :].unsqueeze(1).unsqueeze(1).broadcast_to([P, NG, TPG, NE]), ALU.mult))
            after(b)
            step(V.tensor_reduce(acol[:, :], stk[:, :, :, :].rearrange("p g t e -> p (g t) e"), AX_X, ALU.add))
            after()
            step(V.tensor_tensor(acol[:, :], acol[:, :], rdiv[:, :], ALU.add))
            after()
            for h in range(2):
                ts = slice(h * TT // 2, (h + 1) * TT // 2)
                V.tensor_tensor(OA[:, ts, :], iota_k[:, :].unsqueeze(1).broadcast_to([P, TT // 2, NT]),
                                acol[:, ts].unsqueeze(2).broadcast_to([P, TT // 2, NT]), ALU.is_equal).then_inc(OA_ready, 1)
            weight(NG - 1)
            for h in range(2):
                ts = slice(h * TT // 2, (h + 1) * TT // 2)
                dve.wait_ge(OA_ready, h + 1)
                V.tensor_tensor(OAv[:, ts, 1, :], OA[:, ts, :], iota_t[:, ts, :], ALU.mult).then_inc(OAt_ready, 1)
                if h == 0:
                    for t in range(TPG):
                        i = V.tensor_scalar(OB[:, g * TPG + t, :], iota_b[:, :], rmod[:, g % 2, t:t + 1], None, ALU.is_equal)
                    i.then_inc(OB_ready, 1)
            step(V.tensor_tensor(ecmp[:, :, :], tend[:, :].unsqueeze(1).broadcast_to([P, NT, NE]),
                                 iota_k[:, :].unsqueeze(2).broadcast_to([P, NT, NE]), ALU.is_le))
            after()
            step(V.tensor_reduce(etile[:, :], ecmp[:, :, :], AX_X, ALU.add))
            after()
            step(V.tensor_scalar(etile_i[:, :], etile[:, :], float(NE - 1), None, ALU.min))
            dve.wait_ge(tok_ps, 1)
            step(V.tensor_copy(tokv[:, :], banks[4][:, 0:NT]))
            after()
            step(V.scalar_tensor_tensor(gidx[:, :], banks[4][:, NT:2 * NT], float(P), tokv[:, :], ALU.mult, ALU.add))
            after()
            V.tensor_scalar(gidx_i[:, :], gidx[:, :], -float(P), 0.0, ALU.add, ALU.max).then_inc(tables, 1)
            step(V.tensor_scalar(padv[:, :], gidx[:, :], 64.0, FAR, ALU.is_lt, ALU.mult))
            after()
            V.scalar_tensor_tensor(sidx_i[:, :], gidx[:, :], -float(P), padv[:, :], ALU.add, ALU.add).then_inc(tables, 1)

            def copy_w1(j, first=False):
                e = dve.value_load(etile_i[0:1, bass.ds(j.val, 1)], min_val=0, max_val=NE - 1)
                if not first:
                    dve.wait_ge(pre_ps, j.val - 1)
                    dve.wait_ge(hid_ready, j.val - 1)
                V.tensor_copy(w1t[j.mod2][:, :], W1s[:, bass.ds(e, 1), :].rearrange("p o w -> p (o w)")
                              ).then_inc(w1t_ready, 1)

            def finish(j, first=False):
                dve.wait_ge(y_ps, j.val + 1)
                if j.c >= 2 or not first:
                    dve.wait_ge(outb_ready, j.val - 1)
                V.scalar_tensor_tensor(y2[j.mod2][:, :], banks[6 + j.mod2][:, 0:DM], grow[j.mod8][:, 2 * DM:PAY],
                                       grow[j.mod8][:, PAY:ROW], ALU.mult, ALU.mult).then_inc(y_read, 1)
                dve.wait_ge(y_read, j.val + 1)
                if not first:
                    dve.wait_ge(stored[j.mod4], 16 * j.uses4)
                V.tensor_tensor(outb[j.mod4][:, :], y2[j.mod2][:, :], grow[j.mod8][:, DM:2 * DM],
                                ALU.add).then_inc(outb_ready, 1)

            dve.wait_ge(w_in, 16 * 2 * NE)
            dve.wait_ge(b1_in, 16)
            after()
            copy_w1(Tile(0, 0), True)
            def dve_tile(s, early=0, last=False):
                if not last:
                    copy_w1(s + 1, first=early > 1)
                if early < 2:
                    finish(s + -1, first=s.c < 5 and isinstance(s.i, int) and s.i == 0)

            dve_tile(Tile(0, 0), early=2)
            dve_tile(Tile(0, 1), early=1)
            dve_tile(Tile(0, 2))
            dve_tile(Tile(0, 3))
            dve_tile(Tile(0, 4))
            with dve.Fori(0, (NT - 7) // 8 - 1) as i:
                for q in range(8):
                    dve_tile(Tile(i, 5 + q))
            for s in range(NT - 10, NT + 1):
                dve_tile(Tile(0, s), last=s + 1 >= NT)


def build(nc, ins, outs):
    adaln_block(nc, *ins, *outs)


_INS = ['L0_attn_u', 'L0_attn_log_neg_real', 'L0_attn_imag', 'L0_attn_B_mat', 'L0_attn_C_mat', 'L0_attn_D',
        'L0_attn_gamma', 'L0_attn_beta', 'L0_ffn_Wg', 'L0_ffn_bg', 'L0_ffn_W1', 'L0_ffn_b1', 'L0_ffn_W2',
        'L0_ffn_b2', 'L0_c', 'L0_wmod']


def kernel(**inputs):
    import numpy as _np
    import concourse.bacc as _bacc
    from concourse import mybir as _mybir
    from concourse.bass_utils import run_bass_kernel_spmd as _run

    nc = _bacc.Bacc("TRN2", target_bir_lowering=False, num_devices=1)
    arrays, args = {}, []
    for name in _INS:
        a = _np.ascontiguousarray(inputs[name])
        arrays[f"in_{name}"] = a
        args.append(nc.dram_tensor(f"in_{name}", a.shape, _mybir.dt.from_np(a.dtype), kind="ExternalInput").ap())
    shape = tuple(inputs['L0_attn_u'].shape)
    y = nc.dram_tensor("out_x", shape, _mybir.dt.float32, kind="ExternalOutput").ap()
    build(nc, args, [y])
    r = _run(nc, [arrays], core_ids=[0])
    return r.results[0]["out_x"]
```
